# Optimizing a Trainium2 kernel written in Bass

```python
import numpy as np
import jax
import jax.numpy as jnp

def _softmax(x, axis=-1):
    return jax.nn.softmax(x, axis=axis)

def _gelu(x):
    return jax.nn.gelu(x, approximate=True)

def _silu(x):
    return jax.nn.silu(x)

def _sigmoid(x):
    return jax.nn.sigmoid(x)

def _layernorm(x, axis=-1, eps=1e-05):
    m = jnp.mean(x, axis=axis, keepdims=True)
    v = jnp.var(x, axis=axis, keepdims=True)
    return (x - m) / jnp.sqrt(v + eps)

def _scatter_add(tgt, idx, src, axis=0):
    return tgt.at[idx].add(src)

def _segment_sum(src, seg, n):
    return jax.ops.segment_sum(src, seg, n)
kernel_name = 'mk_gnn_resnorm_d4_gnn_r32_b39a66'

def setup_inputs(seed: int=0):
    np.random.seed(seed)
    _w = jnp.asarray

    def _rec_inputs():
        import jax
        import jax.numpy as jnp
        _gk = jax.random.key(seed)
        x = -0.0002117 + 1 * jax.random.normal(jax.random.fold_in(_gk, 1), (3125, 256), jnp.float32)
        _s = jax.random.randint(jax.random.fold_in(_gk, 2), (25000,), 0, 3125, jnp.int32)
        _d = jax.random.randint(jax.random.fold_in(_gk, 3), (25000,), 0, 3125, jnp.int32)
        _loop = jnp.arange(3125, dtype=jnp.int32)
        src = jnp.concatenate([_s, _d, _loop])
        dst = jnp.concatenate([_d, _s, _loop])
        _o = jnp.argsort(dst, stable=True)
        src = src[_o]
        dst = dst[_o]
        edge_attr_8 = -0.000191324 + 0.999809 * jax.random.normal(jax.random.fold_in(_gk, 12), (53125, 8), jnp.float32)
        edge_weight = jax.random.uniform(jax.random.fold_in(_gk, 14), (53125,), jnp.float32, 0.0, 1)
        return (x, src, dst, edge_attr_8, edge_weight)
    x, src, dst, edge_attr_8, edge_weight = _rec_inputs()

    def _L0_gnn_setup():
        import jax, jax.numpy as jnp
        import numpy as np
        N = 3125
        E = 50000
        IN = 256
        OUT = 64
        H = 4
        SLOPE = 0.01
        key = jax.random.key(seed)
        k1, k2, k3, k4, k5 = jax.random.split(key, 5)
        h = jax.random.normal(k1, (N, IN), dtype=jnp.float32)
        W = jax.random.normal(k2, (H, OUT, IN), dtype=jnp.float32) * (1.0 / np.sqrt(IN))
        attn = jax.random.normal(k3, (H, 2 * OUT), dtype=jnp.float32) * (1.0 / np.sqrt(2 * OUT))
        edge_src = jax.random.randint(k4, (E,), 0, N, dtype=jnp.int32)
        edge_dst = jax.random.randint(k5, (E,), 0, N, dtype=jnp.int32)
        return {'h': h, 'W': W, 'attn': attn, 'edge_src': edge_src, 'edge_dst': edge_dst}
    _L0_gnn_all = _L0_gnn_setup()
    _L0_gnn_in = {k: v for k, v in _L0_gnn_all.items() if k in ('W', 'attn')}
    del _L0_gnn_all

    def _L1_gnn_setup():
        import jax, jax.numpy as jnp
        import numpy as np
        N_NODES = 3125
        D = 256
        N_LAYERS = 3
        N_EDGES = 100000
        BN_EPS = 1e-05

        def _bn_train(x, gamma, beta):
            m = jnp.mean(x, axis=0)
            v = jnp.var(x, axis=0)
            return gamma * (x - m) * jax.lax.rsqrt(v + BN_EPS) + beta
        key = jax.random.key(seed)
        ks = jax.random.split(key, 16)
        s = 1.0 / np.sqrt(D)
        inp = {'x': jax.random.normal(ks[0], (N_NODES, D), dtype=jnp.float32), 'edge_index': jax.random.randint(ks[1], (2, N_EDGES), 0, N_NODES, dtype=jnp.int64 if jax.config.jax_enable_x64 else jnp.int32), 'edge_weight': jax.random.uniform(ks[2], (N_EDGES,), dtype=jnp.float32), 'W_in': jax.random.uniform(ks[3], (D, D), jnp.float32, -s, s), 'b_in': jax.random.uniform(ks[4], (D,), jnp.float32, -s, s), 'W1': jax.random.uniform(ks[5], (N_LAYERS, D, D), jnp.float32, -s, s), 'b1': jax.random.uniform(ks[6], (N_LAYERS, D), jnp.float32, -s, s), 'g1': jnp.ones((N_LAYERS, D), jnp.float32), 'be1': jnp.zeros((N_LAYERS, D), jnp.float32), 'W2': jax.random.uniform(ks[7], (N_LAYERS, D, D), jnp.float32, -s, s), 'b2': jax.random.uniform(ks[8], (N_LAYERS, D), jnp.float32, -s, s), 'g_out': jnp.ones((N_LAYERS, D), jnp.float32), 'b_out': jnp.zeros((N_LAYERS, D), jnp.float32)}
        return inp
    _L1_gnn_all = _L1_gnn_setup()
    _L1_gnn_in = {k: v for k, v in _L1_gnn_all.items() if k in ('W_in', 'b_in', 'W1', 'b1', 'g1', 'be1', 'W2', 'b2', 'g_out', 'b_out')}
    del _L1_gnn_all

    def _L2_gnn_setup():
        import jax, jax.numpy as jnp
        import numpy as np
        N = 3125
        E = 100000
        D_IN = 256
        D_OUT = 256
        EPS = 1e-12
        key = jax.random.key(seed)
        k1, k2, k3, k4, k5, k6 = jax.random.split(key, 6)
        inputs = jax.random.normal(k1, (N, D_IN), dtype=jnp.float32)
        edge_src = jax.random.randint(k2, (E,), 0, N, dtype=jnp.int32)
        edge_dst = jax.random.randint(k3, (E,), 0, N, dtype=jnp.int32)
        edge_vals = jax.random.uniform(k4, (E,), dtype=jnp.float32)
        stdv = 1.0 / np.sqrt(D_OUT)
        W = jax.random.uniform(k5, (D_IN, D_OUT), minval=-stdv, maxval=stdv, dtype=jnp.float32)
        b = jax.random.uniform(k6, (D_OUT,), minval=-stdv, maxval=stdv, dtype=jnp.float32)
        return {'inputs': inputs, 'edge_src': edge_src, 'edge_dst': edge_dst, 'edge_vals': edge_vals, 'W': W, 'b': b}
    _L2_gnn_all = _L2_gnn_setup()
    _L2_gnn_in = {k: v for k, v in _L2_gnn_all.items() if k in ('W', 'b')}
    del _L2_gnn_all

    def _L3_gnn_setup():
        import jax, jax.numpy as jnp
        import numpy as np

        def gcn_conv(x, edge_index, W, b):
            N = x.shape[0]
            x = x @ W
            loops = jnp.arange(N, dtype=edge_index.dtype)
            row = jnp.concatenate([edge_index[0], loops])
            col = jnp.concatenate([edge_index[1], loops])
            ones = jnp.ones(row.shape[0], dtype=x.dtype)
            deg = jax.ops.segment_sum(ones, col, num_segments=N)
            deg_inv_sqrt = jnp.where(deg > 0, jax.lax.rsqrt(deg), 0.0)
            norm = deg_inv_sqrt[row] * deg_inv_sqrt[col]
            msgs = x[row] * norm[:, None]
            agg = jax.ops.segment_sum(msgs, col, num_segments=N)
            return agg + b
        key = jax.random.key(seed)
        k1, k2, k3, k4, k5 = jax.random.split(key, 5)
        N, E, D_IN, D_OUT, D_E = (625, 20000, 256, 256, 8)
        hn = jax.random.normal(k1, (N, D_IN), dtype=jnp.float32)
        he = jax.random.normal(k2, (E, D_E), dtype=jnp.float32)
        W = jax.random.normal(k3, (D_IN, D_OUT), dtype=jnp.float32) * (1.0 / np.sqrt(D_IN))
        b = jax.random.normal(k4, (D_OUT,), dtype=jnp.float32) * 0.01
        edge_index = jax.random.randint(k5, (2, E), 0, N, dtype=jnp.int64)
        return {'hn': hn, 'he': he, 'W': W, 'b': b, 'edge_index': edge_index}
    _L3_gnn_all = _L3_gnn_setup()
    _L3_gnn_in = {k: v for k, v in _L3_gnn_all.items() if k in ('W', 'b')}
    del _L3_gnn_all
    return {'x': x, 'src': src, 'dst': dst, 'edge_attr_8': edge_attr_8, 'edge_weight': edge_weight, 'L0_gnn_W': _L0_gnn_in['W'], 'L0_gnn_attn': _L0_gnn_in['attn'], 'L1_gnn_W_in': _L1_gnn_in['W_in'], 'L1_gnn_b_in': _L1_gnn_in['b_in'], 'L1_gnn_W1': _L1_gnn_in['W1'], 'L1_gnn_b1': _L1_gnn_in['b1'], 'L1_gnn_g1': _L1_gnn_in['g1'], 'L1_gnn_be1': _L1_gnn_in['be1'], 'L1_gnn_W2': _L1_gnn_in['W2'], 'L1_gnn_b2': _L1_gnn_in['b2'], 'L1_gnn_g_out': _L1_gnn_in['g_out'], 'L1_gnn_b_out': _L1_gnn_in['b_out'], 'L2_gnn_W': _L2_gnn_in['W'], 'L2_gnn_b': _L2_gnn_in['b'], 'L3_gnn_W': _L3_gnn_in['W'], 'L3_gnn_b': _L3_gnn_in['b']}

def reference(x, src, dst, edge_attr_8, edge_weight, L0_gnn_W, L0_gnn_attn, L1_gnn_W_in, L1_gnn_b_in, L1_gnn_W1, L1_gnn_b1, L1_gnn_g1, L1_gnn_be1, L1_gnn_W2, L1_gnn_b2, L1_gnn_g_out, L1_gnn_b_out, L2_gnn_W, L2_gnn_b, L3_gnn_W, L3_gnn_b):
    import jax
    import jax.numpy as jnp

    def _L0_gnn_ref(h, W, attn, edge_src, edge_dst):
        import jax, jax.numpy as jnp
        import numpy as np
        N = 3125
        E = 50000
        IN = 256
        OUT = 64
        H = 4
        SLOPE = 0.01
        a0 = attn[0]
        a_src, a_dst = (a0[:OUT], a0[OUT:])
        outs = []
        for hd in range(H):
            z = h @ W[hd].T
            s_src = z @ a_src
            s_dst = z @ a_dst
            e = jax.nn.leaky_relu(s_src[edge_src] + s_dst[edge_dst], SLOPE)
            m = jax.ops.segment_max(e, edge_dst, num_segments=N)
            m = jnp.where(jnp.isfinite(m), m, 0.0)
            ex = jnp.exp(e - m[edge_dst])
            den = jax.ops.segment_sum(ex, edge_dst, num_segments=N)
            alpha = ex / jnp.maximum(den[edge_dst], 1e-09)
            msg = alpha[:, None] * z[edge_src]
            outs.append(jax.ops.segment_sum(msg, edge_dst, num_segments=N))
        return jnp.concatenate(outs, axis=1)

    def _L1_gnn_ref(x, edge_index, edge_weight, W_in, b_in, W1, b1, g1, be1, W2, b2, g_out, b_out):
        import jax, jax.numpy as jnp
        import numpy as np
        N_NODES = 3125
        D = 256
        N_LAYERS = 3
        N_EDGES = 100000
        BN_EPS = 1e-05

        def _bn_train(x, gamma, beta):
            m = jnp.mean(x, axis=0)
            v = jnp.var(x, axis=0)
            return gamma * (x - m) * jax.lax.rsqrt(v + BN_EPS) + beta
        row, col = (edge_index[0], edge_index[1])
        h = x @ W_in + b_in
        for l in range(N_LAYERS):
            msgs = edge_weight[:, None] * h[col]
            pooled = jax.ops.segment_sum(msgs, row, num_segments=N_NODES) + h
            hid = jax.nn.relu(_bn_train(pooled @ W1[l] + b1[l], g1[l], be1[l]))
            rep = hid @ W2[l] + b2[l]
            h = jax.nn.relu(_bn_train(rep, g_out[l], b_out[l]))
        return h

    def _L2_gnn_ref(inputs, edge_src, edge_dst, edge_vals, W, b):
        import jax, jax.numpy as jnp
        import numpy as np
        N = 3125
        E = 100000
        D_IN = 256
        D_OUT = 256
        EPS = 1e-12
        x = inputs @ W
        msgs = edge_vals[:, None] * x[edge_src]
        x = jax.ops.segment_sum(msgs, edge_dst, num_segments=N)
        x = jax.nn.relu(x + b)
        norm = jnp.linalg.norm(x, axis=1, keepdims=True)
        out = x / jnp.maximum(norm, EPS)
        return out

    def _L3_gnn_ref(hn, he, W, b, edge_index):
        import jax, jax.numpy as jnp
        import numpy as np

        def gcn_conv(x, edge_index, W, b):
            N = x.shape[0]
            x = x @ W
            loops = jnp.arange(N, dtype=edge_index.dtype)
            row = jnp.concatenate([edge_index[0], loops])
            col = jnp.concatenate([edge_index[1], loops])
            ones = jnp.ones(row.shape[0], dtype=x.dtype)
            deg = jax.ops.segment_sum(ones, col, num_segments=N)
            deg_inv_sqrt = jnp.where(deg > 0, jax.lax.rsqrt(deg), 0.0)
            norm = deg_inv_sqrt[row] * deg_inv_sqrt[col]
            msgs = x[row] * norm[:, None]
            agg = jax.ops.segment_sum(msgs, col, num_segments=N)
            return agg + b
        out = jnp.tanh(gcn_conv(hn, edge_index, W, b)) + 0.0 * he.mean()
        return out
    edge_index = jnp.stack([src, dst])
    x = _layernorm(x + _L0_gnn_ref(x, L0_gnn_W, L0_gnn_attn, src, dst), axis=-1)
    x = _layernorm(x + _L1_gnn_ref(x, edge_index, edge_weight, L1_gnn_W_in, L1_gnn_b_in, L1_gnn_W1, L1_gnn_b1, L1_gnn_g1, L1_gnn_be1, L1_gnn_W2, L1_gnn_b2, L1_gnn_g_out, L1_gnn_b_out), axis=-1)
    x = _layernorm(x + _L2_gnn_ref(x, src, dst, edge_weight, L2_gnn_W, L2_gnn_b), axis=-1)
    x = _layernorm(x + _L3_gnn_ref(x, edge_attr_8, L3_gnn_W, L3_gnn_b, edge_index), axis=-1)
    return x

_drawn_inputs = setup_inputs


def setup_inputs(seed=0):
    import zlib

    import numpy as np

    out = dict(_drawn_inputs(seed))
    spreads = {'L1_gnn_g1': (1.0, 0.2),
     'L1_gnn_be1': (0.0, 0.1),
     'L1_gnn_g_out': (1.0, 0.2),
     'L1_gnn_b_out': (0.0, 0.1)}
    factors = {'L1_gnn_b1': 64.0, 'L1_gnn_b2': 64.0, 'L2_gnn_b': 31.937, 'L3_gnn_b': 6.926}
    for name, (base, spread) in spreads.items():
        noise = np.random.default_rng([zlib.crc32(name.encode()), seed]).standard_normal(out[name].shape)
        drawn = base * np.exp(spread * noise) if base else spread * noise
        out[name] = jnp.asarray(drawn.astype(out[name].dtype))
    for name, factor in factors.items():
        out[name] = (out[name] * factor).astype(out[name].dtype)
    return out
```

```python
import concourse.bass as bass
from concourse import mybir
from contextlib import ExitStack, contextmanager

F32 = mybir.dt.float32
I32 = mybir.dt.int32
BF16 = mybir.dt.bfloat16
U32 = mybir.dt.uint32
U8 = mybir.dt.uint8
ALU = mybir.AluOpType
ACT = mybir.ActivationFunctionType
AX = mybir.AxisListType

P = 128
N = 3125
E = 53125
D = 256
H, OUT = 4, 64
LAYERS = 3
KC = D // P
NT = -(-N // P)
NPAD = NT * P
LAST = N - (NT - 1) * P
EC = -(-E // P)
EFULL = E // EC
ETAIL = E - EFULL * EC
RING = 8
BPC = 2
BPI = RING * BPC
GROUP = 2 * P
SHIFT = GROUP.bit_length() - 1
BPG = GROUP // P
GPC = BPC // BPG
GPI = RING * GPC
ITER = -(-((E + NT * (GROUP - 1)) // GROUP) // GPI)
GROUPS = ITER * GPI
BLOCKS = GROUPS * BPG
GATHERED = [f"s_gath{r}" for r in range(RING)]
LEAD = 4
SPARE = BPG
TRASH = NT
REC = 4
HW = OUT + 1
HZ = H * HW
AW = HZ + 1
PARTS = 3
ZW = AW + PARTS * H // 2
LROWS = P * EC + GROUP
AWAY = -1.0e6
NEG = -2.0 ** 100
SLOPE = 0.01
LN_EPS = 1e-5
BN_EPS = 1e-5
NORM_EPS = 1e-12
DEN_EPS = 1e-9
NCOL = 512
CHUNKS = [(c, min(NCOL, NPAD - c)) for c in range(0, NPAD, NCOL)]
SU = 8
AHEAD = 3
SITER = EC // (2 * SU)
assert SITER * 2 * SU == EC
SG = 2
SB = SG * RING
SPAIRS = EC // (2 * SB)
assert SPAIRS * 2 * SB == EC and 2 * SPAIRS < ITER
EA = E * 8 // 125


class Chain:

    def __init__(self, engine, sem):
        self.engine, self.sem, self.n = engine, sem, 0

    def __call__(self, instruction):
        instruction.then_inc(self.sem, 1)
        self.n += 1

    def wait(self):
        self.engine.wait_ge(self.sem, self.n)

    def step(self, instruction):
        self(instruction)
        self.wait()


def build(nc, A):
    stages = []

    @contextmanager
    def stage(*names):
        stages.append(names)
        sems = [nc.alloc_semaphore(f"{n}_{len(stages)}") for n in names]
        with nc.Block() as block:
            yield sems, block
        nc.clear_and_free_semaphores(sems)
        nc.all_engine_barrier()

    dram = {n: nc.dram_tensor(n, s, F32).ap() for n, s in (
        ("list_by_dst", [LROWS, REC]), ("list_by_src", [P * (BLOCKS + SPARE), REC]),
        ("z_table", [NPAD, ZW]), ("node_table", [NPAD, D]))}
    list_dst_d, list_src_d, z_d, node_d = (
        dram[n] for n in ("list_by_dst", "list_by_src", "z_table", "node_table"))

    with ExitStack() as outer:
        def sb(name, shape, dt=F32, where=outer):
            return where.enter_context(nc.sbuf_tensor(name, shape, dt))

        def rows(t):
            return t.rearrange("(t p) f -> p t f", p=P)

        tile_by_dst = sb("tile_by_dst", [1, LEAD + GROUPS], U8)
        tile_by_src = sb("tile_by_src", [1, LEAD + GROUPS], U8)
        row_by_dst = sb("row_by_dst", [1, GROUPS], I32)
        ident = sb("ident", [P, P])
        iota = sb("iota", [P, P])
        x = sb("x", [P, NT, D])
        acc = sb("acc", [P, NT + 1, AW])
        list_dst = sb("edges_by_dst", [P, BLOCKS, REC])
        list_src = sb("edges_by_src", [P, BLOCKS, REC])
        dst_score = sb("dst_score", [P, NT + 1, H])
        dinv = sb("dinv", [P, NT])
        stats = sb("node_stats", [P, NT, 6])
        meanvar = sb("node_meanvar", [P, NT, 2])
        rstd = sb("node_rstd", [P, NT])
        zero_mean = sb("zero_times_mean", [P, 1])
        eps = sb("eps", [P, 1])
        brow = sb("bias_row", [P, D])

        rec_src = sb("rec_src", [P, EC, REC])
        pos_src = sb("pos_src", [P, EC], U32)

        big = sb("big", [P, NT, ZW])
        xT = sb("xT", [P, KC, NPAD])
        hT = big[:, :, :].rearrange("p t f -> p (t f)")[:, 0:KC * NPAD].rearrange("p (k n) -> p k n", k=KC)
        w_sb = sb("w_sb", [P, KC, HZ + H])
        w2_sb = sb("w2_sb", [P, KC, D])
        column = sb("column", [P, 8, KC])

        pre = outer.enter_context(ExitStack())
        prefix = sb("prefix", [P, 2, EC], F32, pre)
        key_dst = sb("key_dst", [P, EC], I32, pre)
        key_src = sb("key_src", [P, EC], I32, pre)
        key_next = sb("key_next", [P, EC], I32, pre)
        weight = sb("weight", [P, EC], F32, pre)
        tile_f = sb("tile_f", [P, EC], F32, pre)
        tile_next = sb("tile_next", [P, EC], F32, pre)
        part = sb("part", [P, EC], I32, pre)
        ones_row = sb("ones_row", [P, EC], F32, pre)
        mask = sb("mask", [P, 2, EC], F32, pre)
        term = sb("term", [P, 2, EC], F32, pre)
        count_dst = sb("count_dst", [P, NT + 1], F32, pre)
        count_src = sb("count_src", [P, NT + 1], F32, pre)
        first_edge = sb("first_edge", [P, NT + 1], F32, pre)
        offset = sb("offset", [P, NT + 1], F32, pre)
        group_id = sb("group_id", [P, GROUPS], F32, pre)
        reached = sb("reached", [NT, GROUPS], F32, pre)
        row_f = sb("row_f", [1, GROUPS], F32, pre)
        key_by_dst = sb("key_by_dst", [P, GROUPS], F32, pre)
        groups_i = sb("groups_i", [NT, 1], I32, pre)
        groups_f = sb("groups_f", [NT, 1], F32, pre)
        group_end = sb("group_end", [NT, 1], F32, pre)
        surplus = sb("surplus", [NT, 1], F32, pre)
        surplus_row = sb("surplus_row", [NT, P], F32, pre)
        rec_dst = sb("rec_dst", [P, EC, REC], F32, pre)
        pos_f = sb("pos_f", [P, EC], F32, pre)
        sizes = sb("sizes", [P, NT + 1], F32, pre)
        sizes_i = sb("sizes_i", [P, NT + 1], I32, pre)
        slot = sb("slot", [P, EC], I32, pre)
        slot_p = sb("slot_p", [P, EC], I32, pre)
        slot_b = sb("slot_b", [P, EC], I32, pre)
        before = sb("before", [P, P], F32, pre)
        upto = sb("upto", [P, P], F32, pre)
        every = sb("every", [P, P], F32, pre)
        away = sb("away", [P, BPG, REC], F32, pre)
        attr = big[0:125, :, :].rearrange("p t f -> p (t f)")[:, 0:EA]
        attr_sum = sb("attr_sum", [P, 1], F32, pre)
        jumps = sb("jumps", [P, 1], F32, pre)
        unordered = sb("unordered", [P, 1], I32, pre)

        def tile_numbers(last, key, to):
            last.step(nc.vector.tensor_scalar(part[:, :], key[:, :], 7, None, ALU.logical_shift_right))
            last.step(nc.vector.tensor_copy(to[:, :], part[:, :]))

        def records(last, key, other, rec):
            last(nc.vector.tensor_copy(rec[:, :, 1], key[:, :]))
            last(nc.vector.tensor_scalar(rec[:, :, 0], other[:, :], float(N - 1), None, ALU.min))
            last(nc.vector.tensor_copy(rec[:, :, 2], weight[:, :]))

        def tables(last, pe_steps, tile_of, totals, small, wide):
            last.step(nc.vector.tensor_scalar(groups_i[:, :], totals, float(GROUP - 1), None, ALU.add))
            last.step(nc.vector.tensor_scalar(groups_i[:, :], groups_i[:, :], SHIFT, None, ALU.logical_shift_right))
            last.step(nc.vector.tensor_copy(groups_f[:, :], groups_i[:, :]))
            last.step(nc.vector.scalar_tensor_tensor(surplus[:, :], groups_f[:, :], -float(GROUP), totals,
                                                     ALU.mult, ALU.add))
            last.step(nc.vector.tensor_copy(surplus_row[:, :], surplus[:, :].broadcast_to([NT, P])))
            pe_steps()
            last.step(nc.vector.tensor_copy(group_end[:, :], small))
            last.step(nc.vector.tensor_scalar(reached[:, 0:GROUPS], group_id[0:NT, 0:GROUPS], group_end[:, 0:1], None, ALU.is_ge))
            pe_steps()
            last.step(nc.vector.tensor_copy(tile_of[0:1, LEAD:LEAD + GROUPS], wide[0][0:1, 0:GROUPS]))

        def tables_pe(pe, s_dve, s_pe, n0, small, wide):
            pe.wait_ge(s_dve, n0 + 1)
            nc.tensor.matmul(small, upto[0:NT, 0:NT], groups_f[:, :], start=True, stop=True).then_inc(s_pe, 1)
            pe.wait_ge(s_dve, n0 + 2)
            nc.tensor.matmul(wide[0][:, 0:GROUPS], every[0:NT, :], reached[:, 0:GROUPS], start=True, stop=True)
            nc.tensor.matmul(wide[1][:, 0:GROUPS], surplus_row[:, :], reached[:, 0:GROUPS], start=True, stop=True).then_inc(s_pe, 1)

        def exchange(dve, s_dve, s_pe):
            n = [0]

            def step():
                n[0] += 1
                dve.sem_inc(s_dve, 1)
                dve.wait_ge(s_pe, n[0])
            return step

        def positions(last, ahead, sizes, pos):
            last.step(nc.vector.tensor_tensor_scan(first_edge[:, :], ones_row[:, 0:NT + 1], sizes, 0.0, ALU.mult, ALU.add))
            last.step(nc.vector.tensor_tensor(offset[:, :], first_edge[:, :], sizes, ALU.subtract))
            last.step(nc.vector.scalar_tensor_tensor(offset[:, :], offset[:, :], -1.0, ahead, ALU.add, ALU.add))
            last(nc.vector.memset(pos_f[:, :], 0.0))
            for t in range(NT + 1):
                last.step(nc.vector.tensor_scalar(mask[:, t % 2, :], tile_f[:, :], float(t), None, ALU.is_equal))
                last.step(nc.vector.tensor_tensor_scan(prefix[:, t % 2, :], ones_row[:, :], mask[:, t % 2, :], 0.0, ALU.mult, ALU.add))
                last.step(nc.vector.scalar_tensor_tensor(term[:, t % 2, :], prefix[:, t % 2, :], offset[:, t:t + 1],
                                                         mask[:, t % 2, :], ALU.add, ALU.mult))
                last(nc.vector.tensor_tensor(pos_f[:, :], pos_f[:, :], term[:, t % 2, :], ALU.add))
            last.wait()
            last.step(nc.vector.tensor_copy(pos[:, :], pos_f[:, :]))

        def count_tiles(last, counts):
            for t in range(NT + 1):
                last.step(nc.vector.tensor_scalar(mask[:, t % 2, :], tile_f[:, :], float(t), None, ALU.is_equal, ALU.add,
                                                  accum_out=counts[:, t:t + 1]))
            last.wait()

        with ExitStack() as ps, stage(
            "s_cleared", "s_edges", "s_const", "s_pool", "s_chain", "s_dve", "s_pe", "s_x", "s_attr",
        ) as ((s_cleared, s_edges, s_const, s_pool, s_chain, s_dve, s_pe, s_x, s_attr), block):
            sums = ps.enter_context(nc.psum_tensor("sums", [P, 64], F32))
            wide = [ps.enter_context(nc.psum_tensor(f"wide{i}", [P, 512], F32)) for i in range(2)]

            @block.sync
            def _(sp):
                def load(name, to, first):
                    sp.dma_start(to[0:EFULL, :], A[name][first:EFULL * EC + first].rearrange("(p c) -> p c", c=EC)).then_inc(s_edges, 16)
                    sp.dma_start(to[EFULL:EFULL + 1, 0:ETAIL - first],
                                 A[name][EFULL * EC + first:E].rearrange("(p c) -> p c", p=1)).then_inc(s_edges, 16)
                sp.wait_ge(s_cleared, 1)
                load("dst", key_dst, 0)
                load("dst", key_next, 1)
                load("src", key_src, 0)
                load("edge_weight", weight, 0)
                sp.dma_start(attr[:, :], A["edge_attr_8"].rearrange("(p e) a -> p (e a)", p=125)).then_inc(s_attr, 16)
                sp.dma_start(x[:, 0:NT - 1, :],
                             A["x"][0:(NT - 1) * P, :].rearrange("(t p) f -> p t f", p=P)).then_inc(s_x, 16)
                sp.dma_start(x[0:LAST, NT - 1, :], A["x"][(NT - 1) * P:N, :]).then_inc(s_x, 16)
                sp.wait_ge(s_cleared, 2)
                sp.dma_start(list_dst_d[P * EC:LROWS, :].rearrange("(p r) w -> p r w", p=P), away[:, :, :]).then_inc(s_x, 16)
                sp.dma_start(list_src_d.rearrange("(p b) w -> p b w", p=P)[:, 0:BLOCKS, :], list_src[:, :, :]).then_inc(s_x, 16)
                sp.wait_ge(s_x, 64)

            @block.gpsimd
            def _(pool):
                nc.gpsimd.memset(ident[:, :], 0.0).then_inc(s_pool, 1)
                nc.gpsimd.memset(before[:, :], 1.0).then_inc(s_pool, 1)
                nc.gpsimd.memset(upto[:, :], 1.0).then_inc(s_pool, 1)
                nc.gpsimd.iota(iota[:, :], [[1, P]], 0, channel_multiplier=0,
                               allow_small_or_imprecise_dtypes=True).then_inc(s_pool, 1)
                nc.gpsimd.iota(group_id[:, :], [[1, GROUPS]], 0, channel_multiplier=0,
                               allow_small_or_imprecise_dtypes=True).then_inc(s_pool, 1)
                pool.wait_ge(s_pool, 5)
                nc.gpsimd.affine_select(out=ident[:, :], in_=ident[:, :], compare_op=ALU.not_equal, fill=1.0,
                                        base=0, pattern=[[-1, P]], channel_multiplier=1).then_inc(s_const, 1)
                nc.gpsimd.affine_select(out=before[:, :], in_=before[:, :], compare_op=ALU.is_gt, fill=0.0,
                                        base=0, pattern=[[1, P]], channel_multiplier=-1).then_inc(s_const, 1)
                nc.gpsimd.affine_select(out=upto[:, :], in_=upto[:, :], compare_op=ALU.is_ge, fill=0.0,
                                        base=0, pattern=[[1, P]], channel_multiplier=-1).then_inc(s_const, 1)

            @block.vector
            def _(dve):
                last = Chain(dve, s_chain)
                for tile_, value in ((key_dst, NPAD), (key_src, NPAD), (key_next, NPAD), (weight, 0.0)):
                    last(nc.vector.memset(tile_[:, :], value))
                last.step(nc.vector.memset(x[:, NT - 1, :], 0.0))
                dve.sem_inc(s_cleared, 1)
                last(nc.vector.memset(away[:, :, :], 0.0))
                last.step(nc.vector.memset(list_src[:, :, :], 0.0))
                last(nc.vector.memset(away[:, :, 1:2], AWAY))
                last.step(nc.vector.memset(list_src[:, :, 1:2], AWAY))
                dve.sem_inc(s_cleared, 1)
                last(nc.vector.memset(ones_row[:, :], 1.0))
                last(nc.vector.memset(tile_by_dst[:, 0:LEAD], TRASH))
                last(nc.vector.memset(tile_by_src[:, 0:LEAD], TRASH))
                last(nc.vector.memset(every[:, :], 1.0))
                last(nc.vector.memset(eps[:, :], LN_EPS))
                last(nc.vector.memset(attr_sum[:, :], 0.0))
                last(nc.vector.memset(rec_dst[:, :, 3:4], 0.0))
                last(nc.vector.memset(rec_src[:, :, 3:4], 0.0))
                last(nc.vector.memset(dst_score[:, TRASH, :], 0.0))
                dve.wait_ge(s_edges, 128)
                dve.wait_ge(s_const, 3)
                tile_numbers(last, key_next, tile_next)
                tile_numbers(last, key_dst, tile_f)
                last(nc.vector.tensor_tensor(term[:, 0, :], tile_next[:, :], tile_f[:, :], ALU.is_lt))
                count_tiles(last, count_dst)
                last.step(nc.vector.reduce_sum(jumps[:, :], term[:, 0, :], AX.X))
                records(last, key_dst, key_src, rec_dst)
                records(last, key_src, key_dst, rec_src)
                dve.wait_ge(s_attr, 16)
                last.step(nc.vector.reduce_sum(attr_sum[0:125, :], attr[:, :], AX.X))
                step = exchange(dve, s_dve, s_pe)
                step()
                last(nc.vector.tensor_copy(unordered[:, :], sums[:, 0:1]))
                last(nc.vector.tensor_scalar(zero_mean[:, :], sums[:, 1:2], 1.0 / (8 * E), 0.0, ALU.mult, ALU.mult))
                tables(last, step, tile_by_dst, sums[0:NT, 2:3], sums[0:NT, 3:4], wide)
                last(nc.vector.tensor_scalar(key_by_dst[:, :], wide[0][:, 0:GROUPS], float(P), None, ALU.mult))
                last.step(nc.vector.scalar_tensor_tensor(row_f[:, :], group_id[0:1, 0:GROUPS], float(GROUP),
                                                         wide[1][0:1, 0:GROUPS], ALU.mult, ALU.add))
                last.step(nc.vector.tensor_scalar(row_by_dst[:, :], row_f[:, :], float(E), None, ALU.min))

            @block.tensor
            def _(pe):
                pe.wait_ge(s_dve, 1)
                nc.tensor.matmul(sums[:, 0:1], every[:, :], jumps[:, :], start=True, stop=True)
                nc.tensor.matmul(sums[:, 1:2], every[:, :], attr_sum[:, :], start=True, stop=True)
                nc.tensor.matmul(sums[0:NT, 2:3], count_dst[:, 0:NT], every[:, 0:1], start=True, stop=True).then_inc(s_pe, 1)
                tables_pe(pe, s_dve, s_pe, 1, sums[0:NT, 3:4], wide)

        with ExitStack() as ps, stage("s_chain", "s_staged", "s_scat0", "s_scat1", "s_seen", "s_dve", "s_pe", "s_copied") as (
                (s_chain, s_staged, s_scat0, s_scat1, s_seen, s_dve, s_pe, s_copied), block):
            s_scat = (s_scat0, s_scat1)
            sums2 = ps.enter_context(nc.psum_tensor("sums2", [P, 2, 32], F32))
            rec_stage = sb("rec_stage", [P, 2, SU, REC], F32, ps)
            pos_stage = sb("pos_stage", [P, 2, SU], U32, ps)
            pos_dst = sb("pos_dst", [P, EC], U32, ps)
            is_unordered = lambda engine: engine.value_load(unordered[0:1, 0:1], min_val=0, max_val=P * EC) != 0

            @block.sync
            def _(sp):
                with sp.If(is_unordered(sp)):
                    pass
                with sp.Else():
                    sp.dma_start(list_dst_d[0:P * EC, :].rearrange("(p c) w -> p (c w)", c=EC),
                                 rec_dst[:, :, :].rearrange("p c w -> p (c w)")).then_inc(s_copied, 16)
                    sp.wait_ge(s_copied, 16)

            @block.vector
            def _(dve):
                with dve.If(is_unordered(dve)):
                    last = Chain(dve, s_chain)
                    dve.sem_inc(s_dve, 1)
                    dve.wait_ge(s_pe, 1)
                    positions(last, sums2[:, 0, 0:NT + 1], sums2[:, 1, 0:NT + 1], pos_dst)

                    def copy(col, h):
                        nc.vector.tensor_scalar(rec_stage[:, h, :, :], rec_dst[:, bass.ds(col, SU), :], 1.0, None, ALU.mult).then_inc(s_staged, 1)
                        nc.vector.tensor_scalar(pos_stage[:, h, :], pos_dst[:, bass.ds(col, SU)], 1.0, None, ALU.mult).then_inc(s_staged, 1)
                    for h in range(2):
                        copy(h * SU, h)
                    with dve.Fori(1, SITER) as it:
                        for h in range(2):
                            dve.wait_ge(s_scat[h], it * (16 * SU))
                            copy(it * (2 * SU) + h * SU, h)

            @block.tensor
            def _(pe):
                with pe.If(is_unordered(pe)):
                    pe.wait_ge(s_dve, 1)
                    nc.tensor.matmul(sums2[:, 0, 0:NT + 1], before[:, :], count_dst[:, :], start=True, stop=True)
                    nc.tensor.matmul(sums2[:, 1, 0:NT + 1], every[:, :], count_dst[:, :], start=True, stop=True).then_inc(s_pe, 1)

            @block.gpsimd
            def _(pool):
                with pool.If(is_unordered(pool)):
                    with pool.Fori(0, SITER) as it:
                        for h in range(2):
                            pool.wait_ge(s_staged, it * 4 + 2 * h + 2)
                            pool.sem_inc(s_seen, 1)
                            for j in range(SU):
                                pool.indirect_dma_start(list_dst_d, bass.IndirectOffsetOnAxis(ap=pos_stage[:, h, j:j + 1], axis=0),
                                                        rec_stage[:, h, j, :], None).then_inc(s_scat[h], 16)
                    for h in range(2):
                        pool.wait_ge(s_scat[h], SITER * 16 * SU)

        def load_numbers(engine, table, top):
            return nc.values_load_multi_w_load_instructions(table, engines=[engine.engine], min_val=0, max_val=top)[1]

        def load_tiles(engine, tile_of_group, turn, lead):
            words = load_numbers(engine, tile_of_group[:, :].bitcast(I32)[0:1, bass.ds(
                turn * (GPI // 4) + (LEAD - lead) // 4, (GPI + lead) // 4)], (TRASH + 1) << 24)
            return [nc.s_assert_within((word >> (8 * j)) & 255, 0, TRASH,
                                       skip_runtime_bounds_check_because="it is a count of the NT tiles that a group lies beyond")
                    for word in words for j in range(4)]

        def load_by_dst(engine, first, count, s_rows):
            with engine.Fori(0, count // 4) as i:
                rows_ = load_numbers(engine, row_by_dst[0:1, bass.ds(i * 4 + first, 4)], E)
                for j, row in enumerate(rows_):
                    g = i * 4 + (first + j)
                    engine.dma_start(list_dst[:, bass.ds(g * BPG, BPG), :],
                                     list_dst_d[bass.ds(row, GROUP), :].rearrange("(p b) w -> p b w", p=P)).then_inc(s_rows, 16)

        def layer_norm(dve, last, act_sem, sqrt_sem):
            for t in range(NT):
                last(nc.vector.bn_stats(stats[:, t, :], x[:, t, :]))
            last.wait()
            for t in range(NT):
                last(nc.vector.bn_aggr(meanvar[:, t, :], stats[:, t, :]))
            last.wait()
            dve.sem_inc(act_sem, 1)
            dve.wait_ge(sqrt_sem, 1)
            last.step(nc.vector.reciprocal(rstd[:, :], rstd[:, :]))
            for t in range(NT):
                last(nc.vector.tensor_scalar(x[:, t, :], x[:, t, :], meanvar[:, t, 0:1], rstd[:, t:t + 1],
                                             ALU.subtract, ALU.mult))
            last.wait()

        def to_feature_major(source, s_out):
            with ExitStack() as ps, stage("s_turned", "s_copied") as ((s_turned, s_copied), block):
                turned = [ps.enter_context(nc.psum_tensor(f"turned{i}_{s_out}", [P, 4 * P], F32)) for i in range(4)]
                units = [(k, t, min(4, NT - t)) for t in range(0, NT, 4) for k in range(KC)]

                @block.tensor
                def _(pe):
                    for n, (k, t0, nt) in enumerate(units):
                        if n >= 4:
                            pe.wait_ge(s_copied, n - 3)
                        for t in range(nt):
                            last = nc.tensor.transpose(turned[n % 4][:, t * P:(t + 1) * P],
                                                       source[:, t0 + t, k * P:(k + 1) * P], ident[:, :])
                        last.then_inc(s_turned, 1)

                @block.scalar
                def _(act):
                    for n, (k, t0, nt) in enumerate(units):
                        act.wait_ge(s_turned, n + 1)
                        nc.scalar.activation(xT[:, k, t0 * P:(t0 + nt) * P], turned[n % 4][:, 0:nt * P],
                                             ACT.Copy).then_inc(s_copied, 1)

        def project(tag, loads, width, finish, table, table_width):
            with ExitStack() as ps, stage("s_w", "s_prod", "s_fin", "s_stored") as ((s_w, s_prod, s_fin, s_stored), block):
                prod = [ps.enter_context(nc.psum_tensor(f"prod{i}_{tag}", [P, 512], F32)) for i in range(4)]

                @block.sync
                def _(sp):
                    for to, of in loads:
                        sp.dma_start(to, of).then_inc(s_w, 16)
                    sp.wait_ge(s_fin, NT)
                    rows_sb = finish(None, None)
                    for t0 in range(0, NT, 5):
                        sp.dma_start(rows(table)[:, t0:t0 + 5, :], rows_sb[:, t0:t0 + 5, 0:table_width]).then_inc(s_stored, 16)
                    sp.wait_ge(s_stored, 16 * (NT // 5))

                @block.tensor
                def _(pe):
                    if loads:
                        pe.wait_ge(s_w, 16 * len(loads))
                    for t in range(NT):
                        if t >= 4:
                            pe.wait_ge(s_fin, t - 3)
                        for k in range(KC):
                            last = nc.tensor.matmul(prod[t % 4][:, 0:width], xT[:, k, t * P:(t + 1) * P],
                                                    w_sb[:, k, 0:width], start=k == 0, stop=k == KC - 1)
                        last.then_inc(s_prod, 1)

                @block.vector
                def _(dve):
                    if loads:
                        dve.wait_ge(s_w, 16 * len(loads))
                    for t in range(NT):
                        dve.wait_ge(s_prod, t + 1)
                        finish(t, prod[t % 4]).then_inc(s_fin, 1)

        def aggregate(tag, edges, tile_of_group, weighted):
            with ExitStack() as ps, stage("s_index", "s_seen", *GATHERED, "s_select",
                                          "s_sum", "s_added") as (
                    (s_index, s_seen, *s_gath, s_select, s_sum, s_added), block):
                total = [ps.enter_context(nc.psum_tensor(f"total{i}_{tag}", [P, 512], F32)) for i in range(GPI)]

                @block.scalar
                def _(act):
                    with act.Fori(0, ITER) as it:
                        for r in range(RING):
                            act.wait_ge(s_sum, it * GPI + (r + 1) * GPC)
                            nc.scalar.activation(slot_node[:, r, 0:BPC], edges[:, bass.ds(it * BPI + r * BPC, BPC), 0],
                                                 ACT.Copy).then_inc(s_index, 1)

                @block.gpsimd
                def _(pool):
                    with pool.Fori(0, ITER) as it:
                        for r in range(RING):
                            pool.wait_ge(s_index, it * RING + (r + 1))
                            pool.sem_inc(s_seen, 1)
                            for j in range(BPC):
                                pool.indirect_dma_start(gathered[:, r, j, 0:D], None, node_d,
                                                        bass.IndirectOffsetOnAxis(ap=slot_node[:, r, j:j + 1], axis=0)
                                                        ).then_inc(s_gath[r], 16)

                @block.tensor
                def _(pe):
                    pe.sem_inc(s_sum, GPI)
                    with pe.Fori(0, ITER) as it:
                        for r in range(RING):
                            pe.wait_ge(s_gath[r], it * (16 * BPC) + 16 * BPC)
                            pe.wait_ge(s_select, it * BPI + (r + 1) * BPC)
                            for g in range(r * GPC, (r + 1) * GPC):
                                pe.wait_ge(s_added, it * GPI + (g + 1))
                                for b in range(BPG):
                                    j = (g - r * GPC) * BPG + b
                                    last = nc.tensor.matmul(total[g][:, 0:D], select[:, r, j, :], gathered[:, r, j, 0:D],
                                                            start=b == 0, stop=b == BPG - 1)
                                last.then_inc(s_sum, 1)

                @block.vector
                def _(dve):
                    def one_hots(it, r):
                        dve.wait_ge(s_sum, it * GPI + (r + 1) * GPC)
                        for j in range(BPC):
                            at = edges[:, bass.ds(it * BPI + (r * BPC + j), 1), :]
                            if weighted:
                                one = nc.vector.tensor_scalar(select[:, r, j, :], iota[:, :], at[:, 0, 1:2], at[:, 0, 2:3],
                                                              ALU.is_equal, ALU.mult)
                            else:
                                one = nc.vector.tensor_scalar(select[:, r, j, :], iota[:, :], at[:, 0, 1:2], None, ALU.is_equal)
                            one.then_inc(s_select, 1)

                    def add(it, r, tiles):
                        for g in range(r * GPC, (r + 1) * GPC):
                            group = it * GPI + g
                            t = tiles[g]
                            dve.wait_ge(s_sum, group + (GPI + 1))
                            dve.wait_ge(s_added, group + GPI)
                            nc.vector.tensor_tensor(acc[:, bass.ds(t, 1), 0:D], total[g][:, 0:D],
                                                    acc[:, bass.ds(t, 1), 0:D], ALU.add).then_inc(s_added, 1)

                    dve.sem_inc(s_added, GPI)
                    with dve.Fori(0, ITER) as it:
                        tiles = load_tiles(dve, tile_of_group, it, 0)
                        for r in range(RING):
                            one_hots(it, r)
                            if r:
                                add(it, r - 1, tiles)
                        add(it, RING - 1, tiles)

        first_table(nc, A, stage, locals())
        pre.close()
        gathered = sb("gathered", [P, RING, BPC, ZW])
        select = sb("select", [P, RING, BPC, P])
        slot_node = sb("slot_node", [P, RING, BPC], U32)
        attention(nc, A, stage, locals())
        to_feature_major(x, "h0")

        bias_load = lambda name: (brow[:, :], A[name].rearrange("(a n) -> a n", a=1).broadcast_to([P, D]))
        load_w = lambda to, w: [(to[:, k, 0:D], w[k * P:(k + 1) * P, :]) for k in range(KC)]

        def h0_rows(t, prod):
            if t is None:
                return acc
            return nc.vector.tensor_tensor(acc[:, t, 0:D], prod[:, 0:D], brow[:, :], ALU.add)

        project("h0", load_w(w_sb, A["L1_gnn_W_in"]) + [bias_load("L1_gnn_b_in")], D, h0_rows, node_d, D)
        for l in range(LAYERS):
            aggregate(f"l{l}", list_src, tile_by_src, True)
            to_feature_major(acc, f"pool{l}")
            layer_mlp(nc, A, stage, locals())
        residual_norm(nc, stage, locals(), "n2", acc, None)
        to_feature_major(x, "x3")

        def rows3(t, prod):
            if t is None:
                return big
            return nc.vector.tensor_copy(big[:, t, 0:D], prod[:, 0:D])

        project("x3", load_w(w_sb, A["L2_gnn_W"]), D, rows3, node_d, D)
        with stage("s_clear") as ((s_clear,), block):
            @block.vector
            def _(dve):
                nc.vector.memset(acc[:, :, :], 0.0).then_inc(s_clear, 1)
                dve.wait_ge(s_clear, 1)
        aggregate("g3", list_dst, tile_by_dst, True)
        residual_norm(nc, stage, locals(), "n3", acc, "unit")
        to_feature_major(x, "x4")

        def rows4(t, prod):
            if t is None:
                return acc
            return nc.vector.tensor_scalar(acc[:, t, 0:D], prod[:, 0:D], dinv[:, t:t + 1], None, ALU.mult)

        project("x4", load_w(w_sb, A["L3_gnn_W"]), D, rows4, node_d, D)
        aggregate("g4", list_dst, tile_by_dst, False)
        residual_norm(nc, stage, locals(), "n4", acc, "tanh")

        with stage("s_out") as ((s_out,), block):
            @block.sync
            def _(sp):
                sp.dma_start(A["out"][0:(NT - 1) * P, :].rearrange("(t p) f -> p t f", p=P), x[:, 0:NT - 1, :]).then_inc(s_out, 16)
                sp.dma_start(A["out"][(NT - 1) * P:N, :], x[0:LAST, NT - 1, :]).then_inc(s_out, 16)
                sp.wait_ge(s_out, 32)


def residual_norm(nc, stage, v, tag, acc, how):
    x, brow, dinv, rstd, meanvar, eps, big = (v[n] for n in ("x", "brow", "dinv", "rstd", "meanvar", "eps", "big"))
    A = v["A"]
    with stage("s_chain", "s_bias", "s_var", "s_std", "s_pre", "s_tanh") as ((s_chain, s_bias, s_var, s_std, s_pre, s_tanh), block):
        bias = {"unit": "L2_gnn_b", "tanh": "L3_gnn_b", None: None}[how]

        @block.sync
        def _(sp):
            if bias:
                sp.dma_start(brow[:, :], A[bias].rearrange("(a n) -> a n", a=1).broadcast_to([P, D])).then_inc(s_bias, 16)
                sp.wait_ge(s_bias, 16)

        @block.scalar
        def _(act):
            if how == "unit":
                act.wait_ge(s_pre, 1)
                nc.scalar.activation(rstd[:, :], rstd[:, :], ACT.Sqrt).then_inc(s_tanh, 1)
            if how == "tanh":
                for t in range(NT):
                    act.wait_ge(s_pre, t + 1)
                    nc.scalar.activation(acc[:, t, 0:D], acc[:, t, 0:D], ACT.Tanh).then_inc(s_tanh, 1)
            act.wait_ge(s_var, 1)
            if how == "unit":
                act.wait_ge(s_tanh, 2)
            nc.scalar.activation(rstd[:, :], meanvar[:, :, 1], ACT.Sqrt, bias=eps[:, 0:1]).then_inc(s_std, 1)

        @block.vector
        def _(dve):
            last = Chain(dve, s_chain)
            if bias:
                dve.wait_ge(s_bias, 16)
            if how is None:
                last.step(nc.vector.tensor_tensor(x[:, :, :], x[:, :, :], acc[:, 0:NT, 0:D], ALU.add))
            if how == "unit":
                for t in range(NT):
                    last(nc.vector.tensor_tensor(acc[:, t, 0:D], acc[:, t, 0:D], brow[:, :], ALU.add))
                last.wait()
                for t in range(NT):
                    last(nc.vector.tensor_scalar(acc[:, t, 0:D], acc[:, t, 0:D], 0.0, None, ALU.max))
                last.wait()
                last.step(nc.vector.tensor_tensor(big[:, 0:NT, 0:D], acc[:, 0:NT, 0:D], acc[:, 0:NT, 0:D], ALU.mult))
                last.step(nc.vector.reduce_sum(rstd[:, :], big[:, 0:NT, 0:D], AX.X))
                dve.sem_inc(s_pre, 1)
                dve.wait_ge(s_tanh, 1)
                last.step(nc.vector.tensor_scalar(rstd[:, :], rstd[:, :], NORM_EPS, None, ALU.max))
                last.step(nc.vector.reciprocal(rstd[:, :], rstd[:, :]))
                for t in range(NT):
                    last(nc.vector.scalar_tensor_tensor(x[:, t, :], acc[:, t, 0:D], rstd[:, t:t + 1], x[:, t, :],
                                                        ALU.mult, ALU.add))
                last.wait()
                dve.sem_inc(s_tanh, 1)
            if how == "tanh":
                for t in range(NT):
                    last(nc.vector.scalar_tensor_tensor(acc[:, t, 0:D], acc[:, t, 0:D], dinv[:, t:t + 1], brow[:, :],
                                                        ALU.mult, ALU.add))
                    last.wait()
                    dve.sem_inc(s_pre, 1)
                for t in range(NT):
                    dve.wait_ge(s_tanh, t + 1)
                    last(nc.vector.scalar_tensor_tensor(x[:, t, :], acc[:, t, 0:D], v["zero_mean"][:, 0:1], x[:, t, :],
                                                        ALU.add, ALU.add))
                last.wait()
            v["layer_norm"](dve, last, s_var, s_std)


def layer_mlp(nc, A, stage, v):
    l, xT, hT, acc, column, ident, sb, rows, node_d = (
        v[n] for n in ("l", "xT", "hT", "acc", "column", "ident", "sb", "rows", "node_d"))
    w = (v["w_sb"], v["w2_sb"])
    with ExitStack() as own:
        bstats = sb(f"bstats{l}", [P, KC, len(CHUNKS), 6], F32, own)
        bmv = sb(f"bmv{l}", [P, KC, 2], F32, own)
        scale = sb(f"bscale{l}", [P, KC], F32, own)
        shift = sb(f"bshift{l}", [P, KC], F32, own)
        weights = [A["L1_gnn_W1"], A["L1_gnn_W2"]]
        vectors = ["L1_gnn_b1", "L1_gnn_g1", "L1_gnn_be1", "L1_gnn_b2", "L1_gnn_g_out", "L1_gnn_b_out"]
        for m, (src, dst) in enumerate(((xT, hT), (hT, xT))):
            with ExitStack() as ps, stage("s_w", "s_prod", "s_out", "s_stat", "s_std", "s_chain", "s_coef", "s_vec") as (
                    (s_w, s_prod, s_out, s_stat, s_std, s_chain, s_coef, s_vec), block):
                prod = [ps.enter_context(nc.psum_tensor(f"mlp{l}{m}{i}", [P, NCOL], F32)) for i in range(4)]
                units = [(c, n, f) for c, n in CHUNKS for f in range(KC)]

                @block.sync
                def _(sp):
                    for k in range(KC):
                        sp.dma_start(w[m][:, k, 0:D], weights[m][l, k * P:(k + 1) * P, :]).then_inc(s_w, 16)
                    for i in range(3):
                        for k in range(KC):
                            sp.dma_start(column[:, 3 * m + i, k:k + 1],
                                         A[vectors[3 * m + i]][l, k * P:(k + 1) * P].rearrange("(p a) -> p a", a=1)).then_inc(s_vec, 16)

                @block.tensor
                def _(pe):
                    pe.wait_ge(s_w, 16 * KC)
                    for u, (c, n, f) in enumerate(units):
                        if u >= 4:
                            pe.wait_ge(s_out, u - 3)
                        for k in range(KC):
                            last = nc.tensor.matmul(prod[u % 4][:, 0:n], w[m][:, k, f * P:(f + 1) * P], src[:, k, c:c + n],
                                                    start=k == 0, stop=k == KC - 1)
                        last.then_inc(s_prod, 1)

                @block.scalar
                def _(act):
                    act.wait_ge(s_vec, 16 * 3 * KC)
                    for u, (c, n, f) in enumerate(units):
                        act.wait_ge(s_prod, u + 1)
                        nc.scalar.activation(dst[:, f, c:c + n], prod[u % 4][:, 0:n], ACT.Identity,
                                             bias=column[:, 3 * m, f:f + 1]).then_inc(s_out, 1)
                    act.wait_ge(s_stat, 1)
                    nc.scalar.activation(scale[:, :], bmv[:, :, 1], ACT.Sqrt, bias=v["eps"][:, 0:1]).then_inc(s_std, 1)
                    act.wait_ge(s_coef, 1)
                    for f in range(KC):
                        nc.scalar.activation(dst[:, f, :], dst[:, f, :], ACT.Relu, bias=shift[:, f:f + 1], scale=scale[:, f:f + 1])

                @block.vector
                def _(dve):
                    last = Chain(dve, s_chain)
                    dve.wait_ge(s_vec, 16 * 3 * KC)
                    for u, (c, n, f) in enumerate(units):
                        dve.wait_ge(s_out, u + 1)
                        n = min(n, N - c)
                        last(nc.vector.bn_stats(bstats[:, f, c // NCOL, :], dst[:, f, c:c + n]))
                    last.wait()
                    for f in range(KC):
                        last(nc.vector.bn_aggr(bmv[:, f, :], bstats[:, f, :, :]))
                    last.wait()
                    dve.sem_inc(s_stat, 1)
                    dve.wait_ge(s_std, 1)
                    last.step(nc.vector.reciprocal(scale[:, :], scale[:, :]))
                    last.step(nc.vector.tensor_tensor(scale[:, :], scale[:, :], column[:, 3 * m + 1, :], ALU.mult))
                    last.step(nc.vector.tensor_tensor(shift[:, :], bmv[:, :, 0], scale[:, :], ALU.mult))
                    last.step(nc.vector.tensor_tensor(shift[:, :], column[:, 3 * m + 2, :], shift[:, :], ALU.subtract))
                    dve.sem_inc(s_coef, 1)

        with ExitStack() as ps, stage("s_turned", "s_copied", "s_stored") as ((s_turned, s_copied, s_stored), block):
            turned = [ps.enter_context(nc.psum_tensor(f"back{l}{i}", [P, 2, D], F32)) for i in range(4)]
            units = [(t, min(2, NT - t)) for t in range(0, NT, 2)]

            @block.tensor
            def _(pe):
                for n, (t0, nt) in enumerate(units):
                    if n >= 4:
                        pe.wait_ge(s_copied, n - 3)
                    for t in range(nt):
                        for k in range(KC):
                            last = nc.tensor.transpose(turned[n % 4][:, t, k * P:(k + 1) * P],
                                                       xT[:, k, (t0 + t) * P:(t0 + t + 1) * P], ident[:, :])
                    last.then_inc(s_turned, 1)

            @block.scalar
            def _(act):
                for n, (t0, nt) in enumerate(units):
                    act.wait_ge(s_turned, n + 1)
                    nc.scalar.activation(acc[:, t0:t0 + nt, 0:D], turned[n % 4][:, 0:nt, :], ACT.Copy).then_inc(s_copied, 1)

            @block.sync
            def _(sp):
                if l < LAYERS - 1:
                    for t0 in range(0, NT, 5):
                        sp.wait_ge(s_copied, (t0 + 5 + 1) // 2)
                        sp.dma_start(rows(node_d)[:, t0:t0 + 5, :], acc[:, t0:t0 + 5, 0:D]).then_inc(s_stored, 16)
                    sp.wait_ge(s_stored, 16 * (NT // 5))


def first_table(nc, A, stage, v):
    sb, rows, z_d, xT, big, acc, w_sb, w2_sb, dst_score, pos_src = (
        v[n] for n in ("sb", "rows", "z_d", "xT", "big", "acc", "w_sb", "w2_sb", "dst_score", "pos_src"))
    with ExitStack() as ps, ExitStack() as small, stage(
            "s_zero", "s_load", "s_prod", "s_weights", "s_row", "s_ready", "s_stored", "s_rows", "s_chain", "s_dve",
            "s_pe", "s_parts") as (
            (s_zero, s_load, s_prod, s_weights, s_row, s_ready, s_stored, s_rows, s_chain, s_dve, s_pe, s_parts), block):
        a_diag = sb("a_diag", [P, KC, 2 * H], F32, small)
        rest = sb("rest", [P, NT, H], F32, small)
        score_w = ps.enter_context(nc.psum_tensor("score_w", [P, KC, 2 * H], F32))
        prod = [ps.enter_context(nc.psum_tensor(f"z_prod{i}", [P, 512], F32)) for i in range(3)]
        sums = ps.enter_context(nc.psum_tensor("sums3", [P, 2, 32], F32))
        totals = ps.enter_context(nc.psum_tensor("totals", [P, 8], F32))
        wide = [ps.enter_context(nc.psum_tensor(f"wide_b{i}", [P, 512], F32)) for i in range(2)]
        heads = w_sb[:, :, 0:HZ].rearrange("p k (h o) -> p k h o", h=H)
        parts = big[:, :, AW:ZW].bitcast(BF16)
        scores = big[:, :, 0:HZ].rearrange("p t (h o) -> p t h o", h=H)[:, :, :, OUT]

        @block.sync
        def _(sp):
            sp.wait_ge(s_zero, 3)
            for k in range(KC):
                sp.dma_start(w2_sb[:, k, :], A["W_rows"][k * P:(k + 1) * P, :]).then_inc(s_load, 16)
            for h in range(H):
                at = (h * OUT) % P
                for side in range(2):
                    c = side * H + h
                    sp.dma_start(a_diag[at:at + OUT, h * OUT // P, c:c + 1],
                                 A["L0_gnn_attn"][0, side * OUT:(side + 1) * OUT].rearrange("(p a) -> p a", a=1)).then_inc(s_load, 16)
            for k in range(KC):
                sp.dma_start(xT[:, k, 0:N], A["xT"][k * P:(k + 1) * P, :]).then_inc(s_load, 16)
                sp.dma_start(heads[:, k, :, 0:OUT],
                             A["W_cols"][k * P:(k + 1) * P, :].rearrange("p (h o) -> p h o", h=H)).then_inc(s_load, 16)
            v["load_by_dst"](sp, GROUPS // 2, GROUPS // 2, s_rows)
            sp.wait_ge(s_parts, 1)
            for t0 in range(0, NT, 5):
                sp.dma_start(rows(z_d)[:, t0:t0 + 5, :], big[:, t0:t0 + 5, :]).then_inc(s_stored, 16)
            sp.wait_ge(s_stored, 16 * (NT // 5))

        @block.gpsimd
        def _(pool):
            nc.gpsimd.memset(a_diag[:, :, :], 0.0).then_inc(s_zero, 1)
            nc.gpsimd.memset(xT[:, :, N:NPAD], 0.0).then_inc(s_zero, 1)
            nc.gpsimd.memset(big[:, :, HZ:AW], 1.0).then_inc(s_zero, 1)
            nc.gpsimd.memset(acc[:, :, :], 0.0).then_inc(s_zero, 1)
            pool.wait_ge(s_zero, 4)

        @block.tensor
        def _(pe):
            pe.wait_ge(s_load, 16 * (3 * KC + 2 * H))
            for m in range(KC):
                for k in range(KC):
                    last = nc.tensor.matmul(score_w[:, m, :], w2_sb[:, k, m * P:(m + 1) * P], a_diag[:, k, :],
                                            start=k == 0, stop=k == KC - 1)
            last.then_inc(s_prod, 1)
            pe.wait_ge(s_weights, 1)
            for t in range(NT):
                if t >= 3:
                    pe.wait_ge(s_row, t - 2)
                for k in range(KC):
                    last = nc.tensor.matmul(prod[t % 3][:, 0:HZ + H], xT[:, k, t * P:(t + 1) * P], w_sb[:, k, :],
                                            start=k == 0, stop=k == KC - 1)
                last.then_inc(s_prod, 1)
            pe.wait_ge(s_dve, 1)
            nc.tensor.matmul(sums[:, 0, 0:NT + 1], v["before"][:, :], v["count_src"][:, :], start=True, stop=True)
            nc.tensor.matmul(sums[:, 1, 0:NT + 1], v["every"][:, :], v["count_src"][:, :], start=True, stop=True)
            nc.tensor.matmul(totals[0:NT, 0:1], v["count_src"][:, 0:NT], v["every"][:, 0:1], start=True, stop=True).then_inc(s_pe, 1)
            v["tables_pe"](pe, s_dve, s_pe, 1, totals[0:NT, 1:2], wide)

        @block.scalar
        def _(act):
            act.wait_ge(s_prod, 1)
            nc.scalar.activation(heads[:, :, :, OUT], score_w[:, :, 0:H], ACT.Copy)
            nc.scalar.activation(w_sb[:, :, HZ:HZ + H], score_w[:, :, H:2 * H], ACT.Copy).then_inc(s_weights, 1)
            for t in range(NT):
                act.wait_ge(s_prod, t + 2)
                nc.scalar.activation(dst_score[:, t, :], prod[t % 3][:, HZ:HZ + H], ACT.Copy)
                nc.scalar.activation(big[:, t, 0:HZ], prod[t % 3][:, 0:HZ], ACT.Copy).then_inc(s_row, 1)
            v["load_by_dst"](act, 0, GROUPS // 2, s_rows)

        @block.vector
        def _(dve):
            last = Chain(dve, s_chain)
            v["tile_numbers"](last, v["key_src"], v["tile_f"])
            last(nc.vector.scalar_tensor_tensor(v["rec_src"][:, :, 1], v["tile_f"][:, :], -float(P), v["rec_src"][:, :, 1],
                                                ALU.mult, ALU.add))
            v["count_tiles"](last, v["count_src"])
            dve.wait_ge(s_row, NT)
            first = scores
            for i in range(PARTS):
                to = parts[:, :, i * H:(i + 1) * H]
                last.step(nc.vector.tensor_copy(to, first))
                if i < PARTS - 1:
                    last.step(nc.vector.tensor_tensor(rest[:, :, :], first, to, ALU.subtract))
                    first = rest[:, :, :]
            dve.sem_inc(s_parts, 1)
            step = v["exchange"](dve, s_dve, s_pe)
            step()
            sizes, sizes_i = v["sizes"], v["sizes_i"]
            last.step(nc.vector.tensor_scalar(sizes_i[:, :], sums[:, 1, 0:NT + 1], float(GROUP - 1), None, ALU.add))
            last.step(nc.vector.tensor_scalar(sizes_i[:, :], sizes_i[:, :], SHIFT, None, ALU.logical_shift_right))
            last.step(nc.vector.tensor_scalar(sizes[:, :], sizes_i[:, :], float(GROUP), None, ALU.mult))
            slot, slot_p, slot_b = v["slot"], v["slot_p"], v["slot_b"]
            v["positions"](last, sums[:, 0, 0:NT + 1], sizes[:, :], slot)
            last(nc.vector.tensor_scalar(slot_p[:, :], slot[:, :], P - 1, None, ALU.bitwise_and))
            last.step(nc.vector.tensor_scalar(slot_b[:, :], slot[:, :], P.bit_length() - 1, None, ALU.logical_shift_right))
            last.step(nc.vector.scalar_tensor_tensor(pos_src[:, :], slot_p[:, :], float(BLOCKS + SPARE), slot_b[:, :],
                                                     ALU.mult, ALU.add))
            v["tables"](last, step, v["tile_by_src"], totals[0:NT, 0:1], totals[0:NT, 1:2], wide)
            dve.wait_ge(s_rows, 16 * GROUPS)
            at = v["list_dst"][:, :, 1].rearrange("p (g b) -> p g b", b=BPG)
            last.step(nc.vector.tensor_tensor(at, at, v["key_by_dst"][:, :].rearrange("p (g b) -> p g b", b=1).broadcast_to(
                [P, GROUPS, BPG]), ALU.subtract))


def attention(nc, A, stage, v):
    sb, z_d, x, acc, ident, iota, gathered, select, slot_node, dst_score = (
        v[n] for n in ("sb", "z_d", "x", "acc", "ident", "iota", "gathered",
                       "select", "slot_node", "dst_score"))
    edges, dinv, rec_src, pos_src = v["list_dst"], v["dinv"], v["rec_src"], v["pos_src"]
    tile_of_group = v["tile_by_dst"]
    with ExitStack() as own:
        node_state = sb("node_state", [P, NT + 1, 2 * H], F32, own)
        raise_to = sb("raise_to", [P, 2 * H], F32, own)
        pick = sb("pick", [P, H, P], BF16, own)
        ident4 = sb("ident4", [P, H, P], BF16, own)
        ident_b = sb("ident_b", [P, P], BF16, own)
        pick_col = sb("pick_col", [P, H], F32, own)
        miss = sb("miss", [P, 4, GROUP], BF16, own)
        select_t = sb("select_t", [P, 2, GROUP], F32, own)
        one = sb("one", [P, 1], F32, own)
        neg = sb("neg", [P, 1], F32, own)
        score_t = sb("score_t", [P, 2, GROUP], BF16, own)
        block_top = sb("block_top", [P, H], F32, own)
        node_side = sb("node_side", [P, 2 * H], F32, own)
        raised = sb("raised", [P, H], F32, own)
        keep = sb("keep", [P, 4, H], F32, own)
        logit = sb("logit", [P, 2, BPG, H], F32, own)
        logit2 = sb("logit2", [P, BPG, H], F32, own)
        rec_stage = sb("rec_stage_src", [P, 2, SB, REC], F32, own)
        pos_stage = sb("pos_stage_src", [P, 2, SB], U32, own)

        with stage("s_init") as ((s_init,), block):
            @block.vector
            def _(dve):
                last = Chain(dve, s_init)
                nc.vector.tensor_copy(node_state[:, :, 0:H], dst_score[:, :, :])
                nc.vector.memset(node_state[:, :, H:2 * H], NEG * SLOPE)
                nc.vector.memset(raise_to[:, :], NEG)
                nc.vector.memset(score_t[:, :, :], 0.0)
                nc.vector.memset(one[:, :], 1.0)
                nc.vector.memset(neg[:, :], NEG)
                nc.vector.tensor_copy(ident_b[:, :], ident[:, :])
                nc.vector.tensor_copy(ident4[:, :, :], ident[:, :].rearrange("p (a m) -> p a m", a=1).broadcast_to([P, H, P]))
                last.step(nc.vector.tensor_tensor(pick_col[:, :], ident[:, 0:H], ident[:, H:2 * H], ALU.add))
                last.step(nc.vector.tensor_tensor(pick_col[:, :], pick_col[:, :], ident[:, 2 * H:3 * H], ALU.add))
                last.step(nc.vector.tensor_copy(pick[:, :, :], pick_col[:, :].rearrange("p (h m) -> p h m", m=1).broadcast_to([P, H, P])))

        names = ("s_index", "s_seen", *GATHERED, "s_hot", "s_miss", "s_turned", "s_score_t",
                 "s_miss_t", "s_masked_t", "s_chain", "s_top", "s_nodes", "s_keep", "s_select_t", "s_side", "s_logit", "s_exp", "s_row",
                 "s_sum", "s_scaled", "s_added", "s_stage0", "s_stage1", "s_scat0", "s_scat1")
        with ExitStack() as ps, stage(*names) as (
                (s_index, s_seen, *s_gath, s_hot, s_miss, s_turned, s_score_t,
                 s_miss_t, s_masked_t, s_chain, s_top, s_nodes, s_keep, s_select_t, s_side, s_logit, s_exp, s_row,
                 s_sum, s_scaled, s_added, s_stage0, s_stage1, s_scat0, s_scat1), block):
            s_stage, s_scat = (s_stage0, s_stage1), (s_scat0, s_scat1)
            masked_t = ps.enter_context(nc.psum_tensor("masked_t", [P, BPG, H, P], F32))
            miss_t = ps.enter_context(nc.psum_tensor("miss_t", [P, 2 * 512], BF16))
            turned = ps.enter_context(nc.psum_tensor("turned", [P, 2 * 512], BF16))
            side = [ps.enter_context(nc.psum_tensor(f"side{i}", [P, BPG, 2 * H], F32)) for i in range(2)]
            total = [ps.enter_context(nc.psum_tensor(f"total{i}", [P, 512], F32)) for i in range(2)]

            def wait(engine, sem, value):
                if not isinstance(value, int) or value > 0:
                    engine.wait_ge(sem, value)

            def place_of(g):
                g = g % GPI
                return g // GPC, (g % GPC) * BPG

            def turns(engine, body):
                body(0, first=True, last=False)
                with engine.Fori(1, ITER - 1) as it:
                    body(it, first=False, last=False)
                body(ITER - 1, first=False, last=True)

            @block.sync
            def _(sp):
                def load(i, h):
                    col = i * (2 * SB) + h * SB
                    sp.dma_start(rec_stage[:, h, :, :], rec_src[:, bass.ds(col, SB), :]).then_inc(s_stage[h], 16)
                    sp.dma_start(pos_stage[:, h, :], pos_src[:, bass.ds(col, SB)]).then_inc(s_stage[h], 16)

                for h in range(2):
                    load(0, h)
                with sp.Fori(1, SPAIRS) as i:
                    for h in range(2):
                        sp.wait_ge(s_scat[h], i * (16 * SB))
                        load(i, h)

            @block.gpsimd
            def _(pool):
                def turn(it, h, pair):
                    for r in range(RING):
                        pool.wait_ge(s_index, it * RING + (r + 1))
                        pool.sem_inc(s_seen, 1)
                        for j in range(BPC):
                            pool.indirect_dma_start(gathered[:, r, j, 0:ZW], None, z_d,
                                                    bass.IndirectOffsetOnAxis(ap=slot_node[:, r, j:j + 1], axis=0)
                                                    ).then_inc(s_gath[r], 16)
                        if pair is not None:
                            if r == 0:
                                pool.wait_ge(s_stage[h], pair * 32 + 32)
                                pool.sem_inc(s_seen, 1)
                            for j in range(r * SG, (r + 1) * SG):
                                pool.indirect_dma_start(
                                    v["list_src_d"], bass.IndirectOffsetOnAxis(ap=pos_stage[:, h, j:j + 1], axis=0),
                                    rec_stage[:, h, j, :], None).then_inc(s_scat[h], 16)

                turn(0, 0, None)
                with pool.Fori(0, SPAIRS) as pair:
                    for h in range(2):
                        turn(pair * 2 + (h + 1), h, pair)
                for it in range(2 * SPAIRS + 1, ITER):
                    turn(it, 0, None)
                for h in range(2):
                    pool.wait_ge(s_scat[h], 16 * SB * SPAIRS)

            @block.scalar
            def _(act):
                def index(it, r):
                    nc.scalar.activation(slot_node[:, r, :], edges[:, bass.ds(it * BPI + r * BPC, BPC), 0],
                                         ACT.Copy).then_inc(s_index, 1)

                def copy_scores(it, g):
                    n = it * GPI + g
                    act.wait_ge(s_turned, n + 1)
                    wait(act, s_masked_t, n - 1)
                    nc.scalar.activation(score_t[0:PARTS * H, g % 2, :], turned[0:PARTS * H, 0:GROUP], ACT.Copy).then_inc(s_score_t, 1)

                def make_miss(it, g):
                    n = it * GPI + g
                    r, b0 = place_of(g)
                    act.wait_ge(s_hot, n + 1)
                    wait(act, s_masked_t, n - 3)
                    nc.scalar.activation(miss[:, g % 4, :].rearrange("p (b m) -> p b m", m=P), select[:, r, b0:b0 + BPG, :], ACT.Identity,
                                         scale=-NEG, bias=neg[:, 0:1]).then_inc(s_miss, 1)

                def copy_miss(it, g):
                    n = it * GPI + g
                    act.wait_ge(s_miss_t, n + 1)
                    wait(act, s_side, n - 1)
                    nc.scalar.activation(select_t[:, g % 2, :], miss_t[:, 0:GROUP], ACT.Identity, scale=-1.0 / NEG,
                                         bias=one[:, 0:1]).then_inc(s_select_t, 1)

                def weigh(n, g):
                    r, b0 = place_of(g)
                    act.wait_ge(s_logit, n + 1)
                    slot_rows = gathered[:, r, b0:b0 + BPG, 0:HZ].rearrange("p b (q o) -> p b q o", q=H)
                    nc.scalar.activation(slot_rows[:, :, :, OUT], logit[:, g % 2, :, :], ACT.Exp).then_inc(s_exp, 1)
                    act.wait_ge(s_exp, n + 1)
                    for b in range(BPG):
                        for q in range(H):
                            ins = nc.scalar.activation(slot_rows[:, b, q, 0:OUT], slot_rows[:, b, q, 0:OUT], ACT.Identity,
                                                       scale=slot_rows[:, b, q, OUT:HW])
                    ins.then_inc(s_row, 1)

                def body(it, first, last):
                    for g in range(GPI):
                        n = it * GPI + g
                        if not (last and g >= GPI - 2):
                            copy_scores(it, g + 2)
                        if not (last and g == GPI - 1):
                            copy_miss(it, g + 1)
                        act.wait_ge(s_nodes, n + 1)
                        wait(act, s_added, n - 3)
                        nc.scalar.activation(keep[:, g % 4, :], raised[:, :], ACT.Exp).then_inc(s_keep, 1)
                        if not (first and g == 0):
                            weigh(n - 1, (g - 1) % GPI)
                        ahead = 1 if g >= 2 else 0
                        if not (last and ahead):
                            wait(act, s_sum, n - 1)
                            index(it + ahead, (g - 2) % RING)
                        if not (last and g >= GPI - AHEAD):
                            make_miss(it, g + AHEAD)
                    if last:
                        weigh(n, GPI - 1)

                for r in range(RING - 2):
                    index(0, r)
                for g in range(AHEAD):
                    make_miss(0, g)
                copy_scores(0, 0)
                copy_miss(0, 0)
                copy_scores(0, 1)
                turns(act, body)

            @block.tensor
            def _(pe):
                def turn_miss(it, g):
                    n = it * GPI + g
                    r, b0 = place_of(g)
                    pe.wait_ge(s_miss, n + 1)
                    wait(pe, s_select_t, n)
                    for b in range(BPG):
                        ins = nc.tensor.transpose(miss_t[:, b * P:(b + 1) * P], miss[:, g % 4, b * P:(b + 1) * P], ident_b[:, :])
                    ins.then_inc(s_miss_t, 1)

                def turn_scores(it, g):
                    n = it * GPI + g
                    r, b0 = place_of(g)
                    pe.wait_ge(s_gath[r], (it + g // GPI) * (16 * BPC) + 16 * BPC)
                    wait(pe, s_score_t, n)
                    for b in range(BPG):
                        ins = nc.tensor.transpose(turned[0:PARTS * H, b * P:(b + 1) * P],
                                                  gathered[:, r, b0 + b, AW:ZW].bitcast(BF16), ident_b[:, :])
                    ins.then_inc(s_turned, 1)

                def sum_rows(n, g):
                    r, b0 = place_of(g)
                    pe.wait_ge(s_row, n + 1)
                    pe.wait_ge(s_hot, n + 1)
                    wait(pe, s_added, n - 1)
                    for b in range(BPG):
                        ins = nc.tensor.matmul(total[g % 2][:, 0:AW], select[:, r, b0 + b, :],
                                               gathered[:, r, b0 + b, 0:AW], start=b == 0, stop=b == BPG - 1)
                    ins.then_inc(s_sum, 1)

                def spread(it, g):
                    n = it * GPI + g
                    pe.wait_ge(s_score_t, n + 1)
                    wait(pe, s_top, n)
                    for b in range(BPG):
                        nc.tensor.matmul(masked_t[:, b, :, :], miss[:, g % 4, b * P:(b + 1) * P], ident4[:, :, :],
                                         start=True, stop=False)
                        for q in range(H):
                            ins = nc.tensor.matmul(masked_t[:, b, q, :], pick[:, q, :], score_t[:, g % 2, b * P:(b + 1) * P],
                                                   start=False, stop=q == H - 1)
                    ins.then_inc(s_masked_t, 1)

                def body(it, first, last):
                    for g in range(GPI):
                        n = it * GPI + g
                        if not (last and g == GPI - 1):
                            spread(it, g + 1)
                        if not (first and g < 2):
                            sum_rows(n - 2, (g - 2) % GPI)
                        if not (last and g >= GPI - 2):
                            turn_scores(it, g + 2)
                            turn_miss(it, g + 2)
                        pe.wait_ge(s_select_t, n + 1)
                        pe.wait_ge(s_nodes, n + 1)
                        wait(pe, s_logit, n - 1)
                        for b in range(BPG):
                            ins = nc.tensor.matmul(side[g % 2][:, b, :], select_t[:, g % 2, b * P:(b + 1) * P], node_side[:, :],
                                                   start=True, stop=True)
                        ins.then_inc(s_side, 1)
                    if last:
                        for back in (1, 0):
                            sum_rows(n - back, GPI - 1 - back)

                for g in range(2):
                    turn_scores(0, g)
                    turn_miss(0, g)
                spread(0, 0)
                turns(pe, body)

            @block.vector
            def _(dve):
                NODE_LINKS, SLOT_LINKS = 4, 3

                def one_hot(it, g, b):
                    n = it * GPI + g
                    r, b0 = place_of(g)
                    wait(dve, s_sum, n - (GPI - 1))
                    ins = nc.vector.tensor_scalar(select[:, r, b0 + b, :], iota[:, :], edges[:, bass.ds(n * BPG + b, 1), 1],
                                                  None, ALU.is_equal)
                    if b == BPG - 1:
                        ins.then_inc(s_hot, 1)

                def rescale(n, g, t):
                    dve.wait_ge(s_keep, n + 1)
                    wait(dve, s_added, n)
                    sums = acc[:, bass.ds(t, 1), 0:HZ].rearrange("p a (q o) -> p (a q) o", q=H)
                    nc.vector.tensor_tensor(sums, sums,
                                            keep[:, g % 4, :].rearrange("p (q a) -> p q a", a=1).broadcast_to([P, H, HW]),
                                            ALU.mult).then_inc(s_scaled, 1)

                def add(n, g, t):
                    dve.wait_ge(s_scaled, n + 1)
                    dve.wait_ge(s_sum, n + 1)
                    nc.vector.tensor_tensor(acc[:, bass.ds(t, 1), :], total[g % 2][:, 0:AW], acc[:, bass.ds(t, 1), :],
                                            ALU.add).then_inc(s_added, 1)

                def logits(n, g, link):
                    r, b0 = place_of(g)
                    dve.wait_ge(s_side, n + 1)
                    scores = gathered[:, r, b0:b0 + BPG, 0:HZ].rearrange("p b (q o) -> p b q o", q=H)
                    link(nc.vector.tensor_tensor(logit2[:, :, :], scores[:, :, :, OUT], side[g % 2][:, :, 0:H], ALU.add))
                    link(nc.vector.scalar_tensor_tensor(logit2[:, :, :], logit2[:, :, :], SLOPE, logit2[:, :, :],
                                                        ALU.mult, ALU.max))
                    link(nc.vector.tensor_tensor(logit2[:, :, :], logit2[:, :, :], side[g % 2][:, :, H:2 * H], ALU.subtract))
                    nc.vector.tensor_scalar(logit[:, g % 2, :, :], logit2[:, :, :], 0.0, None, ALU.min).then_inc(s_logit, 1)

                def body(it, first, last):
                    tiles = v["load_tiles"](dve, tile_of_group, it, LEAD)
                    tile_of = lambda g: tiles[LEAD + g]
                    for g in range(GPI):
                        n = it * GPI + g
                        c = [0 if first and g == 0 else n * (NODE_LINKS + SLOT_LINKS) - SLOT_LINKS]

                        def link(ins, between=None):
                            ins.then_inc(s_chain, 1)
                            c[0] = c[0] + 1
                            if between:
                                between()
                            dve.wait_ge(s_chain, c[0])

                        old = not (first and g < 3)
                        ahead = not (last and g >= GPI - AHEAD)
                        t = tile_of(g)
                        dve.wait_ge(s_masked_t, n + 1)
                        nc.vector.tensor_reduce(block_top[:, :], masked_t[:, :, :, :].rearrange("p b q e -> p q b e"),
                                                AX.XY, ALU.max).then_inc(s_top, 1)
                        if ahead:
                            one_hot(it, g + AHEAD, 0)
                        dve.wait_ge(s_top, n + 1)
                        state = node_state[:, bass.ds(t, 1), :]
                        link(nc.vector.tensor_tensor(block_top[:, :], block_top[:, :], state[:, 0, 0:H], ALU.add),
                             (lambda: one_hot(it, g + AHEAD, 1)) if ahead else None)
                        link(nc.vector.scalar_tensor_tensor(raise_to[:, H:2 * H], block_top[:, :], SLOPE, block_top[:, :],
                                                            ALU.mult, ALU.max),
                             (lambda: rescale(n - 3, (g - 3) % GPI, tile_of(g - 3))) if old else None)
                        wait(dve, s_side, n)
                        link(nc.vector.tensor_tensor(node_side[:, :], state[:, 0, :], raise_to[:, :], ALU.max))
                        wait(dve, s_keep, n)
                        link(nc.vector.tensor_tensor(raised[:, :], state[:, 0, H:2 * H], node_side[:, H:2 * H], ALU.subtract))
                        nc.vector.tensor_scalar(state[:, 0, H:2 * H], node_side[:, H:2 * H], 1.0, None, ALU.mult).then_inc(s_nodes, 1)
                        if old:
                            add(n - 3, (g - 3) % GPI, tile_of(g - 3))
                        if not (first and g == 0):
                            logits(n - 1, (g - 1) % GPI, link)
                    if last:
                        dve.wait_ge(s_logit, n)
                        logits(n, GPI - 1, link)
                        for back in (2, 1, 0):
                            rescale(n - back, GPI - 1 - back, tile_of(GPI - 1 - back))
                            add(n - back, GPI - 1 - back, tile_of(GPI - 1 - back))

                for g in range(AHEAD):
                    for b in range(BPG):
                        one_hot(0, g, b)
                turns(dve, body)

        rden = sb("rden", [P, NT, H], F32, own)
        with stage("s_chain", "s_deg", "s_root", "s_var", "s_std", "s_rows") as (
                (s_chain, s_deg, s_root, s_var, s_std, s_rows), block):
            @block.sync
            def _(sp):
                sp.dma_start(v["list_src"][:, :, :], v["list_src_d"].rearrange("(p b) w -> p b w", p=P)[:, 0:BLOCKS, :]).then_inc(s_rows, 16)
                sp.wait_ge(s_rows, 16)

            @block.scalar
            def _(act):
                act.wait_ge(s_deg, 1)
                nc.scalar.activation(dinv[:, :], dinv[:, :], ACT.Sqrt).then_inc(s_root, 1)
                act.wait_ge(s_var, 1)
                nc.scalar.activation(v["rstd"][:, :], v["meanvar"][:, :, 1], ACT.Sqrt, bias=v["eps"][:, 0:1]).then_inc(s_std, 1)

            @block.vector
            def _(dve):
                last = Chain(dve, s_chain)
                last.step(nc.vector.tensor_scalar(dinv[:, :], acc[:, 0:NT, HZ], 1.0, None, ALU.add))
                dve.sem_inc(s_deg, 1)
                sums = acc[:, 0:NT, 0:HZ].rearrange("p t (q o) -> p t q o", q=H)
                last.step(nc.vector.tensor_scalar(rden[:, :, :], sums[:, :, :, OUT], DEN_EPS, None, ALU.max))
                last.step(nc.vector.reciprocal(rden[:, :, :], rden[:, :, :]))
                for q in range(H):
                    last(nc.vector.tensor_tensor(sums[:, :, q, 0:OUT], sums[:, :, q, 0:OUT],
                                                 rden[:, :, q:q + 1].broadcast_to([P, NT, OUT]), ALU.mult))
                last.wait()
                for q in range(H):
                    last(nc.vector.tensor_tensor(x[:, :, q * OUT:(q + 1) * OUT], x[:, :, q * OUT:(q + 1) * OUT],
                                                 sums[:, :, q, 0:OUT], ALU.add))
                last.wait()
                dve.wait_ge(s_root, 1)
                last.step(nc.vector.reciprocal(dinv[:, :], dinv[:, :]))
                v["layer_norm"](dve, last, s_var, s_std)


_INS = ["x", "src", "dst", "edge_attr_8", "edge_weight", "L0_gnn_attn", "L1_gnn_W_in", "L1_gnn_b_in", "L1_gnn_W1",
        "L1_gnn_b1", "L1_gnn_g1", "L1_gnn_be1", "L1_gnn_W2", "L1_gnn_b2", "L1_gnn_g_out", "L1_gnn_b_out", "L2_gnn_W",
        "L2_gnn_b", "L3_gnn_W", "L3_gnn_b"]


def kernel(**inputs):
    import numpy as _np
    import concourse.bacc as _bacc
    from concourse.bass_utils import run_bass_kernel_spmd as _run

    laid = {name: _np.ascontiguousarray(inputs[name]) for name in _INS}
    laid["xT"] = _np.ascontiguousarray(_np.asarray(inputs["x"]).T)
    laid["W_rows"] = _np.ascontiguousarray(_np.asarray(inputs["L0_gnn_W"]).reshape(H * OUT, D))
    laid["W_cols"] = _np.ascontiguousarray(laid["W_rows"].T)
    nc = _bacc.Bacc("TRN2", target_bir_lowering=False, num_devices=1)
    arrays, handles = {}, {}
    for name, a in laid.items():
        arrays[f"in_{name}"] = a
        handles[name] = nc.dram_tensor(f"in_{name}", a.shape, mybir.dt.from_np(a.dtype), kind="ExternalInput").ap()
    handles["out"] = nc.dram_tensor("out_0", (N, D), F32, kind="ExternalOutput").ap()
    build(nc, handles)
    r = _run(nc, [arrays], core_ids=[0])
    return r.results[0]["out_0"]
```

```python
import concourse.bass as bass
from concourse import mybir
from contextlib import ExitStack, contextmanager

F32 = mybir.dt.float32
I32 = mybir.dt.int32
BF16 = mybir.dt.bfloat16
U32 = mybir.dt.uint32
U8 = mybir.dt.uint8
ALU = mybir.AluOpType
ACT = mybir.ActivationFunctionType
AX = mybir.AxisListType

P = 128
N = 3125
E = 53125
D = 256
H, OUT = 4, 64
LAYERS = 3
KC = D // P
NT = -(-N // P)
NPAD = NT * P
LAST = N - (NT - 1) * P
EC = -(-E // P)
EFULL = E // EC
ETAIL = E - EFULL * EC
RING = 8
BPC = 2
BPI = RING * BPC
GROUP = 2 * P
SHIFT = GROUP.bit_length() - 1
BPG = GROUP // P
GPC = BPC // BPG
GPI = RING * GPC
ITER = -(-((E + NT * (GROUP - 1)) // GROUP) // GPI)
GROUPS = ITER * GPI
BLOCKS = GROUPS * BPG
GATHERED = [f"s_gath{r}" for r in range(RING)]
LEAD = 4
BY_SP = GROUPS // 12 * 4
BY_ACT = GROUPS // 16 * 4
SPARE = BPG
TRASH = NT
REC = 4
HW = OUT + 1
HZ = H * HW
AW = HZ + 1
PARTS = 3
ZW = AW + PARTS * H // 2
LROWS = P * EC + GROUP
AWAY = -1.0e6
NEG = -2.0 ** 100
SLOPE = 0.01
LN_EPS = 1e-5
BN_EPS = 1e-5
NORM_EPS = 1e-12
DEN_EPS = 1e-9
NCOL = 512
CHUNKS = [(c, min(NCOL, NPAD - c)) for c in range(0, NPAD, NCOL)]
SU = 8
SET = 5
assert NT % SET == 0
AHEAD = 3
SITER = EC // (2 * SU)
assert SITER * 2 * SU == EC
SG = 2
SB = SG * RING
SPAIRS = EC // (2 * SB)
assert SPAIRS * 2 * SB == EC and 2 * SPAIRS < ITER
EA = E * 8 // 125


class Chain:

    def __init__(self, engine, sem):
        self.engine, self.sem, self.n = engine, sem, 0

    def __call__(self, instruction):
        instruction.then_inc(self.sem, 1)
        self.n += 1

    def wait(self):
        self.engine.wait_ge(self.sem, self.n)

    def step(self, instruction):
        self(instruction)
        self.wait()


def build(nc, A):
    stages = []

    @contextmanager
    def stage(*names):
        stages.append(names)
        sems = [nc.alloc_semaphore(f"{n}_{len(stages)}") for n in names]
        with nc.Block() as block:
            yield sems, block
        nc.clear_and_free_semaphores(sems)
        nc.all_engine_barrier()

    dram = {n: nc.dram_tensor(n, s, F32).ap() for n, s in (
        ("list_by_dst", [LROWS, REC]), ("list_by_src", [P * (BLOCKS + SPARE), REC]),
        ("z_table", [NPAD, ZW]), ("node_table", [NPAD, D]))}
    list_dst_d, list_src_d, z_d, node_d = (
        dram[n] for n in ("list_by_dst", "list_by_src", "z_table", "node_table"))

    with ExitStack() as outer:
        def sb(name, shape, dt=F32, where=outer):
            return where.enter_context(nc.sbuf_tensor(name, shape, dt))

        def rows(t):
            return t.rearrange("(t p) f -> p t f", p=P)

        tile_by_dst = sb("tile_by_dst", [1, LEAD + GROUPS], U8)
        tile_by_src = sb("tile_by_src", [1, LEAD + GROUPS], U8)
        row_by_dst = sb("row_by_dst", [1, GROUPS], I32)
        ident = sb("ident", [P, P])
        iota = sb("iota", [P, P])
        x = sb("x", [P, NT, D])
        acc = sb("acc", [P, NT + 1, AW])
        list_dst = sb("edges_by_dst", [P, BLOCKS, REC])
        list_src = sb("edges_by_src", [P, BLOCKS, REC])
        dst_score = sb("dst_score", [P, NT + 1, H])
        dinv = sb("dinv", [P, NT])
        rden = sb("rden", [P, NT, H])
        shift = sb("shift", [P, NT])
        stats = sb("node_stats", [P, NT, 6])
        meanvar = sb("node_meanvar", [P, NT, 2])
        rstd = sb("node_rstd", [P, NT])
        zero_mean = sb("zero_times_mean", [P, 1])
        eps = sb("eps", [P, 1])
        brow = sb("bias_row", [P, D])

        rec_src = sb("rec_src", [P, EC, REC])
        pos_src = sb("pos_src", [P, EC], U32)

        big = sb("big", [P, NT, ZW])
        xT = sb("xT", [P, KC, NPAD])
        hT = big[:, :, :].rearrange("p t f -> p (t f)")[:, 0:KC * NPAD].rearrange("p (k n) -> p k n", k=KC)
        w_sb = sb("w_sb", [P, KC, HZ + H])
        w2_sb = sb("w2_sb", [P, KC, D])
        column = sb("column", [P, 8, KC])

        pre = outer.enter_context(ExitStack())
        prefix = sb("prefix", [P, 2, EC], F32, pre)
        key_dst = sb("key_dst", [P, EC], I32, pre)
        key_src = sb("key_src", [P, EC], I32, pre)
        key_next = sb("key_next", [P, EC], I32, pre)
        weight = sb("weight", [P, EC], F32, pre)
        tile_f = sb("tile_f", [P, EC], F32, pre)
        tile_next = sb("tile_next", [P, EC], F32, pre)
        part = sb("part", [P, EC], I32, pre)
        ones_row = sb("ones_row", [P, EC], F32, pre)
        mask = sb("mask", [P, 2, EC], F32, pre)
        term = sb("term", [P, 2, EC], F32, pre)
        count_dst = sb("count_dst", [P, NT + 1], F32, pre)
        count_src = sb("count_src", [P, NT + 1], F32, pre)
        first_edge = sb("first_edge", [P, NT + 1], F32, pre)
        offset = sb("offset", [P, NT + 1], F32, pre)
        group_id = sb("group_id", [P, GROUPS], F32, pre)
        reached = sb("reached", [NT, GROUPS], F32, pre)
        row_f = sb("row_f", [1, GROUPS], F32, pre)
        key_by_dst = sb("key_by_dst", [P, GROUPS], F32, pre)
        groups_i = sb("groups_i", [NT, 1], I32, pre)
        groups_f = sb("groups_f", [NT, 1], F32, pre)
        group_end = sb("group_end", [NT, 1], F32, pre)
        surplus = sb("surplus", [NT, 1], F32, pre)
        surplus_row = sb("surplus_row", [NT, P], F32, pre)
        rec_dst = sb("rec_dst", [P, EC, REC], F32, pre)
        pos_f = sb("pos_f", [P, EC], F32, pre)
        sizes = sb("sizes", [P, NT + 1], F32, pre)
        sizes_i = sb("sizes_i", [P, NT + 1], I32, pre)
        slot = sb("slot", [P, EC], I32, pre)
        slot_p = sb("slot_p", [P, EC], I32, pre)
        slot_b = sb("slot_b", [P, EC], I32, pre)
        before = sb("before", [P, P], F32, pre)
        upto = sb("upto", [P, P], F32, pre)
        every = sb("every", [P, P], F32, pre)
        away = sb("away", [P, BPG, REC], F32, pre)
        attr = big[0:125, :, :].rearrange("p t f -> p (t f)")[:, 0:EA]
        attr_sum = sb("attr_sum", [P, 1], F32, pre)
        jumps = sb("jumps", [P, 1], F32, pre)
        unordered = sb("unordered", [P, 1], I32, pre)

        def tile_numbers(last, key, to):
            last.step(nc.vector.tensor_scalar(part[:, :], key[:, :], 7, None, ALU.logical_shift_right))
            last.step(nc.vector.tensor_copy(to[:, :], part[:, :]))

        def records(last, key, other, rec):
            last(nc.vector.tensor_copy(rec[:, :, 1], key[:, :]))
            last(nc.vector.tensor_scalar(rec[:, :, 0], other[:, :], float(N - 1), None, ALU.min))
            last(nc.vector.tensor_copy(rec[:, :, 2], weight[:, :]))

        def tables(last, pe_steps, tile_of, totals, small, wide):
            last.step(nc.vector.tensor_scalar(groups_i[:, :], totals, float(GROUP - 1), None, ALU.add))
            last.step(nc.vector.tensor_scalar(groups_i[:, :], groups_i[:, :], SHIFT, None, ALU.logical_shift_right))
            last.step(nc.vector.tensor_copy(groups_f[:, :], groups_i[:, :]))
            last.step(nc.vector.scalar_tensor_tensor(surplus[:, :], groups_f[:, :], -float(GROUP), totals,
                                                     ALU.mult, ALU.add))
            last.step(nc.vector.tensor_copy(surplus_row[:, :], surplus[:, :].broadcast_to([NT, P])))
            pe_steps()
            last.step(nc.vector.tensor_copy(group_end[:, :], small))
            last.step(nc.vector.tensor_scalar(reached[:, 0:GROUPS], group_id[0:NT, 0:GROUPS], group_end[:, 0:1], None, ALU.is_ge))
            pe_steps()
            last.step(nc.vector.tensor_copy(tile_of[0:1, LEAD:LEAD + GROUPS], wide[0][0:1, 0:GROUPS]))

        def tables_pe(pe, s_dve, s_pe, n0, small, wide):
            pe.wait_ge(s_dve, n0 + 1)
            nc.tensor.matmul(small, upto[0:NT, 0:NT], groups_f[:, :], start=True, stop=True).then_inc(s_pe, 1)
            pe.wait_ge(s_dve, n0 + 2)
            nc.tensor.matmul(wide[0][:, 0:GROUPS], every[0:NT, :], reached[:, 0:GROUPS], start=True, stop=True)
            nc.tensor.matmul(wide[1][:, 0:GROUPS], surplus_row[:, :], reached[:, 0:GROUPS], start=True, stop=True).then_inc(s_pe, 1)

        def exchange(dve, s_dve, s_pe):
            n = [0]

            def step():
                n[0] += 1
                dve.sem_inc(s_dve, 1)
                dve.wait_ge(s_pe, n[0])
            return step

        def positions(last, ahead, sizes, pos):
            last.step(nc.vector.tensor_tensor_scan(first_edge[:, :], ones_row[:, 0:NT + 1], sizes, 0.0, ALU.mult, ALU.add))
            last.step(nc.vector.tensor_tensor(offset[:, :], first_edge[:, :], sizes, ALU.subtract))
            last.step(nc.vector.scalar_tensor_tensor(offset[:, :], offset[:, :], -1.0, ahead, ALU.add, ALU.add))
            last(nc.vector.memset(pos_f[:, :], 0.0))
            for t in range(NT + 1):
                last.step(nc.vector.tensor_scalar(mask[:, t % 2, :], tile_f[:, :], float(t), None, ALU.is_equal))
                last.step(nc.vector.tensor_tensor_scan(prefix[:, t % 2, :], ones_row[:, :], mask[:, t % 2, :], 0.0, ALU.mult, ALU.add))
                last.step(nc.vector.scalar_tensor_tensor(term[:, t % 2, :], prefix[:, t % 2, :], offset[:, t:t + 1],
                                                         mask[:, t % 2, :], ALU.add, ALU.mult))
                last(nc.vector.tensor_tensor(pos_f[:, :], pos_f[:, :], term[:, t % 2, :], ALU.add))
            last.wait()
            last.step(nc.vector.tensor_copy(pos[:, :], pos_f[:, :]))

        def count_tiles(last, counts):
            for t in range(NT + 1):
                last.step(nc.vector.tensor_scalar(mask[:, t % 2, :], tile_f[:, :], float(t), None, ALU.is_equal, ALU.add,
                                                  accum_out=counts[:, t:t + 1]))
            last.wait()

        with ExitStack() as ps, stage(
            "s_cleared", "s_edges", "s_const", "s_pool", "s_chain", "s_dve", "s_pe", "s_x", "s_attr",
        ) as ((s_cleared, s_edges, s_const, s_pool, s_chain, s_dve, s_pe, s_x, s_attr), block):
            sums = ps.enter_context(nc.psum_tensor("sums", [P, 64], F32))
            wide = [ps.enter_context(nc.psum_tensor(f"wide{i}", [P, 512], F32)) for i in range(2)]

            @block.sync
            def _(sp):
                def load(name, to, first):
                    sp.dma_start(to[0:EFULL, :], A[name][first:EFULL * EC + first].rearrange("(p c) -> p c", c=EC)).then_inc(s_edges, 16)
                    sp.dma_start(to[EFULL:EFULL + 1, 0:ETAIL - first],
                                 A[name][EFULL * EC + first:E].rearrange("(p c) -> p c", p=1)).then_inc(s_edges, 16)
                sp.wait_ge(s_cleared, 1)
                load("dst", key_dst, 0)
                load("dst", key_next, 1)
                load("src", key_src, 0)
                load("edge_weight", weight, 0)
                sp.dma_start(attr[:, :], A["edge_attr_8"].rearrange("(p e) a -> p (e a)", p=125)).then_inc(s_attr, 16)
                sp.dma_start(x[:, 0:NT - 1, :],
                             A["x"][0:(NT - 1) * P, :].rearrange("(t p) f -> p t f", p=P)).then_inc(s_x, 16)
                sp.dma_start(x[0:LAST, NT - 1, :], A["x"][(NT - 1) * P:N, :]).then_inc(s_x, 16)
                sp.wait_ge(s_cleared, 2)
                sp.dma_start(list_dst_d[P * EC:LROWS, :].rearrange("(p r) w -> p r w", p=P), away[:, :, :]).then_inc(s_x, 16)
                sp.dma_start(list_src_d.rearrange("(p b) w -> p b w", p=P)[:, 0:BLOCKS, :], list_src[:, :, :]).then_inc(s_x, 16)
                sp.wait_ge(s_x, 64)

            @block.gpsimd
            def _(pool):
                nc.gpsimd.memset(ident[:, :], 0.0).then_inc(s_pool, 1)
                nc.gpsimd.memset(before[:, :], 1.0).then_inc(s_pool, 1)
                nc.gpsimd.memset(upto[:, :], 1.0).then_inc(s_pool, 1)
                nc.gpsimd.iota(iota[:, :], [[1, P]], 0, channel_multiplier=0,
                               allow_small_or_imprecise_dtypes=True).then_inc(s_pool, 1)
                nc.gpsimd.iota(group_id[:, :], [[1, GROUPS]], 0, channel_multiplier=0,
                               allow_small_or_imprecise_dtypes=True).then_inc(s_pool, 1)
                pool.wait_ge(s_pool, 5)
                nc.gpsimd.affine_select(out=ident[:, :], in_=ident[:, :], compare_op=ALU.not_equal, fill=1.0,
                                        base=0, pattern=[[-1, P]], channel_multiplier=1).then_inc(s_const, 1)
                nc.gpsimd.affine_select(out=before[:, :], in_=before[:, :], compare_op=ALU.is_gt, fill=0.0,
                                        base=0, pattern=[[1, P]], channel_multiplier=-1).then_inc(s_const, 1)
                nc.gpsimd.affine_select(out=upto[:, :], in_=upto[:, :], compare_op=ALU.is_ge, fill=0.0,
                                        base=0, pattern=[[1, P]], channel_multiplier=-1).then_inc(s_const, 1)

            @block.vector
            def _(dve):
                last = Chain(dve, s_chain)
                for tile_, value in ((key_dst, NPAD), (key_src, NPAD), (key_next, NPAD), (weight, 0.0)):
                    last(nc.vector.memset(tile_[:, :], value))
                last.step(nc.vector.memset(x[:, NT - 1, :], 0.0))
                dve.sem_inc(s_cleared, 1)
                last(nc.vector.memset(away[:, :, :], 0.0))
                last.step(nc.vector.memset(list_src[:, :, :], 0.0))
                last(nc.vector.memset(away[:, :, 1:2], AWAY))
                last.step(nc.vector.memset(list_src[:, :, 1:2], AWAY))
                dve.sem_inc(s_cleared, 1)
                last(nc.vector.memset(ones_row[:, :], 1.0))
                last(nc.vector.memset(tile_by_dst[:, 0:LEAD], TRASH))
                last(nc.vector.memset(tile_by_src[:, 0:LEAD], TRASH))
                last(nc.vector.memset(every[:, :], 1.0))
                last(nc.vector.memset(eps[:, :], LN_EPS))
                last(nc.vector.memset(attr_sum[:, :], 0.0))
                last(nc.vector.memset(rec_dst[:, :, 3:4], 0.0))
                last(nc.vector.memset(rec_src[:, :, 3:4], 0.0))
                last(nc.vector.memset(dst_score[:, TRASH, :], 0.0))
                dve.wait_ge(s_edges, 128)
                dve.wait_ge(s_const, 3)
                tile_numbers(last, key_next, tile_next)
                tile_numbers(last, key_dst, tile_f)
                last(nc.vector.tensor_tensor(term[:, 0, :], tile_next[:, :], tile_f[:, :], ALU.is_lt))
                count_tiles(last, count_dst)
                last.step(nc.vector.reduce_sum(jumps[:, :], term[:, 0, :], AX.X))
                records(last, key_dst, key_src, rec_dst)
                records(last, key_src, key_dst, rec_src)
                dve.wait_ge(s_attr, 16)
                last.step(nc.vector.reduce_sum(attr_sum[0:125, :], attr[:, :], AX.X))
                step = exchange(dve, s_dve, s_pe)
                step()
                last(nc.vector.tensor_copy(unordered[:, :], sums[:, 0:1]))
                last(nc.vector.tensor_scalar(zero_mean[:, :], sums[:, 1:2], 1.0 / (8 * E), 0.0, ALU.mult, ALU.mult))
                tables(last, step, tile_by_dst, sums[0:NT, 2:3], sums[0:NT, 3:4], wide)
                last(nc.vector.tensor_scalar(key_by_dst[:, :], wide[0][:, 0:GROUPS], float(P), None, ALU.mult))
                last.step(nc.vector.scalar_tensor_tensor(row_f[:, :], group_id[0:1, 0:GROUPS], float(GROUP),
                                                         wide[1][0:1, 0:GROUPS], ALU.mult, ALU.add))
                last.step(nc.vector.tensor_scalar(row_by_dst[:, :], row_f[:, :], float(E), None, ALU.min))

            @block.tensor
            def _(pe):
                pe.wait_ge(s_dve, 1)
                nc.tensor.matmul(sums[:, 0:1], every[:, :], jumps[:, :], start=True, stop=True)
                nc.tensor.matmul(sums[:, 1:2], every[:, :], attr_sum[:, :], start=True, stop=True)
                nc.tensor.matmul(sums[0:NT, 2:3], count_dst[:, 0:NT], every[:, 0:1], start=True, stop=True).then_inc(s_pe, 1)
                tables_pe(pe, s_dve, s_pe, 1, sums[0:NT, 3:4], wide)

        with ExitStack() as ps, stage("s_chain", "s_staged", "s_scat0", "s_scat1", "s_seen", "s_dve", "s_pe", "s_copied") as (
                (s_chain, s_staged, s_scat0, s_scat1, s_seen, s_dve, s_pe, s_copied), block):
            s_scat = (s_scat0, s_scat1)
            sums2 = ps.enter_context(nc.psum_tensor("sums2", [P, 2, 32], F32))
            rec_stage = sb("rec_stage", [P, 2, SU, REC], F32, ps)
            pos_stage = sb("pos_stage", [P, 2, SU], U32, ps)
            pos_dst = sb("pos_dst", [P, EC], U32, ps)
            is_unordered = lambda engine: engine.value_load(unordered[0:1, 0:1], min_val=0, max_val=P * EC) != 0

            @block.sync
            def _(sp):
                with sp.If(is_unordered(sp)):
                    pass
                with sp.Else():
                    sp.dma_start(list_dst_d[0:P * EC, :].rearrange("(p c) w -> p (c w)", c=EC),
                                 rec_dst[:, :, :].rearrange("p c w -> p (c w)")).then_inc(s_copied, 16)
                    sp.wait_ge(s_copied, 16)

            @block.vector
            def _(dve):
                with dve.If(is_unordered(dve)):
                    last = Chain(dve, s_chain)
                    dve.sem_inc(s_dve, 1)
                    dve.wait_ge(s_pe, 1)
                    positions(last, sums2[:, 0, 0:NT + 1], sums2[:, 1, 0:NT + 1], pos_dst)

                    def copy(col, h):
                        nc.vector.tensor_scalar(rec_stage[:, h, :, :], rec_dst[:, bass.ds(col, SU), :], 1.0, None, ALU.mult).then_inc(s_staged, 1)
                        nc.vector.tensor_scalar(pos_stage[:, h, :], pos_dst[:, bass.ds(col, SU)], 1.0, None, ALU.mult).then_inc(s_staged, 1)
                    for h in range(2):
                        copy(h * SU, h)
                    with dve.Fori(1, SITER) as it:
                        for h in range(2):
                            dve.wait_ge(s_scat[h], it * (16 * SU))
                            copy(it * (2 * SU) + h * SU, h)

            @block.tensor
            def _(pe):
                with pe.If(is_unordered(pe)):
                    pe.wait_ge(s_dve, 1)
                    nc.tensor.matmul(sums2[:, 0, 0:NT + 1], before[:, :], count_dst[:, :], start=True, stop=True)
                    nc.tensor.matmul(sums2[:, 1, 0:NT + 1], every[:, :], count_dst[:, :], start=True, stop=True).then_inc(s_pe, 1)

            @block.gpsimd
            def _(pool):
                with pool.If(is_unordered(pool)):
                    with pool.Fori(0, SITER) as it:
                        for h in range(2):
                            pool.wait_ge(s_staged, it * 4 + 2 * h + 2)
                            pool.sem_inc(s_seen, 1)
                            for j in range(SU):
                                pool.indirect_dma_start(list_dst_d, bass.IndirectOffsetOnAxis(ap=pos_stage[:, h, j:j + 1], axis=0),
                                                        rec_stage[:, h, j, :], None).then_inc(s_scat[h], 16)
                    for h in range(2):
                        pool.wait_ge(s_scat[h], SITER * 16 * SU)

        def load_numbers(engine, table, top):
            return nc.values_load_multi_w_load_instructions(table, engines=[engine.engine], min_val=0, max_val=top)[1]

        def load_tiles(engine, tile_of_group, turn, lead):
            words = load_numbers(engine, tile_of_group[:, :].bitcast(I32)[0:1, bass.ds(
                turn * (GPI // 4) + (LEAD - lead) // 4, (GPI + lead) // 4)], (TRASH + 1) << 24)
            return [nc.s_assert_within((word >> (8 * j)) & 255, 0, TRASH,
                                       skip_runtime_bounds_check_because="it is a count of the NT tiles that a group lies beyond")
                    for word in words for j in range(4)]

        def load_by_dst(engine, first, count, s_rows):
            with engine.Fori(0, count // 4) as i:
                rows_ = load_numbers(engine, row_by_dst[0:1, bass.ds(i * 4 + first, 4)], E)
                for j, row in enumerate(rows_):
                    g = i * 4 + (first + j)
                    engine.dma_start(list_dst[:, bass.ds(g * BPG, BPG), :],
                                     list_dst_d[bass.ds(row, GROUP), :].rearrange("(p b) w -> p b w", p=P)).then_inc(s_rows, 16)

        def to_feature_major(source, s_out):
            with ExitStack() as ps, stage("s_turned", "s_copied") as ((s_turned, s_copied), block):
                turned = [ps.enter_context(nc.psum_tensor(f"turned{i}_{s_out}", [P, 4 * P], F32)) for i in range(4)]
                units = [(k, t, min(4, NT - t)) for t in range(0, NT, 4) for k in range(KC)]

                @block.tensor
                def _(pe):
                    for n, (k, t0, nt) in enumerate(units):
                        if n >= 4:
                            pe.wait_ge(s_copied, n - 3)
                        for t in range(nt):
                            last = nc.tensor.transpose(turned[n % 4][:, t * P:(t + 1) * P],
                                                       source[:, t0 + t, k * P:(k + 1) * P], ident[:, :])
                        last.then_inc(s_turned, 1)

                @block.scalar
                def _(act):
                    for n, (k, t0, nt) in enumerate(units):
                        act.wait_ge(s_turned, n + 1)
                        nc.scalar.activation(xT[:, k, t0 * P:(t0 + nt) * P], turned[n % 4][:, 0:nt * P],
                                             ACT.Copy).then_inc(s_copied, 1)

        def aggregate(tag, edges, tile_of_group, weighted):
            with ExitStack() as ps, stage("s_index", "s_seen", *GATHERED, "s_select",
                                          "s_sum", "s_added") as (
                    (s_index, s_seen, *s_gath, s_select, s_sum, s_added), block):
                total = [ps.enter_context(nc.psum_tensor(f"total{i}_{tag}", [P, 512], F32)) for i in range(GPI)]

                @block.scalar
                def _(act):
                    with act.Fori(0, ITER) as it:
                        for r in range(RING):
                            act.wait_ge(s_sum, it * GPI + (r + 1) * GPC)
                            nc.scalar.activation(slot_node[:, r, 0:BPC], edges[:, bass.ds(it * BPI + r * BPC, BPC), 0],
                                                 ACT.Copy).then_inc(s_index, 1)

                @block.gpsimd
                def _(pool):
                    with pool.Fori(0, ITER) as it:
                        for r in range(RING):
                            pool.wait_ge(s_index, it * RING + (r + 1))
                            pool.sem_inc(s_seen, 1)
                            for j in range(BPC):
                                pool.indirect_dma_start(gathered[:, r, j, 0:D], None, node_d,
                                                        bass.IndirectOffsetOnAxis(ap=slot_node[:, r, j:j + 1], axis=0)
                                                        ).then_inc(s_gath[r], 16)

                @block.tensor
                def _(pe):
                    pe.sem_inc(s_sum, GPI)
                    with pe.Fori(0, ITER) as it:
                        for r in range(RING):
                            pe.wait_ge(s_gath[r], it * (16 * BPC) + 16 * BPC)
                            pe.wait_ge(s_select, it * BPI + (r + 1) * BPC)
                            for g in range(r * GPC, (r + 1) * GPC):
                                pe.wait_ge(s_added, it * GPI + (g + 1))
                                for b in range(BPG):
                                    j = (g - r * GPC) * BPG + b
                                    last = nc.tensor.matmul(total[g][:, 0:D], select[:, r, j, :], gathered[:, r, j, 0:D],
                                                            start=b == 0, stop=b == BPG - 1)
                                last.then_inc(s_sum, 1)

                @block.vector
                def _(dve):
                    def one_hots(it, r):
                        dve.wait_ge(s_sum, it * GPI + (r + 1) * GPC)
                        for j in range(BPC):
                            at = edges[:, bass.ds(it * BPI + (r * BPC + j), 1), :]
                            if weighted:
                                one = nc.vector.tensor_scalar(select[:, r, j, :], iota[:, :], at[:, 0, 1:2], at[:, 0, 2:3],
                                                              ALU.is_equal, ALU.mult)
                            else:
                                one = nc.vector.tensor_scalar(select[:, r, j, :], iota[:, :], at[:, 0, 1:2], None, ALU.is_equal)
                            one.then_inc(s_select, 1)

                    def add(it, r, tiles):
                        for g in range(r * GPC, (r + 1) * GPC):
                            group = it * GPI + g
                            t = tiles[g]
                            dve.wait_ge(s_sum, group + (GPI + 1))
                            dve.wait_ge(s_added, group + GPI)
                            nc.vector.tensor_tensor(acc[:, bass.ds(t, 1), 0:D], total[g][:, 0:D],
                                                    acc[:, bass.ds(t, 1), 0:D], ALU.add).then_inc(s_added, 1)

                    dve.sem_inc(s_added, GPI)
                    with dve.Fori(0, ITER) as it:
                        tiles = load_tiles(dve, tile_of_group, it, 0)
                        for r in range(RING):
                            one_hots(it, r)
                            if r:
                                add(it, r - 1, tiles)
                        add(it, RING - 1, tiles)

        first_table(nc, A, stage, locals())
        pre.close()
        gathered = sb("gathered", [P, RING, BPC, ZW])
        select = sb("select", [P, RING, BPC, P])
        slot_node = sb("slot_node", [P, RING, BPC], U32)
        attention(nc, A, stage, locals())
        def load_w(w):
            return [(w_sb[:, k, 0:D], w[k * P:(k + 1) * P, :]) for k in range(KC)]

        def vector(name):
            return [(brow[:, :], A[name].rearrange("(a n) -> a n", a=1).broadcast_to([P, D]))]

        def h0_rows(t, prod):
            return nc.vector.tensor_tensor(acc[:, t, 0:D], prod, brow[:, :], ALU.add)

        def rows3(t, prod):
            return nc.vector.tensor_copy(big[:, t, 0:D], prod)

        def rows4(t, prod):
            return nc.vector.tensor_scalar(acc[:, t, 0:D], prod, dinv[:, t:t + 1], None, ALU.mult)

        norm_and_project(nc, A, stage, locals(), "h0", "attention", load_w(A["L1_gnn_W_in"]) + vector("L1_gnn_b_in"), h0_rows, acc)
        for l in range(LAYERS):
            aggregate(f"l{l}", list_src, tile_by_src, True)
            to_feature_major(acc, f"pool{l}")
            layer_mlp(nc, A, stage, locals())
        norm_and_project(nc, A, stage, locals(), "x3", "sum", load_w(A["L2_gnn_W"]), rows3, big)
        aggregate("g3", list_dst, tile_by_dst, True)
        norm_and_project(nc, A, stage, locals(), "x4", "unit", load_w(A["L3_gnn_W"]) + vector("L2_gnn_b"), rows4, acc)
        aggregate("g4", list_dst, tile_by_dst, False)
        norm_and_project(nc, A, stage, locals(), "n4", "tanh", vector("L3_gnn_b"), None, None)


def norm_and_project(nc, A, stage, v, tag, how, loads, finish, rows_sb):
    x, xT, acc, brow, dinv, rstd, meanvar, eps, big, ident, w_sb, stats, shift, rden = (
        v[n] for n in ("x", "xT", "acc", "brow", "dinv", "rstd", "meanvar", "eps", "big", "ident", "w_sb", "stats", "shift", "rden"))
    sets = NT // SET
    with ExitStack() as ps, stage("s_load", "s_chain", "s_root", "s_rooted", "s_pre", "s_act", "s_norm2", "s_norm", "s_var", "s_std",
                                  "s_coef", "s_x", "s_turned", "s_copied", "s_prod", "s_fin", "s_stored", "s_clear", "s_rows") as (
            (s_load, s_chain, s_root, s_rooted, s_pre, s_act, s_norm2, s_norm, s_var, s_std,
             s_coef, s_x, s_turned, s_copied, s_prod, s_fin, s_stored, s_clear, s_rows), block):
        turned = [ps.enter_context(nc.psum_tensor(f"turned{i}_{tag}", [P, D], F32)) for i in range(3)]
        prod = [ps.enter_context(nc.psum_tensor(f"prod{i}_{tag}", [P, D], F32)) for i in range(4)]
        span = lambda i: range(i * SET, (i + 1) * SET)
        tiles = lambda i: slice(i * SET, (i + 1) * SET)

        @block.sync
        def _(sp):
            for to, of in loads:
                sp.dma_start(to, of).then_inc(s_load, 16)
            if how == "attention":
                sp.dma_start(v["list_src"][:, :, :], v["list_src_d"].rearrange("(p b) w -> p b w", p=P)[:, 0:BLOCKS, :]).then_inc(s_rows, 16)
                sp.wait_ge(s_rows, 16)
            for i in range(sets):
                if finish:
                    sp.wait_ge(s_fin, (i + 1) * SET)
                    sp.dma_start(v["rows"](v["node_d"])[:, tiles(i), :], rows_sb[:, tiles(i), 0:D]).then_inc(s_stored, 16)
                else:
                    sp.wait_ge(s_x, (i + 1) * SET)
                    whole = SET - (i == sets - 1)
                    t0 = i * SET
                    sp.dma_start(A["out"][t0 * P:(t0 + whole) * P, :].rearrange("(t p) f -> p t f", p=P),
                                 x[:, t0:t0 + whole, :]).then_inc(s_stored, 16)
            if not finish:
                sp.dma_start(A["out"][(NT - 1) * P:N, :], x[0:LAST, NT - 1, :]).then_inc(s_stored, 16)
            sp.wait_ge(s_stored, 16 * (sets + (not finish)))

        @block.gpsimd
        def _(pool):
            if how == "sum":
                for i in range(sets):
                    pool.wait_ge(s_var, i + 1)
                    nc.gpsimd.memset(acc[:, tiles(i), :], 0.0).then_inc(s_clear, 1)
                pool.wait_ge(s_clear, sets)

        @block.scalar
        def _(act):
            def elementwise(i):
                act.wait_ge(s_pre, i + 1)
                for t in span(i):
                    if how == "tanh":
                        nc.scalar.activation(acc[:, t, 0:D], acc[:, t, 0:D], ACT.Tanh).then_inc(s_act, 1)
                    else:
                        nc.scalar.activation(acc[:, t, 0:D], acc[:, t, 0:D], ACT.Relu).then_inc(s_act, 1)
                if how == "unit":
                    act.wait_ge(s_act, (i + 1) * SET)
                    for t in span(i):
                        nc.scalar.activation(big[:, t, 0:D], acc[:, t, 0:D], ACT.Square,
                                             accum_out=rden[:, t, 0:1]).then_inc(s_norm2, 1)

            if how == "attention":
                act.wait_ge(s_root, 1)
                nc.scalar.activation(dinv[:, :], dinv[:, :], ACT.Sqrt).then_inc(s_rooted, 1)
            if how == "tanh":
                for i in range(sets):
                    elementwise(i)
            if how == "unit":
                elementwise(0)
            for i in range(sets):
                if how == "unit":
                    act.wait_ge(s_norm, i + 1)
                    nc.scalar.activation(rden[:, tiles(i), 1], rden[:, tiles(i), 1], ACT.Sqrt).then_inc(s_rooted, 1)
                    if i < sets - 1:
                        elementwise(i + 1)
                act.wait_ge(s_var, i + 1)
                nc.scalar.activation(rstd[:, tiles(i)], meanvar[:, tiles(i), 1], ACT.Sqrt, bias=eps[:, 0:1]).then_inc(s_std, 1)
                act.wait_ge(s_coef, i + 1)
                for t in span(i):
                    nc.scalar.activation(x[:, t, :], x[:, t, :], ACT.Identity, scale=rstd[:, t:t + 1],
                                         bias=shift[:, t:t + 1]).then_inc(s_x, 1)
                if finish:
                    for t in span(i):
                        act.wait_ge(s_turned, t + 1)
                        nc.scalar.activation(xT[:, :, t * P:(t + 1) * P], turned[t % 3][:, :].rearrange("p (k n) -> p k n", k=KC),
                                             ACT.Copy).then_inc(s_copied, 1)

        @block.tensor
        def _(pe):
            if finish:
                pe.wait_ge(s_load, 16 * len(loads))
                for i in range(sets):
                    for t in span(i):
                        pe.wait_ge(s_x, t + 1)
                        if t >= 3:
                            pe.wait_ge(s_copied, t - 2)
                        for k in range(KC):
                            last = nc.tensor.transpose(turned[t % 3][:, k * P:(k + 1) * P], x[:, t, k * P:(k + 1) * P], ident[:, :])
                        last.then_inc(s_turned, 1)
                    for t in span(i):
                        pe.wait_ge(s_copied, t + 1)
                        if t >= 4:
                            pe.wait_ge(s_fin, t - 3)
                        for k in range(KC):
                            last = nc.tensor.matmul(prod[t % 4][:, :], xT[:, k, t * P:(t + 1) * P], w_sb[:, k, 0:D],
                                                    start=k == 0, stop=k == KC - 1)
                        last.then_inc(s_prod, 1)

        @block.vector
        def _(dve):
            last = Chain(dve, s_chain)
            some = lambda ap: ap.rearrange("p (t f) -> p t f", t=1).broadcast_to([P, SET, D])

            def prepare(i):
                if how == "unit":
                    last.step(nc.vector.tensor_tensor(acc[:, tiles(i), 0:D], acc[:, tiles(i), 0:D], some(brow[:, :]), ALU.add))
                if how == "tanh":
                    for t in span(i):
                        last(nc.vector.scalar_tensor_tensor(acc[:, t, 0:D], acc[:, t, 0:D], dinv[:, t:t + 1], brow[:, :],
                                                            ALU.mult, ALU.add))
                    last.wait()
                dve.sem_inc(s_pre, 1)

            def update(i):
                if how == "attention":
                    for q in range(H):
                        at = acc[:, tiles(i), q * HW:q * HW + OUT]
                        last(nc.vector.tensor_tensor(at, at, rden[:, tiles(i), q:q + 1].broadcast_to([P, SET, OUT]), ALU.mult))
                    last.wait()
                    for q in range(H):
                        to = x[:, tiles(i), q * OUT:(q + 1) * OUT]
                        last(nc.vector.tensor_tensor(to, to, acc[:, tiles(i), q * HW:q * HW + OUT], ALU.add))
                if how == "sum":
                    last(nc.vector.tensor_tensor(x[:, tiles(i), :], x[:, tiles(i), :], acc[:, tiles(i), 0:D], ALU.add))
                if how == "unit":
                    dve.wait_ge(s_norm2, (i + 1) * SET)
                    last.step(nc.vector.tensor_scalar(rden[:, tiles(i), 1], rden[:, tiles(i), 0], NORM_EPS * NORM_EPS, None, ALU.max))
                    dve.sem_inc(s_norm, 1)
                    dve.wait_ge(s_rooted, i + 1)
                    last.step(nc.vector.reciprocal(rden[:, tiles(i), 2], rden[:, tiles(i), 1]))
                    for t in span(i):
                        last(nc.vector.scalar_tensor_tensor(x[:, t, :], acc[:, t, 0:D], rden[:, t, 2:3], x[:, t, :],
                                                            ALU.mult, ALU.add))
                if how == "tanh":
                    dve.wait_ge(s_act, (i + 1) * SET)
                    last(nc.vector.scalar_tensor_tensor(x[:, tiles(i), :], acc[:, tiles(i), 0:D], v["zero_mean"][:, 0:1],
                                                        x[:, tiles(i), :], ALU.add, ALU.add))
                last.wait()
                for t in span(i):
                    last(nc.vector.bn_stats(stats[:, t, :], x[:, t, :]))
                last.wait()
                for t in span(i):
                    last(nc.vector.bn_aggr(meanvar[:, t, :], stats[:, t, :]))
                last.wait()
                dve.sem_inc(s_var, 1)

            def coefficients(i):
                dve.wait_ge(s_std, i + 1)
                last.step(nc.vector.reciprocal(rstd[:, tiles(i)], rstd[:, tiles(i)]))
                last.step(nc.vector.scalar_tensor_tensor(shift[:, tiles(i)], meanvar[:, tiles(i), 0], -1.0, rstd[:, tiles(i)],
                                                         ALU.mult, ALU.mult))
                dve.sem_inc(s_coef, 1)

            def products(i):
                if finish:
                    for t in span(i):
                        dve.wait_ge(s_prod, t + 1)
                        finish(t, prod[t % 4][:, :]).then_inc(s_fin, 1)

            if how == "attention":
                last.step(nc.vector.tensor_scalar(dinv[:, :], acc[:, 0:NT, HZ], 1.0, None, ALU.add))
                dve.sem_inc(s_root, 1)
                sums = acc[:, 0:NT, 0:HZ].rearrange("p t (q o) -> p t q o", q=H)
                last.step(nc.vector.tensor_scalar(rden[:, :, :], sums[:, :, :, OUT], DEN_EPS, None, ALU.max))
                last.step(nc.vector.reciprocal(rden[:, :, :], rden[:, :, :]))
                dve.wait_ge(s_rooted, 1)
                last.step(nc.vector.reciprocal(dinv[:, :], dinv[:, :]))
            dve.wait_ge(s_load, 16 * len(loads))
            if how == "tanh":
                for i in range(sets):
                    prepare(i)
            if how == "unit":
                prepare(0)
            for i in range(sets):
                if how == "unit" and i < sets - 1:
                    prepare(i + 1)
                update(i)
                coefficients(i)
                if i:
                    products(i - 1)
            products(sets - 1)


def layer_mlp(nc, A, stage, v):
    l, xT, hT, acc, column, ident, sb, rows, node_d = (
        v[n] for n in ("l", "xT", "hT", "acc", "column", "ident", "sb", "rows", "node_d"))
    w = (v["w_sb"], v["w2_sb"])
    with ExitStack() as own:
        bstats = sb(f"bstats{l}", [P, KC, len(CHUNKS), 6], F32, own)
        bmv = sb(f"bmv{l}", [P, KC, 2], F32, own)
        scale = sb(f"bscale{l}", [P, KC], F32, own)
        shift = sb(f"bshift{l}", [P, KC], F32, own)
        weights = [A["L1_gnn_W1"], A["L1_gnn_W2"]]
        vectors = ["L1_gnn_b1", "L1_gnn_g1", "L1_gnn_be1", "L1_gnn_b2", "L1_gnn_g_out", "L1_gnn_b_out"]
        for m, (src, dst) in enumerate(((xT, hT), (hT, xT))):
            with ExitStack() as ps, stage("s_w", "s_prod", "s_out", "s_stat", "s_std", "s_chain", "s_coef", "s_vec") as (
                    (s_w, s_prod, s_out, s_stat, s_std, s_chain, s_coef, s_vec), block):
                prod = [ps.enter_context(nc.psum_tensor(f"mlp{l}{m}{i}", [P, NCOL], F32)) for i in range(4)]
                units = [(c, n, f) for c, n in CHUNKS for f in range(KC)]

                @block.sync
                def _(sp):
                    for k in range(KC):
                        sp.dma_start(w[m][:, k, 0:D], weights[m][l, k * P:(k + 1) * P, :]).then_inc(s_w, 16)
                    for i in range(3):
                        for k in range(KC):
                            sp.dma_start(column[:, 3 * m + i, k:k + 1],
                                         A[vectors[3 * m + i]][l, k * P:(k + 1) * P].rearrange("(p a) -> p a", a=1)).then_inc(s_vec, 16)

                @block.tensor
                def _(pe):
                    pe.wait_ge(s_w, 16 * KC)
                    for u, (c, n, f) in enumerate(units):
                        if u >= 4:
                            pe.wait_ge(s_out, u - 3)
                        for k in range(KC):
                            last = nc.tensor.matmul(prod[u % 4][:, 0:n], w[m][:, k, f * P:(f + 1) * P], src[:, k, c:c + n],
                                                    start=k == 0, stop=k == KC - 1)
                        last.then_inc(s_prod, 1)

                @block.scalar
                def _(act):
                    act.wait_ge(s_vec, 16 * 3 * KC)
                    for u, (c, n, f) in enumerate(units):
                        act.wait_ge(s_prod, u + 1)
                        nc.scalar.activation(dst[:, f, c:c + n], prod[u % 4][:, 0:n], ACT.Identity,
                                             bias=column[:, 3 * m, f:f + 1]).then_inc(s_out, 1)
                    act.wait_ge(s_stat, 1)
                    nc.scalar.activation(scale[:, :], bmv[:, :, 1], ACT.Sqrt, bias=v["eps"][:, 0:1]).then_inc(s_std, 1)
                    act.wait_ge(s_coef, 1)
                    for f in range(KC):
                        nc.scalar.activation(dst[:, f, :], dst[:, f, :], ACT.Relu, bias=shift[:, f:f + 1], scale=scale[:, f:f + 1])

                @block.vector
                def _(dve):
                    last = Chain(dve, s_chain)
                    dve.wait_ge(s_vec, 16 * 3 * KC)
                    for u, (c, n, f) in enumerate(units):
                        dve.wait_ge(s_out, u + 1)
                        n = min(n, N - c)
                        last(nc.vector.bn_stats(bstats[:, f, c // NCOL, :], dst[:, f, c:c + n]))
                    last.wait()
                    for f in range(KC):
                        last(nc.vector.bn_aggr(bmv[:, f, :], bstats[:, f, :, :]))
                    last.wait()
                    dve.sem_inc(s_stat, 1)
                    dve.wait_ge(s_std, 1)
                    last.step(nc.vector.reciprocal(scale[:, :], scale[:, :]))
                    last.step(nc.vector.tensor_tensor(scale[:, :], scale[:, :], column[:, 3 * m + 1, :], ALU.mult))
                    last.step(nc.vector.tensor_tensor(shift[:, :], bmv[:, :, 0], scale[:, :], ALU.mult))
                    last.step(nc.vector.tensor_tensor(shift[:, :], column[:, 3 * m + 2, :], shift[:, :], ALU.subtract))
                    dve.sem_inc(s_coef, 1)

        with ExitStack() as ps, stage("s_turned", "s_copied", "s_stored") as ((s_turned, s_copied, s_stored), block):
            turned = [ps.enter_context(nc.psum_tensor(f"back{l}{i}", [P, 2, D], F32)) for i in range(4)]
            units = [(t, min(2, NT - t)) for t in range(0, NT, 2)]

            @block.tensor
            def _(pe):
                for n, (t0, nt) in enumerate(units):
                    if n >= 4:
                        pe.wait_ge(s_copied, n - 3)
                    for t in range(nt):
                        for k in range(KC):
                            last = nc.tensor.transpose(turned[n % 4][:, t, k * P:(k + 1) * P],
                                                       xT[:, k, (t0 + t) * P:(t0 + t + 1) * P], ident[:, :])
                    last.then_inc(s_turned, 1)

            @block.scalar
            def _(act):
                for n, (t0, nt) in enumerate(units):
                    act.wait_ge(s_turned, n + 1)
                    nc.scalar.activation(acc[:, t0:t0 + nt, 0:D], turned[n % 4][:, 0:nt, :], ACT.Copy).then_inc(s_copied, 1)

            @block.sync
            def _(sp):
                if l < LAYERS - 1:
                    for t0 in range(0, NT, 5):
                        sp.wait_ge(s_copied, (t0 + 5 + 1) // 2)
                        sp.dma_start(rows(node_d)[:, t0:t0 + 5, :], acc[:, t0:t0 + 5, 0:D]).then_inc(s_stored, 16)
                    sp.wait_ge(s_stored, 16 * (NT // 5))


def first_table(nc, A, stage, v):
    sb, rows, z_d, xT, big, acc, w_sb, w2_sb, dst_score, pos_src = (
        v[n] for n in ("sb", "rows", "z_d", "xT", "big", "acc", "w_sb", "w2_sb", "dst_score", "pos_src"))
    with ExitStack() as ps, ExitStack() as small, stage(
            "s_zero", "s_load", "s_prod", "s_weights", "s_row", "s_pool_rows", "s_stored", "s_rows", "s_chain", "s_dve",
            "s_pe", "s_parts") as (
            (s_zero, s_load, s_prod, s_weights, s_row, s_pool_rows, s_stored, s_rows, s_chain, s_dve, s_pe, s_parts), block):
        a_diag = sb("a_diag", [P, KC, 2 * H], F32, small)
        rest = sb("rest", [P, NT, H], F32, small)
        score_w = ps.enter_context(nc.psum_tensor("score_w", [P, KC, 2 * H], F32))
        prod = [ps.enter_context(nc.psum_tensor(f"z_prod{i}", [P, 512], F32)) for i in range(3)]
        sums = ps.enter_context(nc.psum_tensor("sums3", [P, 2, 32], F32))
        totals = ps.enter_context(nc.psum_tensor("totals", [P, 8], F32))
        wide = [ps.enter_context(nc.psum_tensor(f"wide_b{i}", [P, 512], F32)) for i in range(2)]
        heads = w_sb[:, :, 0:HZ].rearrange("p k (h o) -> p k h o", h=H)
        parts = big[:, :, AW:ZW].bitcast(BF16)
        scores = big[:, :, 0:HZ].rearrange("p t (h o) -> p t h o", h=H)[:, :, :, OUT]

        @block.sync
        def _(sp):
            sp.wait_ge(s_zero, 3)
            for k in range(KC):
                sp.dma_start(w2_sb[:, k, :], A["W_rows"][k * P:(k + 1) * P, :]).then_inc(s_load, 16)
            for h in range(H):
                at = (h * OUT) % P
                for side in range(2):
                    c = side * H + h
                    sp.dma_start(a_diag[at:at + OUT, h * OUT // P, c:c + 1],
                                 A["L0_gnn_attn"][0, side * OUT:(side + 1) * OUT].rearrange("(p a) -> p a", a=1)).then_inc(s_load, 16)
            for k in range(KC):
                sp.dma_start(xT[:, k, 0:N], A["xT"][k * P:(k + 1) * P, :]).then_inc(s_load, 16)
                sp.dma_start(heads[:, k, :, 0:OUT],
                             A["W_cols"][k * P:(k + 1) * P, :].rearrange("p (h o) -> p h o", h=H)).then_inc(s_load, 16)
            v["load_by_dst"](sp, 0, BY_SP, s_rows)

        @block.gpsimd
        def _(pool):
            nc.gpsimd.memset(a_diag[:, :, :], 0.0).then_inc(s_zero, 1)
            nc.gpsimd.memset(xT[:, :, N:NPAD], 0.0).then_inc(s_zero, 1)
            nc.gpsimd.memset(big[:, :, HZ:AW], 1.0).then_inc(s_zero, 1)
            nc.gpsimd.memset(acc[:, :, :], 0.0).then_inc(s_zero, 1)
            pool.wait_ge(s_zero, 4)
            v["load_by_dst"](pool, BY_SP + BY_ACT, GROUPS - BY_SP - BY_ACT, s_pool_rows)
            pool.wait_ge(s_parts, 1)
            for t0 in range(0, NT, 5):
                pool.dma_start(rows(z_d)[:, t0:t0 + 5, :], big[:, t0:t0 + 5, :]).then_inc(s_stored, 16)
            pool.wait_ge(s_stored, 16 * (NT // 5))

        @block.tensor
        def _(pe):
            pe.wait_ge(s_load, 16 * (3 * KC + 2 * H))
            for m in range(KC):
                for k in range(KC):
                    last = nc.tensor.matmul(score_w[:, m, :], w2_sb[:, k, m * P:(m + 1) * P], a_diag[:, k, :],
                                            start=k == 0, stop=k == KC - 1)
            last.then_inc(s_prod, 1)
            pe.wait_ge(s_dve, 1)
            nc.tensor.matmul(sums[:, 0, 0:NT + 1], v["before"][:, :], v["count_src"][:, :], start=True, stop=True)
            nc.tensor.matmul(sums[:, 1, 0:NT + 1], v["every"][:, :], v["count_src"][:, :], start=True, stop=True)
            nc.tensor.matmul(totals[0:NT, 0:1], v["count_src"][:, 0:NT], v["every"][:, 0:1], start=True, stop=True).then_inc(s_pe, 1)
            pe.wait_ge(s_weights, 1)
            for t in range(NT):
                if t >= 3:
                    pe.wait_ge(s_row, t - 2)
                for k in range(KC):
                    last = nc.tensor.matmul(prod[t % 3][:, 0:HZ + H], xT[:, k, t * P:(t + 1) * P], w_sb[:, k, :],
                                            start=k == 0, stop=k == KC - 1)
                last.then_inc(s_prod, 1)
            v["tables_pe"](pe, s_dve, s_pe, 1, totals[0:NT, 1:2], wide)

        @block.scalar
        def _(act):
            act.wait_ge(s_prod, 1)
            nc.scalar.activation(heads[:, :, :, OUT], score_w[:, :, 0:H], ACT.Copy)
            nc.scalar.activation(w_sb[:, :, HZ:HZ + H], score_w[:, :, H:2 * H], ACT.Copy).then_inc(s_weights, 1)
            for t in range(NT):
                act.wait_ge(s_prod, t + 2)
                nc.scalar.activation(dst_score[:, t, :], prod[t % 3][:, HZ:HZ + H], ACT.Copy)
                nc.scalar.activation(big[:, t, 0:HZ], prod[t % 3][:, 0:HZ], ACT.Copy).then_inc(s_row, 1)
            v["load_by_dst"](act, BY_SP, BY_ACT, s_rows)

        @block.vector
        def _(dve):
            last = Chain(dve, s_chain)
            v["tile_numbers"](last, v["key_src"], v["tile_f"])
            last(nc.vector.scalar_tensor_tensor(v["rec_src"][:, :, 1], v["tile_f"][:, :], -float(P), v["rec_src"][:, :, 1],
                                                ALU.mult, ALU.add))
            v["count_tiles"](last, v["count_src"])
            step = v["exchange"](dve, s_dve, s_pe)
            step()
            sizes, sizes_i = v["sizes"], v["sizes_i"]
            last.step(nc.vector.tensor_scalar(sizes_i[:, :], sums[:, 1, 0:NT + 1], float(GROUP - 1), None, ALU.add))
            last.step(nc.vector.tensor_scalar(sizes_i[:, :], sizes_i[:, :], SHIFT, None, ALU.logical_shift_right))
            last.step(nc.vector.tensor_scalar(sizes[:, :], sizes_i[:, :], float(GROUP), None, ALU.mult))
            slot, slot_p, slot_b = v["slot"], v["slot_p"], v["slot_b"]
            v["positions"](last, sums[:, 0, 0:NT + 1], sizes[:, :], slot)
            last(nc.vector.tensor_scalar(slot_p[:, :], slot[:, :], P - 1, None, ALU.bitwise_and))
            last.step(nc.vector.tensor_scalar(slot_b[:, :], slot[:, :], P.bit_length() - 1, None, ALU.logical_shift_right))
            last.step(nc.vector.scalar_tensor_tensor(pos_src[:, :], slot_p[:, :], float(BLOCKS + SPARE), slot_b[:, :],
                                                     ALU.mult, ALU.add))
            dve.wait_ge(s_row, NT)
            first = scores
            for i in range(PARTS):
                to = parts[:, :, i * H:(i + 1) * H]
                last.step(nc.vector.tensor_copy(to, first))
                if i < PARTS - 1:
                    last.step(nc.vector.tensor_tensor(rest[:, :, :], first, to, ALU.subtract))
                    first = rest[:, :, :]
            dve.sem_inc(s_parts, 1)
            v["tables"](last, step, v["tile_by_src"], totals[0:NT, 0:1], totals[0:NT, 1:2], wide)
            dve.wait_ge(s_rows, 16 * (BY_SP + BY_ACT))
            dve.wait_ge(s_pool_rows, 16 * (GROUPS - BY_SP - BY_ACT))
            at = v["list_dst"][:, :, 1].rearrange("p (g b) -> p g b", b=BPG)
            last.step(nc.vector.tensor_tensor(at, at, v["key_by_dst"][:, :].rearrange("p (g b) -> p g b", b=1).broadcast_to(
                [P, GROUPS, BPG]), ALU.subtract))


def attention(nc, A, stage, v):
    sb, z_d, x, acc, ident, iota, gathered, select, slot_node, dst_score = (
        v[n] for n in ("sb", "z_d", "x", "acc", "ident", "iota", "gathered",
                       "select", "slot_node", "dst_score"))
    edges, dinv, rec_src, pos_src = v["list_dst"], v["dinv"], v["rec_src"], v["pos_src"]
    tile_of_group = v["tile_by_dst"]
    with ExitStack() as own:
        node_state = sb("node_state", [P, NT + 1, 2 * H], F32, own)
        raise_to = sb("raise_to", [P, 2 * H], F32, own)
        pick = sb("pick", [P, H, P], BF16, own)
        ident4 = sb("ident4", [P, H, P], BF16, own)
        ident_b = sb("ident_b", [P, P], BF16, own)
        pick_col = sb("pick_col", [P, H], F32, own)
        miss = sb("miss", [P, 4, GROUP], BF16, own)
        select_t = sb("select_t", [P, 2, GROUP], F32, own)
        one = sb("one", [P, 1], F32, own)
        neg = sb("neg", [P, 1], F32, own)
        score_t = sb("score_t", [P, 2, GROUP], BF16, own)
        block_top = sb("block_top", [P, H], F32, own)
        node_side = sb("node_side", [P, 2 * H], F32, own)
        raised = sb("raised", [P, H], F32, own)
        keep = sb("keep", [P, 4, H], F32, own)
        logit = sb("logit", [P, 2, BPG, H], F32, own)
        logit2 = sb("logit2", [P, BPG, H], F32, own)
        rec_stage = sb("rec_stage_src", [P, 2, SB, REC], F32, own)
        pos_stage = sb("pos_stage_src", [P, 2, SB], U32, own)

        with stage("s_init") as ((s_init,), block):
            @block.vector
            def _(dve):
                last = Chain(dve, s_init)
                nc.vector.tensor_copy(node_state[:, :, 0:H], dst_score[:, :, :])
                nc.vector.memset(node_state[:, :, H:2 * H], NEG * SLOPE)
                nc.vector.memset(raise_to[:, :], NEG)
                nc.vector.memset(score_t[:, :, :], 0.0)
                nc.vector.memset(one[:, :], 1.0)
                nc.vector.memset(neg[:, :], NEG)
                nc.vector.tensor_copy(ident_b[:, :], ident[:, :])
                nc.vector.tensor_copy(ident4[:, :, :], ident[:, :].rearrange("p (a m) -> p a m", a=1).broadcast_to([P, H, P]))
                last.step(nc.vector.tensor_tensor(pick_col[:, :], ident[:, 0:H], ident[:, H:2 * H], ALU.add))
                last.step(nc.vector.tensor_tensor(pick_col[:, :], pick_col[:, :], ident[:, 2 * H:3 * H], ALU.add))
                last.step(nc.vector.tensor_copy(pick[:, :, :], pick_col[:, :].rearrange("p (h m) -> p h m", m=1).broadcast_to([P, H, P])))

        names = ("s_index", "s_seen", *GATHERED, "s_hot", "s_miss", "s_turned", "s_score_t",
                 "s_miss_t", "s_masked_t", "s_chain", "s_top", "s_nodes", "s_keep", "s_select_t", "s_side", "s_logit", "s_exp", "s_row",
                 "s_sum", "s_scaled", "s_added", "s_stage0", "s_stage1", "s_scat0", "s_scat1")
        with ExitStack() as ps, stage(*names) as (
                (s_index, s_seen, *s_gath, s_hot, s_miss, s_turned, s_score_t,
                 s_miss_t, s_masked_t, s_chain, s_top, s_nodes, s_keep, s_select_t, s_side, s_logit, s_exp, s_row,
                 s_sum, s_scaled, s_added, s_stage0, s_stage1, s_scat0, s_scat1), block):
            s_stage, s_scat = (s_stage0, s_stage1), (s_scat0, s_scat1)
            masked_t = ps.enter_context(nc.psum_tensor("masked_t", [P, BPG, H, P], F32))
            miss_t = ps.enter_context(nc.psum_tensor("miss_t", [P, 2 * 512], BF16))
            turned = ps.enter_context(nc.psum_tensor("turned", [P, 2 * 512], BF16))
            side = [ps.enter_context(nc.psum_tensor(f"side{i}", [P, BPG, 2 * H], F32)) for i in range(2)]
            total = [ps.enter_context(nc.psum_tensor(f"total{i}", [P, 512], F32)) for i in range(2)]

            def wait(engine, sem, value):
                if not isinstance(value, int) or value > 0:
                    engine.wait_ge(sem, value)

            def place_of(g):
                g = g % GPI
                return g // GPC, (g % GPC) * BPG

            def turns(engine, body):
                body(0, first=True, last=False)
                with engine.Fori(1, ITER - 1) as it:
                    body(it, first=False, last=False)
                body(ITER - 1, first=False, last=True)

            @block.sync
            def _(sp):
                def load(i, h):
                    col = i * (2 * SB) + h * SB
                    sp.dma_start(rec_stage[:, h, :, :], rec_src[:, bass.ds(col, SB), :]).then_inc(s_stage[h], 16)
                    sp.dma_start(pos_stage[:, h, :], pos_src[:, bass.ds(col, SB)]).then_inc(s_stage[h], 16)

                for h in range(2):
                    load(0, h)
                with sp.Fori(1, SPAIRS) as i:
                    for h in range(2):
                        sp.wait_ge(s_scat[h], i * (16 * SB))
                        load(i, h)

            @block.gpsimd
            def _(pool):
                def turn(it, h, pair):
                    for r in range(RING):
                        pool.wait_ge(s_index, it * RING + (r + 1))
                        pool.sem_inc(s_seen, 1)
                        for j in range(BPC):
                            pool.indirect_dma_start(gathered[:, r, j, 0:ZW], None, z_d,
                                                    bass.IndirectOffsetOnAxis(ap=slot_node[:, r, j:j + 1], axis=0)
                                                    ).then_inc(s_gath[r], 16)
                        if pair is not None:
                            if r == 0:
                                pool.wait_ge(s_stage[h], pair * 32 + 32)
                                pool.sem_inc(s_seen, 1)
                            for j in range(r * SG, (r + 1) * SG):
                                pool.indirect_dma_start(
                                    v["list_src_d"], bass.IndirectOffsetOnAxis(ap=pos_stage[:, h, j:j + 1], axis=0),
                                    rec_stage[:, h, j, :], None).then_inc(s_scat[h], 16)

                turn(0, 0, None)
                with pool.Fori(0, SPAIRS) as pair:
                    for h in range(2):
                        turn(pair * 2 + (h + 1), h, pair)
                for it in range(2 * SPAIRS + 1, ITER):
                    turn(it, 0, None)
                for h in range(2):
                    pool.wait_ge(s_scat[h], 16 * SB * SPAIRS)

            @block.scalar
            def _(act):
                def index(it, r):
                    nc.scalar.activation(slot_node[:, r, :], edges[:, bass.ds(it * BPI + r * BPC, BPC), 0],
                                         ACT.Copy).then_inc(s_index, 1)

                def copy_scores(it, g):
                    n = it * GPI + g
                    act.wait_ge(s_turned, n + 1)
                    wait(act, s_masked_t, n - 1)
                    nc.scalar.activation(score_t[0:PARTS * H, g % 2, :], turned[0:PARTS * H, 0:GROUP], ACT.Copy).then_inc(s_score_t, 1)

                def make_miss(it, g):
                    n = it * GPI + g
                    r, b0 = place_of(g)
                    act.wait_ge(s_hot, n + 1)
                    wait(act, s_masked_t, n - 3)
                    nc.scalar.activation(miss[:, g % 4, :].rearrange("p (b m) -> p b m", m=P), select[:, r, b0:b0 + BPG, :], ACT.Identity,
                                         scale=-NEG, bias=neg[:, 0:1]).then_inc(s_miss, 1)

                def copy_miss(it, g):
                    n = it * GPI + g
                    act.wait_ge(s_miss_t, n + 1)
                    wait(act, s_side, n - 1)
                    nc.scalar.activation(select_t[:, g % 2, :], miss_t[:, 0:GROUP], ACT.Identity, scale=-1.0 / NEG,
                                         bias=one[:, 0:1]).then_inc(s_select_t, 1)

                def weigh(n, g):
                    r, b0 = place_of(g)
                    act.wait_ge(s_logit, n + 1)
                    slot_rows = gathered[:, r, b0:b0 + BPG, 0:HZ].rearrange("p b (q o) -> p b q o", q=H)
                    nc.scalar.activation(slot_rows[:, :, :, OUT], logit[:, g % 2, :, :], ACT.Exp).then_inc(s_exp, 1)
                    act.wait_ge(s_exp, n + 1)
                    for b in range(BPG):
                        for q in range(H):
                            ins = nc.scalar.activation(slot_rows[:, b, q, 0:OUT], slot_rows[:, b, q, 0:OUT], ACT.Identity,
                                                       scale=slot_rows[:, b, q, OUT:HW])
                    ins.then_inc(s_row, 1)

                def body(it, first, last):
                    for g in range(GPI):
                        n = it * GPI + g
                        if not (last and g >= GPI - 2):
                            copy_scores(it, g + 2)
                        if not (last and g == GPI - 1):
                            copy_miss(it, g + 1)
                        act.wait_ge(s_nodes, n + 1)
                        wait(act, s_added, n - 3)
                        nc.scalar.activation(keep[:, g % 4, :], raised[:, :], ACT.Exp).then_inc(s_keep, 1)
                        if not (first and g == 0):
                            weigh(n - 1, (g - 1) % GPI)
                        ahead = 1 if g >= 2 else 0
                        if not (last and ahead):
                            wait(act, s_sum, n - 1)
                            index(it + ahead, (g - 2) % RING)
                        if not (last and g >= GPI - AHEAD):
                            make_miss(it, g + AHEAD)
                    if last:
                        weigh(n, GPI - 1)

                for r in range(RING - 2):
                    index(0, r)
                for g in range(AHEAD):
                    make_miss(0, g)
                copy_scores(0, 0)
                copy_miss(0, 0)
                copy_scores(0, 1)
                turns(act, body)

            @block.tensor
            def _(pe):
                def turn_miss(it, g):
                    n = it * GPI + g
                    r, b0 = place_of(g)
                    pe.wait_ge(s_miss, n + 1)
                    wait(pe, s_select_t, n)
                    for b in range(BPG):
                        ins = nc.tensor.transpose(miss_t[:, b * P:(b + 1) * P], miss[:, g % 4, b * P:(b + 1) * P], ident_b[:, :])
                    ins.then_inc(s_miss_t, 1)

                def turn_scores(it, g):
                    n = it * GPI + g
                    r, b0 = place_of(g)
                    pe.wait_ge(s_gath[r], (it + g // GPI) * (16 * BPC) + 16 * BPC)
                    wait(pe, s_score_t, n)
                    for b in range(BPG):
                        ins = nc.tensor.transpose(turned[0:PARTS * H, b * P:(b + 1) * P],
                                                  gathered[:, r, b0 + b, AW:ZW].bitcast(BF16), ident_b[:, :])
                    ins.then_inc(s_turned, 1)

                def sum_rows(n, g):
                    r, b0 = place_of(g)
                    pe.wait_ge(s_row, n + 1)
                    pe.wait_ge(s_hot, n + 1)
                    wait(pe, s_added, n - 1)
                    for b in range(BPG):
                        ins = nc.tensor.matmul(total[g % 2][:, 0:AW], select[:, r, b0 + b, :],
                                               gathered[:, r, b0 + b, 0:AW], start=b == 0, stop=b == BPG - 1)
                    ins.then_inc(s_sum, 1)

                def spread(it, g):
                    n = it * GPI + g
                    pe.wait_ge(s_score_t, n + 1)
                    wait(pe, s_top, n)
                    for b in range(BPG):
                        nc.tensor.matmul(masked_t[:, b, :, :], miss[:, g % 4, b * P:(b + 1) * P], ident4[:, :, :],
                                         start=True, stop=False)
                        for q in range(H):
                            ins = nc.tensor.matmul(masked_t[:, b, q, :], pick[:, q, :], score_t[:, g % 2, b * P:(b + 1) * P],
                                                   start=False, stop=q == H - 1)
                    ins.then_inc(s_masked_t, 1)

                def body(it, first, last):
                    for g in range(GPI):
                        n = it * GPI + g
                        if not (last and g == GPI - 1):
                            spread(it, g + 1)
                        if not (first and g < 2):
                            sum_rows(n - 2, (g - 2) % GPI)
                        if not (last and g >= GPI - 2):
                            turn_scores(it, g + 2)
                            turn_miss(it, g + 2)
                        pe.wait_ge(s_select_t, n + 1)
                        pe.wait_ge(s_nodes, n + 1)
                        wait(pe, s_logit, n - 1)
                        for b in range(BPG):
                            ins = nc.tensor.matmul(side[g % 2][:, b, :], select_t[:, g % 2, b * P:(b + 1) * P], node_side[:, :],
                                                   start=True, stop=True)
                        ins.then_inc(s_side, 1)
                    if last:
                        for back in (1, 0):
                            sum_rows(n - back, GPI - 1 - back)

                for g in range(2):
                    turn_scores(0, g)
                    turn_miss(0, g)
                spread(0, 0)
                turns(pe, body)

            @block.vector
            def _(dve):
                NODE_LINKS, SLOT_LINKS = 4, 3

                def one_hot(it, g, b):
                    n = it * GPI + g
                    r, b0 = place_of(g)
                    wait(dve, s_sum, n - (GPI - 1))
                    ins = nc.vector.tensor_scalar(select[:, r, b0 + b, :], iota[:, :], edges[:, bass.ds(n * BPG + b, 1), 1],
                                                  None, ALU.is_equal)
                    if b == BPG - 1:
                        ins.then_inc(s_hot, 1)

                def rescale(n, g, t):
                    dve.wait_ge(s_keep, n + 1)
                    wait(dve, s_added, n)
                    sums = acc[:, bass.ds(t, 1), 0:HZ].rearrange("p a (q o) -> p (a q) o", q=H)
                    nc.vector.tensor_tensor(sums, sums,
                                            keep[:, g % 4, :].rearrange("p (q a) -> p q a", a=1).broadcast_to([P, H, HW]),
                                            ALU.mult).then_inc(s_scaled, 1)

                def add(n, g, t):
                    dve.wait_ge(s_scaled, n + 1)
                    dve.wait_ge(s_sum, n + 1)
                    nc.vector.tensor_tensor(acc[:, bass.ds(t, 1), :], total[g % 2][:, 0:AW], acc[:, bass.ds(t, 1), :],
                                            ALU.add).then_inc(s_added, 1)

                def logits(n, g, link):
                    r, b0 = place_of(g)
                    dve.wait_ge(s_side, n + 1)
                    scores = gathered[:, r, b0:b0 + BPG, 0:HZ].rearrange("p b (q o) -> p b q o", q=H)
                    link(nc.vector.tensor_tensor(logit2[:, :, :], scores[:, :, :, OUT], side[g % 2][:, :, 0:H], ALU.add))
                    link(nc.vector.scalar_tensor_tensor(logit2[:, :, :], logit2[:, :, :], SLOPE, logit2[:, :, :],
                                                        ALU.mult, ALU.max))
                    link(nc.vector.tensor_tensor(logit2[:, :, :], logit2[:, :, :], side[g % 2][:, :, H:2 * H], ALU.subtract))
                    nc.vector.tensor_scalar(logit[:, g % 2, :, :], logit2[:, :, :], 0.0, None, ALU.min).then_inc(s_logit, 1)

                def body(it, first, last):
                    tiles = v["load_tiles"](dve, tile_of_group, it, LEAD)
                    tile_of = lambda g: tiles[LEAD + g]
                    for g in range(GPI):
                        n = it * GPI + g
                        c = [0 if first and g == 0 else n * (NODE_LINKS + SLOT_LINKS) - SLOT_LINKS]

                        def link(ins, between=None):
                            ins.then_inc(s_chain, 1)
                            c[0] = c[0] + 1
                            if between:
                                between()
                            dve.wait_ge(s_chain, c[0])

                        old = not (first and g < 3)
                        ahead = not (last and g >= GPI - AHEAD)
                        t = tile_of(g)
                        dve.wait_ge(s_masked_t, n + 1)
                        nc.vector.tensor_reduce(block_top[:, :], masked_t[:, :, :, :].rearrange("p b q e -> p q b e"),
                                                AX.XY, ALU.max).then_inc(s_top, 1)
                        if ahead:
                            one_hot(it, g + AHEAD, 0)
                        dve.wait_ge(s_top, n + 1)
                        state = node_state[:, bass.ds(t, 1), :]
                        link(nc.vector.tensor_tensor(block_top[:, :], block_top[:, :], state[:, 0, 0:H], ALU.add),
                             (lambda: one_hot(it, g + AHEAD, 1)) if ahead else None)
                        link(nc.vector.scalar_tensor_tensor(raise_to[:, H:2 * H], block_top[:, :], SLOPE, block_top[:, :],
                                                            ALU.mult, ALU.max),
                             (lambda: rescale(n - 3, (g - 3) % GPI, tile_of(g - 3))) if old else None)
                        wait(dve, s_side, n)
                        link(nc.vector.tensor_tensor(node_side[:, :], state[:, 0, :], raise_to[:, :], ALU.max))
                        wait(dve, s_keep, n)
                        link(nc.vector.tensor_tensor(raised[:, :], state[:, 0, H:2 * H], node_side[:, H:2 * H], ALU.subtract))
                        nc.vector.tensor_scalar(state[:, 0, H:2 * H], node_side[:, H:2 * H], 1.0, None, ALU.mult).then_inc(s_nodes, 1)
                        if old:
                            add(n - 3, (g - 3) % GPI, tile_of(g - 3))
                        if not (first and g == 0):
                            logits(n - 1, (g - 1) % GPI, link)
                    if last:
                        dve.wait_ge(s_logit, n)
                        logits(n, GPI - 1, link)
                        for back in (2, 1, 0):
                            rescale(n - back, GPI - 1 - back, tile_of(GPI - 1 - back))
                            add(n - back, GPI - 1 - back, tile_of(GPI - 1 - back))

                for g in range(AHEAD):
                    for b in range(BPG):
                        one_hot(0, g, b)
                turns(dve, body)

    
_INS = ["x", "src", "dst", "edge_attr_8", "edge_weight", "L0_gnn_attn", "L1_gnn_W_in", "L1_gnn_b_in", "L1_gnn_W1",
        "L1_gnn_b1", "L1_gnn_g1", "L1_gnn_be1", "L1_gnn_W2", "L1_gnn_b2", "L1_gnn_g_out", "L1_gnn_b_out", "L2_gnn_W",
        "L2_gnn_b", "L3_gnn_W", "L3_gnn_b"]


def kernel(**inputs):
    import numpy as _np
    import concourse.bacc as _bacc
    from concourse.bass_utils import run_bass_kernel_spmd as _run

    laid = {name: _np.ascontiguousarray(inputs[name]) for name in _INS}
    laid["xT"] = _np.ascontiguousarray(_np.asarray(inputs["x"]).T)
    laid["W_rows"] = _np.ascontiguousarray(_np.asarray(inputs["L0_gnn_W"]).reshape(H * OUT, D))
    laid["W_cols"] = _np.ascontiguousarray(laid["W_rows"].T)
    nc = _bacc.Bacc("TRN2", target_bir_lowering=False, num_devices=1)
    arrays, handles = {}, {}
    for name, a in laid.items():
        arrays[f"in_{name}"] = a
        handles[name] = nc.dram_tensor(f"in_{name}", a.shape, mybir.dt.from_np(a.dtype), kind="ExternalInput").ap()
    handles["out"] = nc.dram_tensor("out_0", (N, D), F32, kind="ExternalOutput").ap()
    build(nc, handles)
    r = _run(nc, [arrays], core_ids=[0])
    return r.results[0]["out_0"]
```

```python
import concourse.bass as bass
from concourse import mybir
from contextlib import ExitStack, contextmanager

F32 = mybir.dt.float32
I32 = mybir.dt.int32
BF16 = mybir.dt.bfloat16
U32 = mybir.dt.uint32
U8 = mybir.dt.uint8
ALU = mybir.AluOpType
ACT = mybir.ActivationFunctionType
AX = mybir.AxisListType

P = 128
N = 3125
E = 53125
D = 256
H, OUT = 4, 64
LAYERS = 3
KC = D // P
NT = -(-N // P)
NPAD = NT * P
LAST = N - (NT - 1) * P
EC = -(-E // P)
EFULL = E // EC
ETAIL = E - EFULL * EC
RING = 8
BPC = 2
BPI = RING * BPC
GROUP = 2 * P
SHIFT = GROUP.bit_length() - 1
BPG = GROUP // P
GPC = BPC // BPG
GPI = RING * GPC
ITER = -(-((E + NT * (GROUP - 1)) // GROUP) // GPI)
GROUPS = ITER * GPI
BLOCKS = GROUPS * BPG
GATHERED = [f"s_gath{r}" for r in range(RING)]
LEAD = 4
BY_SP = GROUPS // 10 * 4
BY_ACT = GROUPS // 16 * 4
SPARE = BPG
TRASH = NT
REC = 4
HW = OUT + 1
HZ = H * HW
AW = HZ + 1
PARTS = 3
ZW = AW + PARTS * H // 2
LROWS = P * EC + GROUP
AWAY = -1.0e6
NEG = -2.0 ** 100
SLOPE = 0.01
LN_EPS = 1e-5
BN_EPS = LN_EPS
NORM_EPS = 1e-12
DEN_EPS = 1e-9
NCOL = 512
CHUNKS = [(c, min(NCOL, NPAD - c)) for c in range(0, NPAD, NCOL)]
SU = 8
SET = 5
assert NT % SET == 0
AHEAD = 3
SITER = EC // (2 * SU)
assert SITER * 2 * SU == EC
SG = 2
SB = SG * RING
SPAIRS = EC // (2 * SB)
assert SPAIRS * 2 * SB == EC and 2 * SPAIRS < ITER
EA = E * 8 // 125


class Chain:

    def __init__(self, engine, sem):
        self.engine, self.sem, self.n = engine, sem, 0

    def __call__(self, instruction):
        instruction.then_inc(self.sem, 1)
        self.n += 1

    def wait(self):
        self.engine.wait_ge(self.sem, self.n)

    def step(self, instruction):
        self(instruction)
        self.wait()


def build(nc, A):
    stages = []

    @contextmanager
    def stage(*names):
        stages.append(names)
        sems = [nc.alloc_semaphore(f"{n}_{len(stages)}") for n in names]
        with nc.Block() as block:
            yield sems, block
        nc.clear_and_free_semaphores(sems)
        nc.all_engine_barrier()

    dram = {n: nc.dram_tensor(n, s, F32).ap() for n, s in (
        ("list_by_dst", [LROWS, REC]), ("list_by_src", [P * (BLOCKS + SPARE), REC]),
        ("z_table", [NPAD, ZW]), ("node_table", [NPAD, D]))}
    list_dst_d, list_src_d, z_d, node_d = (
        dram[n] for n in ("list_by_dst", "list_by_src", "z_table", "node_table"))

    with ExitStack() as outer:
        def sb(name, shape, dt=F32, where=outer):
            return where.enter_context(nc.sbuf_tensor(name, shape, dt))

        def rows(t):
            return t.rearrange("(t p) f -> p t f", p=P)

        tile_by_dst = sb("tile_by_dst", [1, LEAD + GROUPS], U8)
        tile_by_src = sb("tile_by_src", [1, LEAD + GROUPS], U8)
        row_by_dst = sb("row_by_dst", [1, GROUPS], I32)
        ident = sb("ident", [P, P])
        iota = sb("iota", [P, P])
        x = sb("x", [P, NT, D])
        acc = sb("acc", [P, NT + 1, AW])
        list_dst = sb("edges_by_dst", [P, BLOCKS, REC])
        list_src = sb("edges_by_src", [P, BLOCKS, REC])
        dst_score = sb("dst_score", [P, NT + 1, H])
        dinv = sb("dinv", [P, NT])
        rden = sb("rden", [P, NT, H])
        shift = sb("shift", [P, NT])
        stats = sb("node_stats", [P, NT, 6])
        meanvar = sb("node_meanvar", [P, NT, 2])
        rstd = sb("node_rstd", [P, NT])
        zero_mean = sb("zero_times_mean", [P, 1])
        eps = sb("eps", [P, 1])
        brow = sb("bias_row", [P, D])

        rec_src = sb("rec_src", [P, EC, REC])
        pos_src = sb("pos_src", [P, EC], U32)

        big = sb("big", [P, NT, ZW])
        xT = sb("xT", [P, KC, NPAD])
        hT = big[:, :, :].rearrange("p t f -> p (t f)")[:, 0:KC * NPAD].rearrange("p (k n) -> p k n", k=KC)
        w_sb = sb("w_sb", [P, KC, HZ + H])
        w2_sb = sb("w2_sb", [P, KC, D])
        w3_sb = sb("w3_sb", [P, KC, D])
        column = sb("column", [P, 8, KC])

        pre = outer.enter_context(ExitStack())
        prefix = sb("prefix", [P, 2, EC], F32, pre)
        key_dst = sb("key_dst", [P, EC], I32, pre)
        key_src = sb("key_src", [P, EC], I32, pre)
        key_next = sb("key_next", [P, EC], I32, pre)
        weight = sb("weight", [P, EC], F32, pre)
        tile_f = sb("tile_f", [P, EC], F32, pre)
        tile_next = sb("tile_next", [P, EC], F32, pre)
        part = sb("part", [P, EC], I32, pre)
        ones_row = sb("ones_row", [P, EC], F32, pre)
        mask = sb("mask", [P, 2, EC], F32, pre)
        term = sb("term", [P, 2, EC], F32, pre)
        count_dst = sb("count_dst", [P, NT + 1], F32, pre)
        count_src = sb("count_src", [P, NT + 1], F32, pre)
        first_edge = sb("first_edge", [P, NT + 1], F32, pre)
        offset = sb("offset", [P, NT + 1], F32, pre)
        group_id = sb("group_id", [P, GROUPS], F32, pre)
        reached = sb("reached", [NT, GROUPS], F32, pre)
        row_f = sb("row_f", [1, GROUPS], F32, pre)
        key_by_dst = sb("key_by_dst", [P, GROUPS], F32, pre)
        groups_i = sb("groups_i", [NT, 1], I32, pre)
        groups_f = sb("groups_f", [NT, 1], F32, pre)
        group_end = sb("group_end", [NT, 1], F32, pre)
        surplus = sb("surplus", [NT, 1], F32, pre)
        surplus_row = sb("surplus_row", [NT, P], F32, pre)
        rec_dst = sb("rec_dst", [P, EC, REC], F32, pre)
        pos_f = sb("pos_f", [P, EC], F32, pre)
        sizes = sb("sizes", [P, NT + 1], F32, pre)
        sizes_i = sb("sizes_i", [P, NT + 1], I32, pre)
        slot = sb("slot", [P, EC], I32, pre)
        slot_p = sb("slot_p", [P, EC], I32, pre)
        slot_b = sb("slot_b", [P, EC], I32, pre)
        before = sb("before", [P, P], F32, pre)
        upto = sb("upto", [P, P], F32, pre)
        every = sb("every", [P, P], F32, pre)
        away = sb("away", [P, BPG, REC], F32, pre)
        attr = big[0:125, :, :].rearrange("p t f -> p (t f)")[:, 0:EA]
        attr_sum = sb("attr_sum", [P, 1], F32, pre)
        jumps = sb("jumps", [P, 1], F32, pre)
        unordered = sb("unordered", [P, 1], I32, pre)

        def tile_numbers(last, key, to):
            last.step(nc.vector.tensor_scalar(part[:, :], key[:, :], 7, None, ALU.logical_shift_right))
            last.step(nc.vector.tensor_copy(to[:, :], part[:, :]))

        def records(last, key, other, rec):
            last(nc.vector.tensor_copy(rec[:, :, 1], key[:, :]))
            last(nc.vector.tensor_scalar(rec[:, :, 0], other[:, :], float(N - 1), None, ALU.min))
            last(nc.vector.tensor_copy(rec[:, :, 2], weight[:, :]))

        def tables(last, pe_steps, tile_of, totals, small, wide):
            last.step(nc.vector.tensor_scalar(groups_i[:, :], totals, float(GROUP - 1), None, ALU.add))
            last.step(nc.vector.tensor_scalar(groups_i[:, :], groups_i[:, :], SHIFT, None, ALU.logical_shift_right))
            last.step(nc.vector.tensor_copy(groups_f[:, :], groups_i[:, :]))
            last.step(nc.vector.scalar_tensor_tensor(surplus[:, :], groups_f[:, :], -float(GROUP), totals,
                                                     ALU.mult, ALU.add))
            last.step(nc.vector.tensor_copy(surplus_row[:, :], surplus[:, :].broadcast_to([NT, P])))
            pe_steps()
            last.step(nc.vector.tensor_copy(group_end[:, :], small))
            last.step(nc.vector.tensor_scalar(reached[:, 0:GROUPS], group_id[0:NT, 0:GROUPS], group_end[:, 0:1], None, ALU.is_ge))
            pe_steps()
            last.step(nc.vector.tensor_copy(tile_of[0:1, LEAD:LEAD + GROUPS], wide[0][0:1, 0:GROUPS]))

        def tables_pe(pe, s_dve, s_pe, n0, small, wide):
            pe.wait_ge(s_dve, n0 + 1)
            nc.tensor.matmul(small, upto[0:NT, 0:NT], groups_f[:, :], start=True, stop=True).then_inc(s_pe, 1)
            pe.wait_ge(s_dve, n0 + 2)
            nc.tensor.matmul(wide[0][:, 0:GROUPS], every[0:NT, :], reached[:, 0:GROUPS], start=True, stop=True)
            nc.tensor.matmul(wide[1][:, 0:GROUPS], surplus_row[:, :], reached[:, 0:GROUPS], start=True, stop=True).then_inc(s_pe, 1)

        def exchange(dve, s_dve, s_pe):
            n = [0]

            def step():
                n[0] += 1
                dve.sem_inc(s_dve, 1)
                dve.wait_ge(s_pe, n[0])
            return step

        def positions(last, ahead, sizes, pos):
            last.step(nc.vector.tensor_tensor_scan(first_edge[:, :], ones_row[:, 0:NT + 1], sizes, 0.0, ALU.mult, ALU.add))
            last.step(nc.vector.tensor_tensor(offset[:, :], first_edge[:, :], sizes, ALU.subtract))
            last.step(nc.vector.scalar_tensor_tensor(offset[:, :], offset[:, :], -1.0, ahead, ALU.add, ALU.add))
            last(nc.vector.memset(pos_f[:, :], 0.0))
            for t in range(NT + 1):
                last.step(nc.vector.tensor_scalar(mask[:, t % 2, :], tile_f[:, :], float(t), None, ALU.is_equal))
                last.step(nc.vector.tensor_tensor_scan(prefix[:, t % 2, :], ones_row[:, :], mask[:, t % 2, :], 0.0, ALU.mult, ALU.add))
                last.step(nc.vector.scalar_tensor_tensor(term[:, t % 2, :], prefix[:, t % 2, :], offset[:, t:t + 1],
                                                         mask[:, t % 2, :], ALU.add, ALU.mult))
                last(nc.vector.tensor_tensor(pos_f[:, :], pos_f[:, :], term[:, t % 2, :], ALU.add))
            last.wait()
            last.step(nc.vector.tensor_copy(pos[:, :], pos_f[:, :]))

        def count_tiles(last, counts):
            for t in range(NT + 1):
                last.step(nc.vector.tensor_scalar(mask[:, t % 2, :], tile_f[:, :], float(t), None, ALU.is_equal, ALU.add,
                                                  accum_out=counts[:, t:t + 1]))
            last.wait()

        with ExitStack() as ps, stage(
            "s_cleared", "s_edges", "s_const", "s_pool", "s_chain", "s_dve", "s_pe", "s_x", "s_attr",
        ) as ((s_cleared, s_edges, s_const, s_pool, s_chain, s_dve, s_pe, s_x, s_attr), block):
            sums = ps.enter_context(nc.psum_tensor("sums", [P, 64], F32))
            wide = [ps.enter_context(nc.psum_tensor(f"wide{i}", [P, 512], F32)) for i in range(2)]

            @block.sync
            def _(sp):
                def load(name, to, first):
                    sp.dma_start(to[0:EFULL, :], A[name][first:EFULL * EC + first].rearrange("(p c) -> p c", c=EC)).then_inc(s_edges, 16)
                    sp.dma_start(to[EFULL:EFULL + 1, 0:ETAIL - first],
                                 A[name][EFULL * EC + first:E].rearrange("(p c) -> p c", p=1)).then_inc(s_edges, 16)
                sp.wait_ge(s_cleared, 1)
                load("dst", key_dst, 0)
                load("dst", key_next, 1)
                load("src", key_src, 0)
                load("edge_weight", weight, 0)
                sp.dma_start(attr[:, :], A["edge_attr_8"].rearrange("(p e) a -> p (e a)", p=125)).then_inc(s_attr, 16)
                sp.dma_start(x[:, 0:NT - 1, :],
                             A["x"][0:(NT - 1) * P, :].rearrange("(t p) f -> p t f", p=P)).then_inc(s_x, 16)
                sp.dma_start(x[0:LAST, NT - 1, :], A["x"][(NT - 1) * P:N, :]).then_inc(s_x, 16)
                sp.wait_ge(s_cleared, 2)
                sp.dma_start(list_dst_d[P * EC:LROWS, :].rearrange("(p r) w -> p r w", p=P), away[:, :, :]).then_inc(s_x, 16)
                sp.dma_start(list_src_d.rearrange("(p b) w -> p b w", p=P)[:, 0:BLOCKS, :], list_src[:, :, :]).then_inc(s_x, 16)
                sp.wait_ge(s_x, 64)

            @block.gpsimd
            def _(pool):
                nc.gpsimd.memset(ident[:, :], 0.0).then_inc(s_pool, 1)
                nc.gpsimd.memset(before[:, :], 1.0).then_inc(s_pool, 1)
                nc.gpsimd.memset(upto[:, :], 1.0).then_inc(s_pool, 1)
                nc.gpsimd.iota(iota[:, :], [[1, P]], 0, channel_multiplier=0,
                               allow_small_or_imprecise_dtypes=True).then_inc(s_pool, 1)
                nc.gpsimd.iota(group_id[:, :], [[1, GROUPS]], 0, channel_multiplier=0,
                               allow_small_or_imprecise_dtypes=True).then_inc(s_pool, 1)
                pool.wait_ge(s_pool, 5)
                nc.gpsimd.affine_select(out=ident[:, :], in_=ident[:, :], compare_op=ALU.not_equal, fill=1.0,
                                        base=0, pattern=[[-1, P]], channel_multiplier=1).then_inc(s_const, 1)
                nc.gpsimd.affine_select(out=before[:, :], in_=before[:, :], compare_op=ALU.is_gt, fill=0.0,
                                        base=0, pattern=[[1, P]], channel_multiplier=-1).then_inc(s_const, 1)
                nc.gpsimd.affine_select(out=upto[:, :], in_=upto[:, :], compare_op=ALU.is_ge, fill=0.0,
                                        base=0, pattern=[[1, P]], channel_multiplier=-1).then_inc(s_const, 1)

            @block.vector
            def _(dve):
                last = Chain(dve, s_chain)
                for tile_, value in ((key_dst, NPAD), (key_src, NPAD), (key_next, NPAD), (weight, 0.0)):
                    last(nc.vector.memset(tile_[:, :], value))
                last.step(nc.vector.memset(x[:, NT - 1, :], 0.0))
                dve.sem_inc(s_cleared, 1)
                last(nc.vector.memset(away[:, :, :], 0.0))
                last.step(nc.vector.memset(list_src[:, :, :], 0.0))
                last(nc.vector.memset(away[:, :, 1:2], AWAY))
                last.step(nc.vector.memset(list_src[:, :, 1:2], AWAY))
                dve.sem_inc(s_cleared, 1)
                last(nc.vector.memset(ones_row[:, :], 1.0))
                last(nc.vector.memset(tile_by_dst[:, 0:LEAD], TRASH))
                last(nc.vector.memset(tile_by_src[:, 0:LEAD], TRASH))
                last(nc.vector.memset(every[:, :], 1.0))
                last(nc.vector.memset(eps[:, :], LN_EPS))
                last(nc.vector.memset(attr_sum[:, :], 0.0))
                last(nc.vector.memset(rec_dst[:, :, 3:4], 0.0))
                last(nc.vector.memset(rec_src[:, :, 3:4], 0.0))
                last(nc.vector.memset(dst_score[:, TRASH, :], 0.0))
                dve.wait_ge(s_edges, 128)
                dve.wait_ge(s_const, 3)
                tile_numbers(last, key_next, tile_next)
                tile_numbers(last, key_dst, tile_f)
                last(nc.vector.tensor_tensor(term[:, 0, :], tile_next[:, :], tile_f[:, :], ALU.is_lt))
                count_tiles(last, count_dst)
                last.step(nc.vector.reduce_sum(jumps[:, :], term[:, 0, :], AX.X))
                records(last, key_dst, key_src, rec_dst)
                records(last, key_src, key_dst, rec_src)
                dve.wait_ge(s_attr, 16)
                last.step(nc.vector.reduce_sum(attr_sum[0:125, :], attr[:, :], AX.X))
                step = exchange(dve, s_dve, s_pe)
                step()
                last(nc.vector.tensor_copy(unordered[:, :], sums[:, 0:1]))
                last(nc.vector.tensor_scalar(zero_mean[:, :], sums[:, 1:2], 1.0 / (8 * E), 0.0, ALU.mult, ALU.mult))
                tables(last, step, tile_by_dst, sums[0:NT, 2:3], sums[0:NT, 3:4], wide)
                last(nc.vector.tensor_scalar(key_by_dst[:, :], wide[0][:, 0:GROUPS], float(P), None, ALU.mult))
                last.step(nc.vector.scalar_tensor_tensor(row_f[:, :], group_id[0:1, 0:GROUPS], float(GROUP),
                                                         wide[1][0:1, 0:GROUPS], ALU.mult, ALU.add))
                last.step(nc.vector.tensor_scalar(row_by_dst[:, :], row_f[:, :], float(E), None, ALU.min))

            @block.tensor
            def _(pe):
                pe.wait_ge(s_dve, 1)
                nc.tensor.matmul(sums[:, 0:1], every[:, :], jumps[:, :], start=True, stop=True)
                nc.tensor.matmul(sums[:, 1:2], every[:, :], attr_sum[:, :], start=True, stop=True)
                nc.tensor.matmul(sums[0:NT, 2:3], count_dst[:, 0:NT], every[:, 0:1], start=True, stop=True).then_inc(s_pe, 1)
                tables_pe(pe, s_dve, s_pe, 1, sums[0:NT, 3:4], wide)

        with ExitStack() as ps, stage("s_chain", "s_staged", "s_scat0", "s_scat1", "s_seen", "s_dve", "s_pe", "s_copied") as (
                (s_chain, s_staged, s_scat0, s_scat1, s_seen, s_dve, s_pe, s_copied), block):
            s_scat = (s_scat0, s_scat1)
            sums2 = ps.enter_context(nc.psum_tensor("sums2", [P, 2, 32], F32))
            rec_stage = sb("rec_stage", [P, 2, SU, REC], F32, ps)
            pos_stage = sb("pos_stage", [P, 2, SU], U32, ps)
            pos_dst = sb("pos_dst", [P, EC], U32, ps)
            is_unordered = lambda engine: engine.value_load(unordered[0:1, 0:1], min_val=0, max_val=P * EC) != 0

            @block.sync
            def _(sp):
                with sp.If(is_unordered(sp)):
                    pass
                with sp.Else():
                    sp.dma_start(list_dst_d[0:P * EC, :].rearrange("(p c) w -> p (c w)", c=EC),
                                 rec_dst[:, :, :].rearrange("p c w -> p (c w)")).then_inc(s_copied, 16)
                    sp.wait_ge(s_copied, 16)

            @block.vector
            def _(dve):
                with dve.If(is_unordered(dve)):
                    last = Chain(dve, s_chain)
                    dve.sem_inc(s_dve, 1)
                    dve.wait_ge(s_pe, 1)
                    positions(last, sums2[:, 0, 0:NT + 1], sums2[:, 1, 0:NT + 1], pos_dst)

                    def copy(col, h):
                        nc.vector.tensor_scalar(rec_stage[:, h, :, :], rec_dst[:, bass.ds(col, SU), :], 1.0, None, ALU.mult).then_inc(s_staged, 1)
                        nc.vector.tensor_scalar(pos_stage[:, h, :], pos_dst[:, bass.ds(col, SU)], 1.0, None, ALU.mult).then_inc(s_staged, 1)
                    for h in range(2):
                        copy(h * SU, h)
                    with dve.Fori(1, SITER) as it:
                        for h in range(2):
                            dve.wait_ge(s_scat[h], it * (16 * SU))
                            copy(it * (2 * SU) + h * SU, h)

            @block.tensor
            def _(pe):
                with pe.If(is_unordered(pe)):
                    pe.wait_ge(s_dve, 1)
                    nc.tensor.matmul(sums2[:, 0, 0:NT + 1], before[:, :], count_dst[:, :], start=True, stop=True)
                    nc.tensor.matmul(sums2[:, 1, 0:NT + 1], every[:, :], count_dst[:, :], start=True, stop=True).then_inc(s_pe, 1)

            @block.gpsimd
            def _(pool):
                with pool.If(is_unordered(pool)):
                    with pool.Fori(0, SITER) as it:
                        for h in range(2):
                            pool.wait_ge(s_staged, it * 4 + 2 * h + 2)
                            pool.sem_inc(s_seen, 1)
                            for j in range(SU):
                                pool.indirect_dma_start(list_dst_d, bass.IndirectOffsetOnAxis(ap=pos_stage[:, h, j:j + 1], axis=0),
                                                        rec_stage[:, h, j, :], None).then_inc(s_scat[h], 16)
                    for h in range(2):
                        pool.wait_ge(s_scat[h], SITER * 16 * SU)

        def load_numbers(engine, table, top):
            return nc.values_load_multi_w_load_instructions(table, engines=[engine.engine], min_val=0, max_val=top)[1]

        def load_tiles(engine, tile_of_group, turn, lead):
            words = load_numbers(engine, tile_of_group[:, :].bitcast(I32)[0:1, bass.ds(
                turn * (GPI // 4) + (LEAD - lead) // 4, (GPI + lead) // 4)], (TRASH + 1) << 24)
            return [nc.s_assert_within((word >> (8 * j)) & 255, 0, TRASH,
                                       skip_runtime_bounds_check_because="it is a count of the NT tiles that a group lies beyond")
                    for word in words for j in range(4)]

        def load_by_dst(engine, first, count, s_rows):
            with engine.Fori(0, count // 4) as i:
                for j, row in enumerate(load_numbers(engine, row_by_dst[0:1, bass.ds(i * 4 + first, 4)], E)):
                    g = i * 4 + (first + j)
                    engine.dma_start(list_dst[:, bass.ds(g * BPG, BPG), :],
                                     list_dst_d[bass.ds(row, GROUP), :].rearrange("(p b) w -> p b w", p=P)).then_inc(s_rows, 16)

        def aggregate(tag, edges, tile_of_group, weighted, loads):
            with ExitStack() as ps, stage("s_load", "s_index", "s_seen", *GATHERED, "s_select",
                                          "s_sum", "s_added") as (
                    (s_load, s_index, s_seen, *s_gath, s_select, s_sum, s_added), block):
                total = [ps.enter_context(nc.psum_tensor(f"total{i}_{tag}", [P, 512], F32)) for i in range(GPI)]

                @block.sync
                def _(sp):
                    for to, of in loads:
                        sp.dma_start(to, of).then_inc(s_load, 16)
                    sp.wait_ge(s_load, 16 * len(loads))

                @block.scalar
                def _(act):
                    with act.Fori(0, ITER) as it:
                        for r in range(RING):
                            act.wait_ge(s_sum, it * GPI + (r + 1) * GPC)
                            nc.scalar.activation(slot_node[:, r, 0:BPC], edges[:, bass.ds(it * BPI + r * BPC, BPC), 0],
                                                 ACT.Copy).then_inc(s_index, 1)

                @block.gpsimd
                def _(pool):
                    with pool.Fori(0, ITER) as it:
                        for r in range(RING):
                            pool.wait_ge(s_index, it * RING + (r + 1))
                            pool.sem_inc(s_seen, 1)
                            for j in range(BPC):
                                pool.indirect_dma_start(gathered[:, r, j, 0:D], None, node_d,
                                                        bass.IndirectOffsetOnAxis(ap=slot_node[:, r, j:j + 1], axis=0)
                                                        ).then_inc(s_gath[r], 16)

                @block.tensor
                def _(pe):
                    pe.sem_inc(s_sum, GPI)
                    with pe.Fori(0, ITER) as it:
                        for r in range(RING):
                            pe.wait_ge(s_gath[r], it * (16 * BPC) + 16 * BPC)
                            pe.wait_ge(s_select, it * BPI + (r + 1) * BPC)
                            for g in range(r * GPC, (r + 1) * GPC):
                                pe.wait_ge(s_added, it * GPI + (g + 1))
                                for b in range(BPG):
                                    j = (g - r * GPC) * BPG + b
                                    last = nc.tensor.matmul(total[g][:, 0:D], select[:, r, j, :], gathered[:, r, j, 0:D],
                                                            start=b == 0, stop=b == BPG - 1)
                                last.then_inc(s_sum, 1)

                @block.vector
                def _(dve):
                    def one_hots(it, r):
                        dve.wait_ge(s_sum, it * GPI + (r + 1) * GPC)
                        for j in range(BPC):
                            at = edges[:, bass.ds(it * BPI + (r * BPC + j), 1), :]
                            if weighted:
                                one = nc.vector.tensor_scalar(select[:, r, j, :], iota[:, :], at[:, 0, 1:2], at[:, 0, 2:3],
                                                              ALU.is_equal, ALU.mult)
                            else:
                                one = nc.vector.tensor_scalar(select[:, r, j, :], iota[:, :], at[:, 0, 1:2], None, ALU.is_equal)
                            one.then_inc(s_select, 1)

                    def add(it, r, tiles):
                        for g in range(r * GPC, (r + 1) * GPC):
                            group = it * GPI + g
                            t = tiles[g]
                            dve.wait_ge(s_sum, group + (GPI + 1))
                            dve.wait_ge(s_added, group + GPI)
                            nc.vector.tensor_tensor(acc[:, bass.ds(t, 1), 0:D], total[g][:, 0:D],
                                                    acc[:, bass.ds(t, 1), 0:D], ALU.add).then_inc(s_added, 1)

                    dve.sem_inc(s_added, GPI)
                    with dve.Fori(0, ITER) as it:
                        tiles = load_tiles(dve, tile_of_group, it, 0)
                        for r in range(RING):
                            one_hots(it, r)
                            if r:
                                add(it, r - 1, tiles)
                        add(it, RING - 1, tiles)

        first_table(nc, A, stage, locals())
        pre.close()
        gathered = sb("gathered", [P, RING, BPC, ZW])
        select = sb("select", [P, RING, BPC, P])
        slot_node = sb("slot_node", [P, RING, BPC], U32)
        def load_w(w, to=None):
            return [((to or w3_sb)[:, k, 0:D], w[k * P:(k + 1) * P, :]) for k in range(KC)]

        def load_layer(l):
            vectors = ("L1_gnn_b1", "L1_gnn_g1", "L1_gnn_be1", "L1_gnn_b2", "L1_gnn_g_out", "L1_gnn_b_out")
            return load_w(A["L1_gnn_W1"][l], w_sb) + load_w(A["L1_gnn_W2"][l], w2_sb) + [
                (column[:, i, k:k + 1], A[name][l, k * P:(k + 1) * P].rearrange("(p a) -> p a", a=1))
                for i, name in enumerate(vectors) for k in range(KC)]

        def vector(name):
            return [(brow[:, :], A[name].rearrange("(a n) -> a n", a=1).broadcast_to([P, D]))]

        attention(nc, A, stage, locals(), load_w(A["L1_gnn_W_in"]) + vector("L1_gnn_b_in"))
        def h0_rows(t, prod):
            return nc.vector.tensor_tensor(acc[:, t, 0:D], prod, brow[:, :], ALU.add)

        def rows3(t, prod):
            return nc.vector.tensor_copy(big[:, t, 0:D], prod)

        def rows4(t, prod):
            return nc.vector.tensor_scalar(acc[:, t, 0:D], prod, dinv[:, t:t + 1], None, ALU.mult)

        norm_and_project(nc, A, stage, locals(), "h0", "attention", h0_rows, acc)
        for l in range(LAYERS):
            aggregate(f"l{l}", list_src, tile_by_src, True,
                      load_layer(l) + (load_w(A["L2_gnn_W"]) if l == LAYERS - 1 else []))
            layer_mlp(nc, A, stage, locals())
        norm_and_project(nc, A, stage, locals(), "x3", "sum", rows3, big)
        aggregate("g3", list_dst, tile_by_dst, True, load_w(A["L3_gnn_W"]) + vector("L2_gnn_b"))
        norm_and_project(nc, A, stage, locals(), "x4", "unit", rows4, acc)
        aggregate("g4", list_dst, tile_by_dst, False, vector("L3_gnn_b"))
        norm_and_project(nc, A, stage, locals(), "n4", "tanh", None, None)


def norm_and_project(nc, A, stage, v, tag, how, finish, rows_sb):
    x, xT, acc, brow, dinv, rstd, meanvar, eps, big, ident, w3_sb, stats, shift, rden = (
        v[n] for n in ("x", "xT", "acc", "brow", "dinv", "rstd", "meanvar", "eps", "big", "ident", "w3_sb", "stats", "shift", "rden"))
    sets = NT // SET
    with ExitStack() as ps, stage("s_chain", "s_root", "s_rooted", "s_pre", "s_act", "s_norm2", "s_norm", "s_var", "s_std",
                                  "s_coef", "s_x", "s_turned", "s_copied", "s_prod", "s_fin", "s_stored", "s_clear", "s_rows") as (
            (s_chain, s_root, s_rooted, s_pre, s_act, s_norm2, s_norm, s_var, s_std,
             s_coef, s_x, s_turned, s_copied, s_prod, s_fin, s_stored, s_clear, s_rows), block):
        turned = [ps.enter_context(nc.psum_tensor(f"turned{i}_{tag}", [P, D], F32)) for i in range(3)]
        prod = [ps.enter_context(nc.psum_tensor(f"prod{i}_{tag}", [P, D], F32)) for i in range(4)]
        span = lambda i: range(i * SET, (i + 1) * SET)
        tiles = lambda i: slice(i * SET, (i + 1) * SET)

        @block.sync
        def _(sp):
            if how == "attention":
                sp.dma_start(v["list_src"][:, :, :],
                             v["list_src_d"].rearrange("(p b) w -> p b w", p=P)[:, 0:BLOCKS, :]).then_inc(s_rows, 16)
                sp.wait_ge(s_rows, 16)
            for i in range(sets):
                if finish:
                    sp.wait_ge(s_fin, (i + 1) * SET)
                    sp.dma_start(v["rows"](v["node_d"])[:, tiles(i), :], rows_sb[:, tiles(i), 0:D]).then_inc(s_stored, 16)
                else:
                    sp.wait_ge(s_x, (i + 1) * SET)
                    whole = SET - (i == sets - 1)
                    t0 = i * SET
                    sp.dma_start(A["out"][t0 * P:(t0 + whole) * P, :].rearrange("(t p) f -> p t f", p=P),
                                 x[:, t0:t0 + whole, :]).then_inc(s_stored, 16)
            if not finish:
                sp.dma_start(A["out"][(NT - 1) * P:N, :], x[0:LAST, NT - 1, :]).then_inc(s_stored, 16)
            sp.wait_ge(s_stored, 16 * (sets + (not finish)))

        @block.gpsimd
        def _(pool):
            if how == "sum":
                for i in range(sets):
                    pool.wait_ge(s_var, i + 1)
                    nc.gpsimd.memset(acc[:, tiles(i), :], 0.0).then_inc(s_clear, 1)
                pool.wait_ge(s_clear, sets)

        @block.scalar
        def _(act):
            def elementwise(i):
                act.wait_ge(s_pre, i + 1)
                for t in span(i):
                    if how == "tanh":
                        nc.scalar.activation(acc[:, t, 0:D], acc[:, t, 0:D], ACT.Tanh).then_inc(s_act, 1)
                    else:
                        nc.scalar.activation(acc[:, t, 0:D], acc[:, t, 0:D], ACT.Relu).then_inc(s_act, 1)
                if how == "unit":
                    act.wait_ge(s_act, (i + 1) * SET)
                    for t in span(i):
                        nc.scalar.activation(big[:, t, 0:D], acc[:, t, 0:D], ACT.Square,
                                             accum_out=rden[:, t, 0:1]).then_inc(s_norm2, 1)

            def norms(i):
                act.wait_ge(s_norm, i + 1)
                nc.scalar.activation(rden[:, tiles(i), 1], rden[:, tiles(i), 1], ACT.Sqrt).then_inc(s_rooted, 1)

            if how == "attention":
                act.wait_ge(s_root, 1)
                nc.scalar.activation(dinv[:, :], dinv[:, :], ACT.Sqrt).then_inc(s_rooted, 1)
            if how == "tanh":
                for i in range(sets):
                    elementwise(i)
            if how == "unit":
                elementwise(0)
                norms(0)
            for i in range(sets):
                ahead = how == "unit" and i < sets - 1
                if ahead:
                    elementwise(i + 1)
                act.wait_ge(s_var, i + 1)
                nc.scalar.activation(rstd[:, tiles(i)], meanvar[:, tiles(i), 1], ACT.Sqrt, bias=eps[:, 0:1]).then_inc(s_std, 1)
                if ahead:
                    norms(i + 1)
                act.wait_ge(s_coef, i + 1)
                for t in span(i):
                    nc.scalar.activation(x[:, t, :], x[:, t, :], ACT.Identity, scale=rstd[:, t:t + 1],
                                         bias=shift[:, t:t + 1]).then_inc(s_x, 1)
                if finish:
                    for t in span(i):
                        act.wait_ge(s_turned, t + 1)
                        nc.scalar.activation(xT[:, :, t * P:(t + 1) * P], turned[t % 3][:, :].rearrange("p (k n) -> p k n", k=KC),
                                             ACT.Copy).then_inc(s_copied, 1)

        @block.tensor
        def _(pe):
            if finish:
                for i in range(sets):
                    for t in span(i):
                        pe.wait_ge(s_x, t + 1)
                        if t >= 3:
                            pe.wait_ge(s_copied, t - 2)
                        for k in range(KC):
                            last = nc.tensor.transpose(turned[t % 3][:, k * P:(k + 1) * P], x[:, t, k * P:(k + 1) * P], ident[:, :])
                        last.then_inc(s_turned, 1)
                    for t in span(i):
                        pe.wait_ge(s_copied, t + 1)
                        if t >= 4:
                            pe.wait_ge(s_fin, t - 3)
                        for k in range(KC):
                            last = nc.tensor.matmul(prod[t % 4][:, :], xT[:, k, t * P:(t + 1) * P], w3_sb[:, k, :],
                                                    start=k == 0, stop=k == KC - 1)
                        last.then_inc(s_prod, 1)

        @block.vector
        def _(dve):
            last = Chain(dve, s_chain)
            some = lambda ap: ap.rearrange("p (t f) -> p t f", t=1).broadcast_to([P, SET, D])

            def prepare(i):
                if how == "unit":
                    last.step(nc.vector.tensor_tensor(acc[:, tiles(i), 0:D], acc[:, tiles(i), 0:D], some(brow[:, :]), ALU.add))
                if how == "tanh":
                    for t in span(i):
                        last(nc.vector.scalar_tensor_tensor(acc[:, t, 0:D], acc[:, t, 0:D], dinv[:, t:t + 1], brow[:, :],
                                                            ALU.mult, ALU.add))
                    last.wait()
                dve.sem_inc(s_pre, 1)

            def bound_norms(i):
                dve.wait_ge(s_norm2, (i + 1) * SET)
                last.step(nc.vector.tensor_scalar(rden[:, tiles(i), 1], rden[:, tiles(i), 0], NORM_EPS * NORM_EPS, None, ALU.max))
                dve.sem_inc(s_norm, 1)

            def update(i):
                if how == "attention":
                    for q in range(H):
                        at = acc[:, tiles(i), q * HW:q * HW + OUT]
                        last(nc.vector.tensor_tensor(at, at, rden[:, tiles(i), q:q + 1].broadcast_to([P, SET, OUT]), ALU.mult))
                    last.wait()
                    for q in range(H):
                        to = x[:, tiles(i), q * OUT:(q + 1) * OUT]
                        last(nc.vector.tensor_tensor(to, to, acc[:, tiles(i), q * HW:q * HW + OUT], ALU.add))
                if how == "sum":
                    last(nc.vector.tensor_tensor(x[:, tiles(i), :], x[:, tiles(i), :], acc[:, tiles(i), 0:D], ALU.add))
                if how == "unit":
                    dve.wait_ge(s_rooted, i + 1)
                    last.step(nc.vector.reciprocal(rden[:, tiles(i), 2], rden[:, tiles(i), 1]))
                    for t in span(i):
                        last(nc.vector.scalar_tensor_tensor(x[:, t, :], acc[:, t, 0:D], rden[:, t, 2:3], x[:, t, :],
                                                            ALU.mult, ALU.add))
                if how == "tanh":
                    dve.wait_ge(s_act, (i + 1) * SET)
                    last(nc.vector.scalar_tensor_tensor(x[:, tiles(i), :], acc[:, tiles(i), 0:D], v["zero_mean"][:, 0:1],
                                                        x[:, tiles(i), :], ALU.add, ALU.add))
                last.wait()
                for t in span(i):
                    last(nc.vector.bn_stats(stats[:, t, :], x[:, t, :]))
                last.wait()
                for t in span(i):
                    last(nc.vector.bn_aggr(meanvar[:, t, :], stats[:, t, :]))
                last.wait()
                dve.sem_inc(s_var, 1)

            def coefficients(i):
                dve.wait_ge(s_std, i + 1)
                last.step(nc.vector.reciprocal(rstd[:, tiles(i)], rstd[:, tiles(i)]))
                last.step(nc.vector.scalar_tensor_tensor(shift[:, tiles(i)], meanvar[:, tiles(i), 0], -1.0, rstd[:, tiles(i)],
                                                         ALU.mult, ALU.mult))
                dve.sem_inc(s_coef, 1)

            def products(i):
                if finish:
                    for t in span(i):
                        dve.wait_ge(s_prod, t + 1)
                        finish(t, prod[t % 4][:, :]).then_inc(s_fin, 1)

            if how == "attention":
                last.step(nc.vector.tensor_scalar(dinv[:, :], acc[:, 0:NT, HZ], 1.0, None, ALU.add))
                dve.sem_inc(s_root, 1)
                sums = acc[:, 0:NT, 0:HZ].rearrange("p t (q o) -> p t q o", q=H)
                last.step(nc.vector.tensor_scalar(rden[:, :, :], sums[:, :, :, OUT], DEN_EPS, None, ALU.max))
                last.step(nc.vector.reciprocal(rden[:, :, :], rden[:, :, :]))
                dve.wait_ge(s_rooted, 1)
                last.step(nc.vector.reciprocal(dinv[:, :], dinv[:, :]))
            if how == "tanh":
                for i in range(sets):
                    prepare(i)
            if how == "unit":
                prepare(0)
                bound_norms(0)
            for i in range(sets):
                ahead = how == "unit" and i < sets - 1
                if ahead:
                    prepare(i + 1)
                update(i)
                if ahead:
                    bound_norms(i + 1)
                coefficients(i)
                if i:
                    products(i - 1)
            products(sets - 1)


def layer_mlp(nc, A, stage, v):
    l, xT, hT, acc, column, ident, sb, rows, node_d = (
        v[n] for n in ("l", "xT", "hT", "acc", "column", "ident", "sb", "rows", "node_d"))
    w = (v["w_sb"], v["w2_sb"])
    units = [(c, n, f) for c, n in CHUNKS for f in range(KC)]
    U = len(units)
    names = ("s_turned", "s_xT", "s_prod", "s_out", "s_chain", "s_stat", "s_std", "s_coef", "s_relu", "s_back",
             "s_rows", "s_stored")
    with ExitStack() as own, stage(*names) as (
            (s_turned, s_xT, s_prod, s_out, s_chain, s_stat, s_std, s_coef, s_relu, s_back, s_rows, s_stored), block):
        bstats = sb(f"bstats{l}", [P, KC, len(CHUNKS), 6], F32, own)
        bmv = sb(f"bmv{l}", [P, KC, 2], F32, own)
        scale = sb(f"bscale{l}", [P, KC], F32, own)
        shift = sb(f"bshift{l}", [P, KC], F32, own)
        turned = [own.enter_context(nc.psum_tensor(f"mlp_turned{l}{i}", [P, NCOL], F32)) for i in range(4)]
        prod = [own.enter_context(nc.psum_tensor(f"mlp{l}{i}", [P, NCOL], F32)) for i in range(4)]
        steps = ((xT, hT), (hT, xT))

        @block.sync
        def _(sp):
            if l < LAYERS - 1:
                for t0 in range(0, NT, 5):
                    sp.wait_ge(s_rows, t0 + 5)
                    sp.dma_start(rows(node_d)[:, t0:t0 + 5, :], acc[:, t0:t0 + 5, 0:D]).then_inc(s_stored, 16)
                sp.wait_ge(s_stored, 16 * (NT // 5))

        @block.tensor
        def _(pe):
            def turn(u):
                c, n, f = units[u]
                if u >= 4:
                    pe.wait_ge(s_xT, u - 3)
                for t in range(n // P):
                    last = nc.tensor.transpose(turned[u % 4][:, t * P:(t + 1) * P],
                                               acc[:, c // P + t, f * P:(f + 1) * P], ident[:, :])
                last.then_inc(s_turned, 1)

            def product(m, u):
                c, n, f = units[u]
                if m * U + u >= 4:
                    pe.wait_ge(s_out, m * U + u - 3)
                for k in range(KC):
                    last = nc.tensor.matmul(prod[(m * U + u) % 4][:, 0:n], w[m][:, k, f * P:(f + 1) * P],
                                            steps[m][0][:, k, c:c + n], start=k == 0, stop=k == KC - 1)
                last.then_inc(s_prod, 1)

            for u in range(KC):
                turn(u)
            for u0 in range(0, U, KC):
                for u in range(u0 + KC, min(u0 + 2 * KC, U)):
                    turn(u)
                pe.wait_ge(s_xT, u0 + KC)
                for u in range(u0, u0 + KC):
                    product(0, u)
            for u0 in range(0, U, KC):
                pe.wait_ge(s_relu, u0 + KC)
                for u in range(u0, u0 + KC):
                    product(1, u)
            for t in range(NT):
                pe.wait_ge(s_relu, U + KC * (t * P // NCOL + 1))
                if t >= 4:
                    pe.wait_ge(s_rows, t - 3)
                for k in range(KC):
                    last = nc.tensor.transpose(turned[t % 4][:, k * P:(k + 1) * P], xT[:, k, t * P:(t + 1) * P], ident[:, :])
                last.then_inc(s_back, 1)

        @block.scalar
        def _(act):
            def biased(m, u):
                c, n, f = units[u]
                act.wait_ge(s_prod, m * U + u + 1)
                nc.scalar.activation(steps[m][1][:, f, c:c + n], prod[(m * U + u) % 4][:, 0:n], ACT.Identity,
                                     bias=column[:, 3 * m, f:f + 1]).then_inc(s_out, 1)

            def relu(m, u):
                c, n, f = units[u]
                nc.scalar.activation(steps[m][1][:, f, c:c + n], steps[m][1][:, f, c:c + n], ACT.Relu, bias=shift[:, f:f + 1],
                                     scale=scale[:, f:f + 1]).then_inc(s_relu, 1)

            def deviations(m):
                act.wait_ge(s_stat, m + 1)
                nc.scalar.activation(scale[:, :], bmv[:, :, 1], ACT.Sqrt, bias=v["eps"][:, 0:1]).then_inc(s_std, 1)
                act.wait_ge(s_coef, m + 1)

            for u in range(U):
                biased(0, u)
            deviations(0)
            for u in range(U):
                relu(0, u)
                if u >= 2 * KC:
                    biased(1, u - 2 * KC)
            for u in range(U - 2 * KC, U):
                biased(1, u)
            deviations(1)
            for u in range(U):
                relu(1, u)

        @block.vector
        def _(dve):
            last = Chain(dve, s_chain)

            def copy_turned(u):
                c, n, f = units[u]
                dve.wait_ge(s_turned, u + 1)
                nc.vector.tensor_copy(xT[:, f, c:c + n], turned[u % 4][:, 0:n]).then_inc(s_xT, 1)

            def chunk_stats(m, u):
                c, n, f = units[u]
                dve.wait_ge(s_out, m * U + u + 1)
                last(nc.vector.bn_stats(bstats[:, f, c // NCOL, :], steps[m][1][:, f, c:min(c + n, N)]))

            def coefficients(m):
                last.wait()
                for f in range(KC):
                    last(nc.vector.bn_aggr(bmv[:, f, :], bstats[:, f, :, :]))
                last.wait()
                dve.sem_inc(s_stat, 1)
                dve.wait_ge(s_std, m + 1)
                last.step(nc.vector.reciprocal(scale[:, :], scale[:, :]))
                last.step(nc.vector.tensor_tensor(scale[:, :], scale[:, :], column[:, 3 * m + 1, :], ALU.mult))
                last.step(nc.vector.tensor_tensor(shift[:, :], bmv[:, :, 0], scale[:, :], ALU.mult))
                last.step(nc.vector.tensor_tensor(shift[:, :], column[:, 3 * m + 2, :], shift[:, :], ALU.subtract))
                dve.sem_inc(s_coef, 1)

            for u in range(U):
                copy_turned(u)
                if u >= 2 * KC:
                    chunk_stats(0, u - 2 * KC)
            for u in range(U - 2 * KC, U):
                chunk_stats(0, u)
            coefficients(0)
            dve.wait_ge(s_relu, U)
            for u in range(U):
                chunk_stats(1, u)
            coefficients(1)
            for t in range(NT):
                dve.wait_ge(s_back, t + 1)
                nc.vector.tensor_copy(acc[:, t, 0:D], turned[t % 4][:, 0:D]).then_inc(s_rows, 1)


def first_table(nc, A, stage, v):
    sb, rows, z_d, xT, big, acc, w_sb, w2_sb, dst_score, pos_src = (
        v[n] for n in ("sb", "rows", "z_d", "xT", "big", "acc", "w_sb", "w2_sb", "dst_score", "pos_src"))
    with ExitStack() as ps, ExitStack() as small, stage(
            "s_zero", "s_load", "s_prod", "s_weights", "s_row", "s_pool_rows", "s_stored", "s_rows", "s_chain", "s_dve",
            "s_pe", "s_parts") as (
            (s_zero, s_load, s_prod, s_weights, s_row, s_pool_rows, s_stored, s_rows, s_chain, s_dve, s_pe, s_parts), block):
        a_diag = sb("a_diag", [P, KC, 2 * H], F32, small)
        rest = sb("rest", [P, NT, H], F32, small)
        score_w = ps.enter_context(nc.psum_tensor("score_w", [P, KC, 2 * H], F32))
        prod = [ps.enter_context(nc.psum_tensor(f"z_prod{i}", [P, 512], F32)) for i in range(3)]
        sums = ps.enter_context(nc.psum_tensor("sums3", [P, 2, 32], F32))
        totals = ps.enter_context(nc.psum_tensor("totals", [P, 8], F32))
        wide = [ps.enter_context(nc.psum_tensor(f"wide_b{i}", [P, 512], F32)) for i in range(2)]
        heads = w_sb[:, :, 0:HZ].rearrange("p k (h o) -> p k h o", h=H)
        parts = big[:, :, AW:ZW].bitcast(BF16)
        scores = big[:, :, 0:HZ].rearrange("p t (h o) -> p t h o", h=H)[:, :, :, OUT]

        @block.sync
        def _(sp):
            sp.wait_ge(s_zero, 3)
            for k in range(KC):
                sp.dma_start(w2_sb[:, k, :], A["W_rows"][k * P:(k + 1) * P, :]).then_inc(s_load, 16)
            for h in range(H):
                at = (h * OUT) % P
                for side in range(2):
                    c = side * H + h
                    sp.dma_start(a_diag[at:at + OUT, h * OUT // P, c:c + 1],
                                 A["L0_gnn_attn"][0, side * OUT:(side + 1) * OUT].rearrange("(p a) -> p a", a=1)).then_inc(s_load, 16)
            for k in range(KC):
                sp.dma_start(xT[:, k, 0:N], A["xT"][k * P:(k + 1) * P, :]).then_inc(s_load, 16)
                sp.dma_start(heads[:, k, :, 0:OUT],
                             A["W_cols"][k * P:(k + 1) * P, :].rearrange("p (h o) -> p h o", h=H)).then_inc(s_load, 16)
            v["load_by_dst"](sp, 0, BY_SP, s_rows)

        @block.gpsimd
        def _(pool):
            nc.gpsimd.memset(a_diag[:, :, :], 0.0).then_inc(s_zero, 1)
            nc.gpsimd.memset(xT[:, :, N:NPAD], 0.0).then_inc(s_zero, 1)
            nc.gpsimd.memset(big[:, :, HZ:AW], 1.0).then_inc(s_zero, 1)
            nc.gpsimd.memset(acc[:, :, :], 0.0).then_inc(s_zero, 1)
            pool.wait_ge(s_zero, 4)
            v["load_by_dst"](pool, BY_SP + BY_ACT, GROUPS - BY_SP - BY_ACT, s_pool_rows)
            pool.wait_ge(s_parts, 1)
            for t0 in range(0, NT, 5):
                pool.dma_start(rows(z_d)[:, t0:t0 + 5, :], big[:, t0:t0 + 5, :]).then_inc(s_stored, 16)
            pool.wait_ge(s_stored, 16 * (NT // 5))

        @block.tensor
        def _(pe):
            pe.wait_ge(s_load, 16 * (3 * KC + 2 * H))
            for m in range(KC):
                for k in range(KC):
                    last = nc.tensor.matmul(score_w[:, m, :], w2_sb[:, k, m * P:(m + 1) * P], a_diag[:, k, :],
                                            start=k == 0, stop=k == KC - 1)
            last.then_inc(s_prod, 1)
            pe.wait_ge(s_dve, 1)
            nc.tensor.matmul(sums[:, 0, 0:NT + 1], v["before"][:, :], v["count_src"][:, :], start=True, stop=True)
            nc.tensor.matmul(sums[:, 1, 0:NT + 1], v["every"][:, :], v["count_src"][:, :], start=True, stop=True)
            nc.tensor.matmul(totals[0:NT, 0:1], v["count_src"][:, 0:NT], v["every"][:, 0:1], start=True, stop=True).then_inc(s_pe, 1)
            pe.wait_ge(s_weights, 1)
            for t in range(NT):
                if t >= 3:
                    pe.wait_ge(s_row, t - 2)
                for k in range(KC):
                    last = nc.tensor.matmul(prod[t % 3][:, 0:HZ + H], xT[:, k, t * P:(t + 1) * P], w_sb[:, k, :],
                                            start=k == 0, stop=k == KC - 1)
                last.then_inc(s_prod, 1)
            v["tables_pe"](pe, s_dve, s_pe, 1, totals[0:NT, 1:2], wide)

        @block.scalar
        def _(act):
            act.wait_ge(s_prod, 1)
            nc.scalar.activation(heads[:, :, :, OUT], score_w[:, :, 0:H], ACT.Copy)
            nc.scalar.activation(w_sb[:, :, HZ:HZ + H], score_w[:, :, H:2 * H], ACT.Copy).then_inc(s_weights, 1)
            for t in range(NT):
                act.wait_ge(s_prod, t + 2)
                nc.scalar.activation(dst_score[:, t, :], prod[t % 3][:, HZ:HZ + H], ACT.Copy)
                nc.scalar.activation(big[:, t, 0:HZ], prod[t % 3][:, 0:HZ], ACT.Copy).then_inc(s_row, 1)
            v["load_by_dst"](act, BY_SP, BY_ACT, s_rows)

        @block.vector
        def _(dve):
            last = Chain(dve, s_chain)
            v["tile_numbers"](last, v["key_src"], v["tile_f"])
            last(nc.vector.scalar_tensor_tensor(v["rec_src"][:, :, 1], v["tile_f"][:, :], -float(P), v["rec_src"][:, :, 1],
                                                ALU.mult, ALU.add))
            v["count_tiles"](last, v["count_src"])
            step = v["exchange"](dve, s_dve, s_pe)
            step()
            sizes, sizes_i = v["sizes"], v["sizes_i"]
            last.step(nc.vector.tensor_scalar(sizes_i[:, :], sums[:, 1, 0:NT + 1], float(GROUP - 1), None, ALU.add))
            last.step(nc.vector.tensor_scalar(sizes_i[:, :], sizes_i[:, :], SHIFT, None, ALU.logical_shift_right))
            last.step(nc.vector.tensor_scalar(sizes[:, :], sizes_i[:, :], float(GROUP), None, ALU.mult))
            slot, slot_p, slot_b = v["slot"], v["slot_p"], v["slot_b"]
            v["positions"](last, sums[:, 0, 0:NT + 1], sizes[:, :], slot)
            last(nc.vector.tensor_scalar(slot_p[:, :], slot[:, :], P - 1, None, ALU.bitwise_and))
            last.step(nc.vector.tensor_scalar(slot_b[:, :], slot[:, :], P.bit_length() - 1, None, ALU.logical_shift_right))
            last.step(nc.vector.scalar_tensor_tensor(pos_src[:, :], slot_p[:, :], float(BLOCKS + SPARE), slot_b[:, :],
                                                     ALU.mult, ALU.add))
            dve.wait_ge(s_row, NT)
            first = scores
            for i in range(PARTS):
                to = parts[:, :, i * H:(i + 1) * H]
                last.step(nc.vector.tensor_copy(to, first))
                if i < PARTS - 1:
                    last.step(nc.vector.tensor_tensor(rest[:, :, :], first, to, ALU.subtract))
                    first = rest[:, :, :]
            dve.sem_inc(s_parts, 1)
            v["tables"](last, step, v["tile_by_src"], totals[0:NT, 0:1], totals[0:NT, 1:2], wide)
            dve.wait_ge(s_rows, 16 * (BY_SP + BY_ACT))
            dve.wait_ge(s_pool_rows, 16 * (GROUPS - BY_SP - BY_ACT))
            at = v["list_dst"][:, :, 1].rearrange("p (g b) -> p g b", b=BPG)
            last.step(nc.vector.tensor_tensor(at, at, v["key_by_dst"][:, :].rearrange("p (g b) -> p g b", b=1).broadcast_to(
                [P, GROUPS, BPG]), ALU.subtract))


def attention(nc, A, stage, v, loads):
    sb, z_d, x, acc, ident, iota, gathered, select, slot_node, dst_score = (
        v[n] for n in ("sb", "z_d", "x", "acc", "ident", "iota", "gathered",
                       "select", "slot_node", "dst_score"))
    edges, dinv, rec_src, pos_src = v["list_dst"], v["dinv"], v["rec_src"], v["pos_src"]
    tile_of_group = v["tile_by_dst"]
    with ExitStack() as own:
        node_state = sb("node_state", [P, NT + 1, 2 * H], F32, own)
        raise_to = sb("raise_to", [P, 2 * H], F32, own)
        pick = sb("pick", [P, H, P], BF16, own)
        ident4 = sb("ident4", [P, H, P], BF16, own)
        ident_b = sb("ident_b", [P, P], BF16, own)
        pick_col = sb("pick_col", [P, H], F32, own)
        miss = sb("miss", [P, 4, GROUP], BF16, own)
        select_t = sb("select_t", [P, 2, GROUP], F32, own)
        one = sb("one", [P, 1], F32, own)
        neg = sb("neg", [P, 1], F32, own)
        score_t = sb("score_t", [P, 2, GROUP], BF16, own)
        block_top = sb("block_top", [P, H], F32, own)
        node_side = sb("node_side", [P, 2 * H], F32, own)
        raised = sb("raised", [P, H], F32, own)
        keep = sb("keep", [P, 4, H], F32, own)
        logit = sb("logit", [P, 2, BPG, H], F32, own)
        below = sb("below", [P, BPG, H], F32, own)
        logit2 = sb("logit2", [P, BPG, H], F32, own)
        rec_stage = sb("rec_stage_src", [P, 2, SB, REC], F32, own)
        pos_stage = sb("pos_stage_src", [P, 2, SB], U32, own)

        with stage("s_init") as ((s_init,), block):
            @block.vector
            def _(dve):
                last = Chain(dve, s_init)
                nc.vector.tensor_copy(node_state[:, :, 0:H], dst_score[:, :, :])
                nc.vector.memset(node_state[:, :, H:2 * H], NEG * SLOPE)
                nc.vector.memset(raise_to[:, :], NEG)
                nc.vector.memset(score_t[:, :, :], 0.0)
                nc.vector.memset(one[:, :], 1.0)
                nc.vector.memset(neg[:, :], NEG)
                nc.vector.tensor_copy(ident_b[:, :], ident[:, :])
                nc.vector.tensor_copy(ident4[:, :, :], ident[:, :].rearrange("p (a m) -> p a m", a=1).broadcast_to([P, H, P]))
                last.step(nc.vector.tensor_tensor(pick_col[:, :], ident[:, 0:H], ident[:, H:2 * H], ALU.add))
                last.step(nc.vector.tensor_tensor(pick_col[:, :], pick_col[:, :], ident[:, 2 * H:3 * H], ALU.add))
                last.step(nc.vector.tensor_copy(pick[:, :, :], pick_col[:, :].rearrange("p (h m) -> p h m", m=1).broadcast_to([P, H, P])))

        names = ("s_index", "s_seen", *GATHERED, "s_hot", "s_miss", "s_turned", "s_score_t",
                 "s_miss_t", "s_masked_t", "s_chain", "s_top", "s_nodes", "s_keep", "s_select_t", "s_side", "s_logit", "s_below", "s_exp", "s_row",
                 "s_sum", "s_scaled", "s_added", "s_stage0", "s_stage1", "s_scat0", "s_scat1", "s_load")
        with ExitStack() as ps, stage(*names) as (
                (s_index, s_seen, *s_gath, s_hot, s_miss, s_turned, s_score_t,
                 s_miss_t, s_masked_t, s_chain, s_top, s_nodes, s_keep, s_select_t, s_side, s_logit, s_below, s_exp, s_row,
                 s_sum, s_scaled, s_added, s_stage0, s_stage1, s_scat0, s_scat1, s_load), block):
            s_stage, s_scat = (s_stage0, s_stage1), (s_scat0, s_scat1)
            masked_t = ps.enter_context(nc.psum_tensor("masked_t", [P, BPG, H, P], F32))
            miss_t = ps.enter_context(nc.psum_tensor("miss_t", [P, 2 * 512], BF16))
            turned = ps.enter_context(nc.psum_tensor("turned", [P, 2 * 512], BF16))
            side = [ps.enter_context(nc.psum_tensor(f"side{i}", [P, BPG, 2 * H], F32)) for i in range(2)]
            total = [ps.enter_context(nc.psum_tensor(f"total{i}", [P, 512], F32)) for i in range(2)]

            def wait(engine, sem, value):
                if not isinstance(value, int) or value > 0:
                    engine.wait_ge(sem, value)

            def place_of(g):
                g = g % GPI
                return g // GPC, (g % GPC) * BPG

            def turns(engine, body):
                body(0, first=True, last=False)
                with engine.Fori(1, ITER - 1) as it:
                    body(it, first=False, last=False)
                body(ITER - 1, first=False, last=True)

            @block.sync
            def _(sp):
                def load(i, h):
                    col = i * (2 * SB) + h * SB
                    sp.dma_start(rec_stage[:, h, :, :], rec_src[:, bass.ds(col, SB), :]).then_inc(s_stage[h], 16)
                    sp.dma_start(pos_stage[:, h, :], pos_src[:, bass.ds(col, SB)]).then_inc(s_stage[h], 16)

                for h in range(2):
                    load(0, h)
                for to, of in loads:
                    sp.dma_start(to, of).then_inc(s_load, 16)
                sp.wait_ge(s_load, 16 * len(loads))
                with sp.Fori(1, SPAIRS) as i:
                    for h in range(2):
                        sp.wait_ge(s_scat[h], i * (16 * SB))
                        load(i, h)

            @block.gpsimd
            def _(pool):
                def turn(it, h, pair):
                    for r in range(RING):
                        pool.wait_ge(s_index, it * RING + (r + 1))
                        pool.sem_inc(s_seen, 1)
                        for j in range(BPC):
                            pool.indirect_dma_start(gathered[:, r, j, 0:ZW], None, z_d,
                                                    bass.IndirectOffsetOnAxis(ap=slot_node[:, r, j:j + 1], axis=0)
                                                    ).then_inc(s_gath[r], 16)
                        if pair is not None:
                            if r == 0:
                                pool.wait_ge(s_stage[h], pair * 32 + 32)
                                pool.sem_inc(s_seen, 1)
                            for j in range(r * SG, (r + 1) * SG):
                                pool.indirect_dma_start(
                                    v["list_src_d"], bass.IndirectOffsetOnAxis(ap=pos_stage[:, h, j:j + 1], axis=0),
                                    rec_stage[:, h, j, :], None).then_inc(s_scat[h], 16)

                turn(0, 0, None)
                with pool.Fori(0, SPAIRS) as pair:
                    for h in range(2):
                        turn(pair * 2 + (h + 1), h, pair)
                for it in range(2 * SPAIRS + 1, ITER):
                    turn(it, 0, None)
                for h in range(2):
                    pool.wait_ge(s_scat[h], 16 * SB * SPAIRS)

            @block.scalar
            def _(act):
                def index(it, r):
                    nc.scalar.activation(slot_node[:, r, :], edges[:, bass.ds(it * BPI + r * BPC, BPC), 0],
                                         ACT.Copy).then_inc(s_index, 1)

                def copy_scores(it, g):
                    n = it * GPI + g
                    act.wait_ge(s_turned, n + 1)
                    wait(act, s_masked_t, n - 1)
                    nc.scalar.activation(score_t[0:PARTS * H, g % 2, :], turned[0:PARTS * H, 0:GROUP], ACT.Copy).then_inc(s_score_t, 1)

                def make_miss(it, g):
                    n = it * GPI + g
                    r, b0 = place_of(g)
                    act.wait_ge(s_hot, n + 1)
                    wait(act, s_masked_t, n - 3)
                    nc.scalar.activation(miss[:, g % 4, :].rearrange("p (b m) -> p b m", m=P), select[:, r, b0:b0 + BPG, :], ACT.Identity,
                                         scale=-NEG, bias=neg[:, 0:1]).then_inc(s_miss, 1)

                def copy_miss(it, g):
                    n = it * GPI + g
                    act.wait_ge(s_miss_t, n + 1)
                    wait(act, s_side, n - 1)
                    nc.scalar.activation(select_t[:, g % 2, :], miss_t[:, 0:GROUP], ACT.Identity, scale=-1.0 / NEG,
                                         bias=one[:, 0:1]).then_inc(s_select_t, 1)

                def weigh(n, g):
                    r, b0 = place_of(g)
                    act.wait_ge(s_logit, n + 1)
                    slot_rows = gathered[:, r, b0:b0 + BPG, 0:HZ].rearrange("p b (q o) -> p b q o", q=H)
                    nc.scalar.activation(below[:, :, :], logit[:, g % 2, :, :], ACT.Relu).then_inc(s_below, 1)
                    act.wait_ge(s_below, n + 1)
                    nc.scalar.activation(slot_rows[:, :, :, OUT], below[:, :, :], ACT.Exp, scale=-1.0).then_inc(s_exp, 1)
                    act.wait_ge(s_exp, n + 1)
                    for b in range(BPG):
                        for q in range(H):
                            ins = nc.scalar.activation(slot_rows[:, b, q, 0:OUT], slot_rows[:, b, q, 0:OUT], ACT.Identity,
                                                       scale=slot_rows[:, b, q, OUT:HW])
                    ins.then_inc(s_row, 1)

                def body(it, first, last):
                    for g in range(GPI):
                        n = it * GPI + g
                        if not (last and g == GPI - 1):
                            copy_miss(it, g + 1)
                        if not (last and g >= GPI - 2):
                            copy_scores(it, g + 2)
                        act.wait_ge(s_nodes, n + 1)
                        wait(act, s_added, n - 3)
                        nc.scalar.activation(keep[:, g % 4, :], raised[:, :], ACT.Exp).then_inc(s_keep, 1)
                        if not (first and g == 0):
                            weigh(n - 1, (g - 1) % GPI)
                        ahead = 1 if g >= 2 else 0
                        if not (last and ahead):
                            wait(act, s_sum, n - 1)
                            index(it + ahead, (g - 2) % RING)
                        if not (last and g >= GPI - AHEAD):
                            make_miss(it, g + AHEAD)
                    if last:
                        weigh(n, GPI - 1)

                for r in range(RING - 2):
                    index(0, r)
                for g in range(AHEAD):
                    make_miss(0, g)
                copy_scores(0, 0)
                copy_miss(0, 0)
                copy_scores(0, 1)
                turns(act, body)

            @block.tensor
            def _(pe):
                def turn_miss(it, g):
                    n = it * GPI + g
                    r, b0 = place_of(g)
                    pe.wait_ge(s_miss, n + 1)
                    wait(pe, s_select_t, n)
                    for b in range(BPG):
                        ins = nc.tensor.transpose(miss_t[:, b * P:(b + 1) * P], miss[:, g % 4, b * P:(b + 1) * P], ident_b[:, :])
                    ins.then_inc(s_miss_t, 1)

                def turn_scores(it, g):
                    n = it * GPI + g
                    r, b0 = place_of(g)
                    pe.wait_ge(s_gath[r], (it + g // GPI) * (16 * BPC) + 16 * BPC)
                    wait(pe, s_score_t, n)
                    for b in range(BPG):
                        ins = nc.tensor.transpose(turned[0:PARTS * H, b * P:(b + 1) * P],
                                                  gathered[:, r, b0 + b, AW:ZW].bitcast(BF16), ident_b[:, :])
                    ins.then_inc(s_turned, 1)

                def sum_rows(n, g):
                    r, b0 = place_of(g)
                    pe.wait_ge(s_row, n + 1)
                    pe.wait_ge(s_hot, n + 1)
                    wait(pe, s_added, n - 1)
                    for b in range(BPG):
                        ins = nc.tensor.matmul(total[g % 2][:, 0:AW], select[:, r, b0 + b, :],
                                               gathered[:, r, b0 + b, 0:AW], start=b == 0, stop=b == BPG - 1)
                    ins.then_inc(s_sum, 1)

                def spread(it, g):
                    n = it * GPI + g
                    pe.wait_ge(s_score_t, n + 1)
                    wait(pe, s_top, n)
                    for b in range(BPG):
                        nc.tensor.matmul(masked_t[:, b, :, :], miss[:, g % 4, b * P:(b + 1) * P], ident4[:, :, :],
                                         start=True, stop=False)
                        for q in range(H):
                            ins = nc.tensor.matmul(masked_t[:, b, q, :], pick[:, q, :], score_t[:, g % 2, b * P:(b + 1) * P],
                                                   start=False, stop=q == H - 1)
                    ins.then_inc(s_masked_t, 1)

                def body(it, first, last):
                    for g in range(GPI):
                        n = it * GPI + g
                        if not (last and g == GPI - 1):
                            spread(it, g + 1)
                        if not (first and g < 2):
                            sum_rows(n - 2, (g - 2) % GPI)
                        if not (last and g >= GPI - 2):
                            turn_scores(it, g + 2)
                            turn_miss(it, g + 2)
                        pe.wait_ge(s_select_t, n + 1)
                        pe.wait_ge(s_nodes, n + 1)
                        wait(pe, s_logit, n - 1)
                        for b in range(BPG):
                            ins = nc.tensor.matmul(side[g % 2][:, b, :], select_t[:, g % 2, b * P:(b + 1) * P], node_side[:, :],
                                                   start=True, stop=True)
                        ins.then_inc(s_side, 1)
                    if last:
                        for back in (1, 0):
                            sum_rows(n - back, GPI - 1 - back)

                for g in range(2):
                    turn_scores(0, g)
                    turn_miss(0, g)
                spread(0, 0)
                turns(pe, body)

            @block.vector
            def _(dve):
                NODE_LINKS, SLOT_LINKS = 4, 2

                def one_hot(it, g, b):
                    n = it * GPI + g
                    r, b0 = place_of(g)
                    wait(dve, s_sum, n - (GPI - 1))
                    ins = nc.vector.tensor_scalar(select[:, r, b0 + b, :], iota[:, :], edges[:, bass.ds(n * BPG + b, 1), 1],
                                                  None, ALU.is_equal)
                    if b == BPG - 1:
                        ins.then_inc(s_hot, 1)

                def rescale(n, g, t):
                    dve.wait_ge(s_keep, n + 1)
                    wait(dve, s_added, n)
                    sums = acc[:, bass.ds(t, 1), 0:HZ].rearrange("p a (q o) -> p (a q) o", q=H)
                    nc.vector.tensor_tensor(sums, sums,
                                            keep[:, g % 4, :].rearrange("p (q a) -> p q a", a=1).broadcast_to([P, H, HW]),
                                            ALU.mult).then_inc(s_scaled, 1)

                def add(n, g, t):
                    dve.wait_ge(s_scaled, n + 1)
                    dve.wait_ge(s_sum, n + 1)
                    nc.vector.tensor_tensor(acc[:, bass.ds(t, 1), :], total[g % 2][:, 0:AW], acc[:, bass.ds(t, 1), :],
                                            ALU.add).then_inc(s_added, 1)

                def logits(n, g, link):
                    r, b0 = place_of(g)
                    dve.wait_ge(s_side, n + 1)
                    scores = gathered[:, r, b0:b0 + BPG, 0:HZ].rearrange("p b (q o) -> p b q o", q=H)
                    link(nc.vector.tensor_tensor(logit2[:, :, :], scores[:, :, :, OUT], side[g % 2][:, :, 0:H], ALU.add))
                    link(nc.vector.scalar_tensor_tensor(logit2[:, :, :], logit2[:, :, :], SLOPE, logit2[:, :, :],
                                                        ALU.mult, ALU.max))
                    nc.vector.tensor_tensor(logit[:, g % 2, :, :], side[g % 2][:, :, H:2 * H], logit2[:, :, :],
                                            ALU.subtract).then_inc(s_logit, 1)

                def body(it, first, last):
                    tiles = []
                    tile_of = lambda g: tiles[LEAD + g]
                    for g in range(GPI):
                        n = it * GPI + g
                        c = [0 if first and g == 0 else n * (NODE_LINKS + SLOT_LINKS) - SLOT_LINKS]

                        def link(ins, between=None):
                            ins.then_inc(s_chain, 1)
                            c[0] = c[0] + 1
                            if between:
                                between()
                            dve.wait_ge(s_chain, c[0])

                        old = not (first and g < 3)
                        ahead = not (last and g >= GPI - AHEAD)
                        dve.wait_ge(s_masked_t, n + 1)
                        nc.vector.tensor_reduce(block_top[:, :], masked_t[:, :, :, :].rearrange("p b q e -> p q b e"),
                                                AX.XY, ALU.max).then_inc(s_top, 1)
                        if ahead:
                            one_hot(it, g + AHEAD, 0)
                        if g == 0:
                            tiles.extend(v["load_tiles"](dve, tile_of_group, it, LEAD))
                        dve.wait_ge(s_top, n + 1)
                        state = node_state[:, bass.ds(tile_of(g), 1), :]
                        link(nc.vector.tensor_tensor(block_top[:, :], block_top[:, :], state[:, 0, 0:H], ALU.add),
                             (lambda: one_hot(it, g + AHEAD, 1)) if ahead else None)
                        link(nc.vector.scalar_tensor_tensor(raise_to[:, H:2 * H], block_top[:, :], SLOPE, block_top[:, :],
                                                            ALU.mult, ALU.max),
                             (lambda: rescale(n - 3, (g - 3) % GPI, tile_of(g - 3))) if old else None)
                        wait(dve, s_side, n)
                        link(nc.vector.tensor_tensor(node_side[:, :], state[:, 0, :], raise_to[:, :], ALU.max))
                        wait(dve, s_keep, n)
                        link(nc.vector.tensor_tensor(raised[:, :], state[:, 0, H:2 * H], node_side[:, H:2 * H], ALU.subtract))
                        nc.vector.tensor_scalar(state[:, 0, H:2 * H], node_side[:, H:2 * H], 1.0, None, ALU.mult).then_inc(s_nodes, 1)
                        if old:
                            add(n - 3, (g - 3) % GPI, tile_of(g - 3))
                        if not (first and g == 0):
                            logits(n - 1, (g - 1) % GPI, link)
                    if last:
                        dve.wait_ge(s_logit, n)
                        logits(n, GPI - 1, link)
                        for back in (2, 1, 0):
                            rescale(n - back, GPI - 1 - back, tile_of(GPI - 1 - back))
                            add(n - back, GPI - 1 - back, tile_of(GPI - 1 - back))

                for g in range(AHEAD):
                    for b in range(BPG):
                        one_hot(0, g, b)
                turns(dve, body)

    
_INS = ["x", "src", "dst", "edge_attr_8", "edge_weight", "L0_gnn_attn", "L1_gnn_W_in", "L1_gnn_b_in", "L1_gnn_W1",
        "L1_gnn_b1", "L1_gnn_g1", "L1_gnn_be1", "L1_gnn_W2", "L1_gnn_b2", "L1_gnn_g_out", "L1_gnn_b_out", "L2_gnn_W",
        "L2_gnn_b", "L3_gnn_W", "L3_gnn_b"]


def kernel(**inputs):
    import numpy as _np
    import concourse.bacc as _bacc
    from concourse.bass_utils import run_bass_kernel_spmd as _run

    laid = {name: _np.ascontiguousarray(inputs[name]) for name in _INS}
    laid["xT"] = _np.ascontiguousarray(_np.asarray(inputs["x"]).T)
    laid["W_rows"] = _np.ascontiguousarray(_np.asarray(inputs["L0_gnn_W"]).reshape(H * OUT, D))
    laid["W_cols"] = _np.ascontiguousarray(laid["W_rows"].T)
    nc = _bacc.Bacc("TRN2", target_bir_lowering=False, num_devices=1)
    arrays, handles = {}, {}
    for name, a in laid.items():
        arrays[f"in_{name}"] = a
        handles[name] = nc.dram_tensor(f"in_{name}", a.shape, mybir.dt.from_np(a.dtype), kind="ExternalInput").ap()
    handles["out"] = nc.dram_tensor("out_0", (N, D), F32, kind="ExternalOutput").ap()
    build(nc, handles)
    r = _run(nc, [arrays], core_ids=[0])
    return r.results[0]["out_0"]
```
